# Optimizing a Trainium2 kernel written in Bass

```python
import numpy as np
import jax
import jax.numpy as jnp

def _softmax(x, axis=-1):
    return jax.nn.softmax(x, axis=axis)

def _gelu(x):
    return jax.nn.gelu(x, approximate=True)

def _silu(x):
    return jax.nn.silu(x)

def _sigmoid(x):
    return jax.nn.sigmoid(x)

def _layernorm(x, axis=-1, eps=1e-05):
    m = jnp.mean(x, axis=axis, keepdims=True)
    v = jnp.var(x, axis=axis, keepdims=True)
    return (x - m) / jnp.sqrt(v + eps)

def _scatter_add(tgt, idx, src, axis=0):
    return tgt.at[idx].add(src)

def _segment_sum(src, seg, n):
    return jax.ops.segment_sum(src, seg, n)
kernel_name = 'mk_prb_d1_jaxref_r4_a8c214'

def setup_inputs(seed: int=0):
    np.random.seed(seed)
    _w = jnp.asarray

    def _L0_attn_setup():
        import jax, jax.numpy as jnp
        import numpy as np
        LAMBDA_0 = 1.0
        EPS = 1e-06
        key = jax.random.key(seed)
        ks = jax.random.split(key, 5)
        B, T, D, H = (4, 512, 256, 128)
        x = jax.random.normal(ks[0], (B, T, D), dtype=jnp.float32)
        Wq = jax.random.normal(ks[1], (H, D), dtype=jnp.float32) * D ** (-0.5)
        Wk = jax.random.normal(ks[2], (H, D), dtype=jnp.float32) * D ** (-0.5)
        Wv = jax.random.normal(ks[3], (H, D), dtype=jnp.float32) * D ** (-0.5)
        Wo = jax.random.normal(ks[4], (D, H), dtype=jnp.float32) * H ** (-0.5)
        bq = jnp.zeros((H,), jnp.float32)
        bk = jnp.zeros((H,), jnp.float32)
        bv = jnp.zeros((H,), jnp.float32)
        bo = jnp.zeros((D,), jnp.float32)
        return {'x': x, 'Wq': Wq, 'bq': bq, 'Wk': Wk, 'bk': bk, 'Wv': Wv, 'bv': bv, 'Wo': Wo, 'bo': bo}
    _L0_attn_in = _L0_attn_setup()

    def _L0_ffn_setup():
        import jax, jax.numpy as jnp
        import numpy as np
        IN_DIM = 256
        OUT_DIM = 256
        NUM_EXPERTS = 8
        TOP_K = 2
        key = jax.random.key(seed)
        ks = jax.random.split(key, 5)
        s = 1.0 / np.sqrt(IN_DIM)
        x = jax.random.normal(ks[0], (4, 512, IN_DIM), dtype=jnp.float32)
        Wg = jax.random.uniform(ks[1], (IN_DIM, NUM_EXPERTS), jnp.float32, -s, s)
        bg = jnp.zeros((NUM_EXPERTS,), jnp.float32)
        We = jax.random.uniform(ks[2], (NUM_EXPERTS, OUT_DIM, IN_DIM), jnp.float32, -s, s)
        be = jax.random.uniform(ks[3], (NUM_EXPERTS, OUT_DIM), jnp.float32, -s, s)
        return {'x': x, 'Wg': Wg, 'bg': bg, 'We': We, 'be': be}
    _L0_ffn_in = _L0_ffn_setup()
    _d = {'L0_attn_x': _L0_attn_in['x'], 'L0_attn_Wq': _L0_attn_in['Wq'], 'L0_attn_bq': _L0_attn_in['bq'], 'L0_attn_Wk': _L0_attn_in['Wk'], 'L0_attn_bk': _L0_attn_in['bk'], 'L0_attn_Wv': _L0_attn_in['Wv'], 'L0_attn_bv': _L0_attn_in['bv'], 'L0_attn_Wo': _L0_attn_in['Wo'], 'L0_attn_bo': _L0_attn_in['bo'], 'L0_ffn_Wg': _L0_ffn_in['Wg'], 'L0_ffn_bg': _L0_ffn_in['bg'], 'L0_ffn_We': _L0_ffn_in['We'], 'L0_ffn_be': _L0_ffn_in['be']}
    _x0 = _d['L0_attn_x']
    _d['L0_attn_x'] = jax.random.normal(jax.random.fold_in(jax.random.key(seed), 1), (4, 2048, 256), dtype=_x0.dtype)
    del _x0
    return _d

def reference(L0_attn_x, L0_attn_Wq, L0_attn_bq, L0_attn_Wk, L0_attn_bk, L0_attn_Wv, L0_attn_bv, L0_attn_Wo, L0_attn_bo, L0_ffn_Wg, L0_ffn_bg, L0_ffn_We, L0_ffn_be):

    def _L0_attn_ref(x, Wq, bq, Wk, bk, Wv, bv, Wo, bo):
        import jax, jax.numpy as jnp
        import numpy as np
        LAMBDA_0 = 1.0
        EPS = 1e-06
        B, T, D = x.shape
        H = Wq.shape[0]
        Q = jnp.einsum('btd,hd->bth', x, Wq) + bq
        K = jnp.einsum('btd,hd->bth', x, Wk) + bk
        V = jnp.einsum('btd,hd->bth', x, Wv) + bv
        A0 = jnp.broadcast_to(jnp.eye(H, dtype=jnp.float32) / LAMBDA_0, (B, H, H))
        M0 = jnp.zeros((B, H, H), jnp.float32)

        def step(carry, qkv):
            A, M = carry
            q, k, v = qkv
            s_t = jnp.sum(k * q, axis=-1, keepdims=True)
            u = k / (jnp.linalg.norm(k, axis=-1, keepdims=True) + EPS)
            Au = jnp.einsum('bij,bj->bi', A, u)
            denom = 1.0 + jnp.sum(u * Au, axis=-1, keepdims=True)
            A = A - jnp.einsum('bi,bj->bij', Au, Au) / denom[..., None]
            z = Au / denom
            alpha = s_t * z
            M = M + jnp.einsum('bi,bj->bij', v, alpha)
            o = jnp.einsum('bij,bj->bi', M, q)
            return ((A, M), o)
        qkv = (jnp.swapaxes(Q, 0, 1), jnp.swapaxes(K, 0, 1), jnp.swapaxes(V, 0, 1))
        _, O = jax.lax.scan(step, (A0, M0), qkv)
        O = jnp.swapaxes(O, 0, 1)
        return jnp.einsum('bth,dh->btd', O, Wo) + bo

    def _L0_ffn_ref(x, Wg, bg, We, be):
        import jax, jax.numpy as jnp
        import numpy as np
        IN_DIM = 256
        OUT_DIM = 256
        NUM_EXPERTS = 8
        TOP_K = 2
        gate = jax.nn.softmax(x @ Wg + bg, axis=-1)
        topk_vals, topk_idx = jax.lax.top_k(gate, TOP_K)
        onehot = jax.nn.one_hot(topk_idx, NUM_EXPERTS, dtype=gate.dtype)
        gate_sparse = jnp.einsum('bsk,bske->bse', topk_vals, onehot)
        gate_sparse = gate_sparse / jnp.sum(gate_sparse, axis=-1, keepdims=True)
        y = jnp.einsum('bsi,eoi->bseo', x, We) + be[None, None, :, :].transpose(0, 1, 2, 3)
        out = jnp.einsum('bseo,bse->bso', y, gate_sparse)
        return out
    x = L0_attn_x
    xn = _layernorm(x, axis=-1)
    x = x + _L0_attn_ref(xn, L0_attn_Wq, L0_attn_bq, L0_attn_Wk, L0_attn_bk, L0_attn_Wv, L0_attn_bv, L0_attn_Wo, L0_attn_bo) + _L0_ffn_ref(xn, L0_ffn_Wg, L0_ffn_bg, L0_ffn_We, L0_ffn_be)
    return x

_drawn_inputs = setup_inputs


def setup_inputs(seed=0):
    import zlib

    import numpy as np

    out = dict(_drawn_inputs(seed))
    spreads = {'L0_attn_bq': (0.0, 0.1),
     'L0_attn_bk': (0.0, 0.1),
     'L0_attn_bv': (0.0, 0.1),
     'L0_attn_bo': (0.0, 2.0),
     'L0_ffn_bg': (0.0, 2.0)}
    factors = {'L0_ffn_Wg': 8.0, 'L0_ffn_We': 8.0, 'L0_ffn_be': 191.986}
    for name, (base, spread) in spreads.items():
        noise = np.random.default_rng([zlib.crc32(name.encode()), seed]).standard_normal(out[name].shape)
        drawn = base * np.exp(spread * noise) if base else spread * noise
        out[name] = jnp.asarray(drawn.astype(out[name].dtype))
    for name, factor in factors.items():
        out[name] = (out[name] * factor).astype(out[name].dtype)
    return out
```

```python
from contextlib import ExitStack

import concourse.bass as bass
from concourse import mybir

F32 = mybir.dt.float32
ALU = mybir.AluOpType
ACT = mybir.ActivationFunctionType
AX = mybir.AxisListType.X

P = 128
LN_EPS = 1e-5
NORM_EPS = 1e-6
BLK = 32


def newton_scales(largest):
    r = (largest - 1.0) / (largest + 1.0)
    start = 2.0 / (1.0 + largest)
    scales = []
    while r * r > 1e-7:
        scales.append(2.0 / (2.0 - r * r))
        r = r * r / (2.0 - r * r)
    return start, scales + [1.0]


class Steps:

    def __init__(self, eng, sem):
        self.eng, self.sem, self.base, self.n = eng, sem, 0, 0

    def done(self, ins):
        ins.then_inc(self.sem, 1)
        self.n += 1

    def wait(self):
        self.eng.wait_ge(self.sem, self.base + self.n)

    def loop(self, i, per):
        self.start = self.base + self.n
        self.base, self.n = self.start + i * per, 0

    def end(self, rounds, per):
        assert self.n == per, (self.n, per)
        self.base, self.n = self.start + rounds * per, 0


def build(nc, x, wqkvg, bias_row, we, be_bo, wo, out):
    B, T, D = x.shape
    H = wo.shape[0]
    E = be_bo.shape[0] - 1
    DC = D // P
    K = T // P
    NP = B * K
    NQ = 3 * H + E
    NB = E * D // 512
    NJ = P // BLK
    assert B == 4 and D == 2 * H and H == P and NB == 4 and K % 2 == 0 and (K - 1) % 3 == 0

    x_v = x.rearrange("b (k p) d -> k p b d", p=P)
    out_v = out.rearrange("b (k p) d -> k p b d", p=P)
    part_dram = nc.dram_tensor("part_dram", [K, P, B, D], F32, kind="Internal").ap()

    start, scales = newton_scales(1.0 + P * (K - 1))
    NIT = len(scales) - 1

    with ExitStack() as ctx:
        def sem(name):
            return ctx.enter_context(nc.semaphore(name))

        def sb_in(stack):
            return lambda name, shape: stack.enter_context(nc.sbuf_tensor(name, shape, F32))

        def ps_in(stack):
            return lambda name, shape: stack.enter_context(nc.psum_tensor(name, shape, F32))

        sb = sb_in(ctx)
        GR = sb("GR", [P, NP, 2 * P])
        QT = sb("QT", [P, NP, P])
        V_all = sb("V_all", [P, NP, H])
        sdot = sb("sdot", [P, NP])
        RDall = sb("RDall", [P, NP])
        ident = sb("ident", [P, P])
        wo_sb = sb("wo_sb", [P, D])

        with ExitStack() as s1:
            sb = sb_in(s1)
            ps = ps_in(s1)
            we_sb = sb("we_sb", [P, DC, E * D])
            wq_sb = sb("wq_sb", [P, DC, NQ])
            bias_bc = sb("bias_bc", [P, NQ])
            bebo_sb = sb("bebo_sb", [E + 1, D])
            rev = sb("rev", [P, E])
            xbuf = [sb(f"xbuf{i}", [P, B, D]) for i in range(2)]
            xn = sb("xn", [P, B, D])
            xnT = [sb(f"xnT{i}", [P, DC, B, P]) for i in range(2)]
            qkv = sb("qkv", [P, B, NQ])
            U = sb("U", [P, B, H])
            bnst = sb("bnst", [P, B, 6])
            mdiff = sb("mdiff", [P, B])
            msum = sb("msum", [P, B, 2])
            mean = sb("mean", [P, B])
            veps = sb("veps", [P, B])
            std = sb("std", [P, B])
            rstd = sb("rstd", [P, B])
            ksq = sb("ksq", [P, B, H])
            kq = sb("kq", [P, B, H])
            ss = sb("ss", [P, B])
            nrm = sb("nrm", [P, B])
            nrme = sb("nrme", [P, B])
            rn = sb("rn", [P, B])
            gd = sb("gd", [P, B, E])
            gex = sb("gex", [P, B, E])
            gm = sb("gm", [P, B])
            g1 = sb("g1", [P, B, E])
            g2 = sb("g2", [P, B, E])
            g3 = sb("g3", [P, B, E])
            gates = [sb(f"gates{i}", [P, B, E + 1]) for i in range(2)]
            gT = sb("gT", [E + 1, B, P])
            acc = [sb(f"acc{i}", [P, B, D]) for i in range(2)]
            tmp = [sb(f"tmp{i}", [P, 2, 2, D]) for i in range(2)]

            tb = ps("tb", [P, 4, P])
            qb = [ps(f"qb{i}", [P, 512]) for i in range(2)]
            mb = [ps(f"mb{i}", [P, 2, D]) for i in range(NB)]
            psS = ps("psS", [P, B, P])

        with ExitStack() as s2:
            sb = sb_in(s2)
            ps = ps_in(s2)
            NS = 3
            Sst = [sb(f"Sst{i}", [P, B, P]) for i in range(NS)]
            X = [sb(f"X{i}", [P, B, P]) for i in range(NS)]
            Vn = [sb(f"Vn{i}", [P, B, P]) for i in range(NS)]
            AUT = [sb(f"AUT{i}", [P, B, P]) for i in range(NS)]
            twoI = sb("twoI", [P, P])
            firstI = sb("firstI", [P, P])
            pT = [ps(f"pT{i}", [P, B, P]) for i in range(NS)]
            pX = [ps(f"pX{i}", [P, B, P]) for i in range(NS)]

            work = sb("work", [NP, BLK, BLK])
            prod = sb("prod", [NP, BLK, BLK])
            keep = sb("keep", [NP, BLK, BLK])
            unit = sb("unit", [NP, BLK])
            nm = sb("nm", [NP, BLK])
            RD = sb("RD", [NP, BLK])
            YT = [sb(f"YT{i}", [P, B, BLK]) for i in range(2)]
            LT = [sb(f"LT{i}", [P, B, P]) for i in range(2)]
        with ExitStack() as s3:
            ps = ps_in(s3)
            pY = ps("pY", [P, BLK, NP])
            pP = ps("pP", [P, B, 2 * P])
            pU = ps("pU", [P, B, 2 * P])
            pWork = pP[0:NP].rearrange("p b n -> p (b n)").rearrange("p (c r) -> p c r", c=BLK)

        with ExitStack() as s4:
            sb = sb_in(s4)
            ps = ps_in(s4)
            Wst = [sb(f"Wst{i}", [P, B, P]) for i in range(2)]
            WT = sb("WT", [P, B, P])
            Vs = sb("Vs", [P, B, H])
            SD = sb("SD", [P, NP])
            upper = sb("upper", [P, P])
            PTm = sb("PTm", [P, B, P])
            MT = sb("MT", [P, B, H])
            OT = sb("OT", [P, B, P])
            xin = [sb(f"xin{i}", [P, B, D]) for i in range(2)]
            pin = [sb(f"pin{i}", [P, B, D]) for i in range(2)]
            obuf = [sb(f"obuf{i}", [P, B, D]) for i in range(2)]
            pWT = ps("pWT", [P, B, P])
            pPT = ps("pPT", [P, B, P])
            pOT = ps("pOT", [P, B, P])
            pM = ps("pM", [P, B, H])
            pOut = ps("pOut", [P, B, D])

        weights_loaded = sem("weights_loaded")
        consts_ready = sem("consts_ready")
        pool_step = sem("pool_step")
        dve_step = sem("dve_step")
        x_loaded = [sem(f"x_loaded{i}") for i in range(2)]
        var_ready = sem("var_ready")
        std_ready = sem("std_ready")
        xn_ready = sem("xn_ready")
        tb_full = sem("tb_full")
        tb_copied = sem("tb_copied")
        qb_full = [sem(f"qb_full{i}") for i in range(2)]
        qkv_ready = sem("qkv_ready")
        acc_ready = sem("acc_ready")
        squares_done = sem("squares_done")
        norm_ready = sem("norm_ready")
        logits_shifted = sem("logits_shifted")
        exp_ready = sem("exp_ready")
        gates_ready = sem("gates_ready")
        u_ready = sem("u_ready")
        v_kept = sem("v_kept")
        gram_done = sem("gram_done")
        prefix_kept = sem("prefix_kept")
        mb_full = [sem(f"mb_full{i}") for i in range(NB)]
        mb_used = [sem(f"mb_used{i}") for i in range(NB)]
        tile_summed = sem("tile_summed")
        part_stored = [sem(f"part_stored{i}") for i in range(2)]
        stage1_over = sem("stage1_over")

        s_staged = [sem(f"s_staged{i}") for i in range(NS)]
        x_init = [sem(f"x_init{i}") for i in range(NS)]
        t_full = [sem(f"t_full{i}") for i in range(NS)]
        v_ready = [sem(f"v_ready{i}") for i in range(NS)]
        x_full = [sem(f"x_full{i}") for i in range(NS)]
        x_ready = [sem(f"x_ready{i}") for i in range(NS)]
        au_full = [sem(f"au_full{i}") for i in range(NS)]
        au_ready = [sem(f"au_ready{i}") for i in range(NS)]
        g_full = [sem(f"g_full{i}") for i in range(NS)]
        g_kept = [sem(f"g_kept{i}") for i in range(NS)]
        ua_kept = [sem(f"ua_kept{i}") for i in range(NS)]

        blocks_gathered = sem("blocks_gathered")
        blocks_factored = sem("blocks_factored")
        y_transposed = sem("y_transposed")
        rd_kept = sem("rd_kept")
        yt_ready = sem("yt_ready")
        panel_full = sem("panel_full")
        panel_kept = sem("panel_kept")
        lt_ready = sem("lt_ready")
        lt_cleared = sem("lt_cleared")
        yt_cleared = sem("yt_cleared")
        update_full = sem("update_full")
        update_done = sem("update_done")

        w_staged = sem("w_staged")
        wt_full = sem("wt_full")
        wt_ready = sem("wt_ready")
        vs_ready = sem("vs_ready")
        pt_full = sem("pt_full")
        pt_masked = sem("pt_masked")
        ot_full = sem("ot_full")
        ot_ready = sem("ot_ready")
        m_full = sem("m_full")
        m_zeroed = sem("m_zeroed")
        m_kept = sem("m_kept")
        out_full = sem("out_full")
        in_loaded = [sem(f"in_loaded{i}") for i in range(2)]
        in_summed = sem("in_summed")
        out_ready = sem("out_ready")
        out_stored = [sem(f"out_stored{i}") for i in range(2)]

        block = ctx.enter_context(nc.Block())

        def grp(k):
            return bass.ds(k * B, B)

        NE = NS - 1

        @block.sync
        def _(sp):
            def load_x(k, par):
                sp.dma_start(xbuf[par][:], x_v[k]).then_inc(x_loaded[par], 16)

            load_x(0, 0)
            sp.dma_start(wq_sb[:], wqkvg.rearrange("(c p) n -> p c n", p=P)).then_inc(weights_loaded, 16)
            sp.dma_start(bias_bc[:], bias_row.partition_broadcast(P)).then_inc(weights_loaded, 16)
            load_x(1, 1)
            sp.dma_start(we_sb[:], we.rearrange("(c p) n -> p c n", p=P)).then_inc(weights_loaded, 16)
            sp.dma_start(bebo_sb[:], be_bo).then_inc(weights_loaded, 16)
            sp.dma_start(wo_sb[:], wo).then_inc(weights_loaded, 16)
            for k in (2, 3):
                sp.wait_ge(xn_ready, k - 1)
                load_x(k, k % 2)

            def store_part(k, par):
                sp.wait_ge(tile_summed, B * k + B)
                sp.dma_start(part_dram[k], acc[par][:]).then_inc(part_stored[par], 16)

            with sp.Fori(0, K // 2 - 2) as i:
                for par in range(2):
                    k = i * 2 + par
                    sp.wait_ge(xn_ready, k + 3)
                    load_x(k + 4, par)
                    store_part(k, par)
            for k in range(K - 4, K):
                store_part(k, k % 2)

            for par in range(2):
                sp.wait_ge(part_stored[par], 16 * (K // 2))
            sp.wait_ge(stage1_over, 4)
            sp.wait_ge(panel_kept, NJ * K)

            def load_in(k, par):
                sp.dma_start(xin[par][:], x_v[k]).then_inc(in_loaded[par], 16)
                sp.dma_start(pin[par][:], part_dram[k]).then_inc(in_loaded[par], 16)

            def store_out(k, par):
                sp.wait_ge(out_ready, k + 1)
                sp.dma_start(out_v[k], obuf[par][:]).then_inc(out_stored[par], 16)

            load_in(0, 0)
            load_in(1, 1)
            with sp.Fori(0, K // 2 - 1) as i:
                for par in range(2):
                    k = i * 2 + par
                    store_out(k, par)
                    load_in(k + 2, par)
            for k in range(K - 2, K):
                store_out(k, k % 2)
            for par in range(2):
                sp.wait_ge(out_stored[par], 16 * (K // 2))

        @block.gpsimd
        def _(pool):
            st = Steps(pool, pool_step)
            st.done(nc.gpsimd.memset(ident[:], 0.0))
            st.wait()
            nc.gpsimd.affine_select(out=ident[:], in_=ident[:], compare_op=ALU.not_equal, fill=1.0, base=0,
                                    pattern=[[-1, P]], channel_multiplier=1).then_inc(consts_ready, 1)
            for e in range(E):
                nc.gpsimd.memset(rev[:, e:e + 1], float(E - e))
            for par in range(2):
                nc.gpsimd.memset(gates[par][:, :, E:E + 1], 1.0).then_inc(consts_ready, 1)

            def keep_v(g):
                pool.wait_ge(qkv_ready, B * g + B)
                nc.gpsimd.tensor_copy(V_all[:, grp(g), :], qkv[:, :, 2 * H:3 * H]).then_inc(v_kept, 1)

            def sum_tiles(k, par):
                for t in range(B):
                    n = k * B + t
                    pool.wait_ge(mb_used[3], n + 1)
                    four = tmp[t % 2]
                    st.done(nc.gpsimd.tensor_tensor(four[:, 0], four[:, 0], four[:, 1], ALU.add))
                    st.wait()
                    st.done(nc.gpsimd.tensor_tensor(four[:, 0, 0], four[:, 0, 0], four[:, 0, 1], ALU.add))
                    st.wait()
                    pool.wait_ge(mb_used[2], n + 1)
                    nc.gpsimd.tensor_tensor(acc[par][:, t], four[:, 0, 0], acc[par][:, t], ALU.add)\
                        .then_inc(tile_summed, 1)

            keep_v(0)
            with pool.Fori(0, K // 2 - 1) as i:
                st.loop(i, 4 * B)
                for par in range(2):
                    keep_v(i * 2 + par + 1)
                    sum_tiles(i * 2 + par, par)
                st.end(K // 2 - 1, 4 * B)
            keep_v(K - 1)
            for k in (K - 2, K - 1):
                sum_tiles(k, k % 2)
            pool.wait_ge(tile_summed, NP)
            nc.gpsimd.sem_inc(stage1_over, 1)

            pool.wait_ge(stage1_over, 4)
            for par in range(2):
                pool.wait_ge(part_stored[par], 16 * (K // 2))
            nc.gpsimd.tensor_scalar(twoI[:], ident[:], 2.0, None, ALU.mult).then_inc(consts_ready, 1)
            nc.gpsimd.tensor_scalar(firstI[:], ident[:], 2.0 * start * scales[0], None, ALU.mult).then_inc(consts_ready, 1)
            st.done(nc.gpsimd.memset(keep[:], 1.0))
            st.wait()
            nc.gpsimd.affine_select(out=keep[:], in_=keep[:], compare_op=ALU.is_ge, fill=0.0, base=0,
                                    pattern=[[1, BLK], [-1, BLK]], channel_multiplier=0).then_inc(consts_ready, 1)
            st.done(nc.gpsimd.memset(unit[:], 0.0))
            st.wait()
            nc.gpsimd.memset(unit[:, 0:1], 1.0).then_inc(consts_ready, 1)
            with pool.Fori(0, (K - 1) // NS) as i:
                for s in range(NS):
                    pool.wait_ge(t_full[s], i * NIT + 1)
                    nc.gpsimd.tensor_copy(Sst[s][:], GR[:, grp(i * NS + (s + 1)), 0:P]).then_inc(s_staged[s], 1)

            for j in range(NJ):
                rows = slice(BLK * j, BLK * j + BLK)
                c0 = BLK * (j + 1)
                if j:
                    pool.wait_ge(update_full, j * K)
                    pool.wait_ge(panel_full, j * K)
                for par in range(2):
                    nc.gpsimd.memset(YT[par][:], 0.0).then_inc(yt_cleared, 1)
                if j == NJ - 1:
                    break
                for par in range(2):
                    nc.gpsimd.memset(LT[par][:], 0.0).then_inc(lt_cleared, 1)
                pool.wait_ge(lt_cleared, 2 * j + 2)
                pool.wait_ge(rd_kept, j + 1)

                def make_lt(g, par):
                    pool.wait_ge(panel_kept, g + (j * K + 1))
                    nc.gpsimd.tensor_tensor(LT[par][rows, :, c0:P], GR[rows, grp(g), c0:P],
                                            RDall[rows, grp(g)].unsqueeze(2).broadcast_to([BLK, B, P - c0]),
                                            ALU.mult).then_inc(lt_ready, 1)

                make_lt(0, 0)
                make_lt(1, 1)
                with pool.Fori(1, K // 2) as i:
                    for par in range(2):
                        pool.wait_ge(update_full, i * 2 + (j * K + par - 1))
                        make_lt(i * 2 + par, par)

            pool.wait_ge(panel_kept, NJ * K)
            pool.wait_ge(update_done, (NJ - 1) * K)
            st.done(nc.gpsimd.memset(upper[:], 1.0))
            st.wait()
            nc.gpsimd.affine_select(out=upper[:], in_=upper[:], compare_op=ALU.is_ge, fill=0.0, base=0,
                                    pattern=[[1, P]], channel_multiplier=-1).then_inc(consts_ready, 1)

            def stage_w(k, par, done):
                if done is not None:
                    pool.wait_ge(m_full, done)
                nc.gpsimd.tensor_copy(Wst[par][:], GR[:, grp(k), P:2 * P]).then_inc(w_staged, 1)

            def add_in(k, par, i):
                pool.wait_ge(in_loaded[par], i * 32 + 32)
                nc.gpsimd.tensor_tensor(pin[par][:], pin[par][:], xin[par][:], ALU.add).then_inc(in_summed, 1)

            stage_w(0, 0, None)
            stage_w(1, 1, None)
            with pool.Fori(0, K // 2 - 1) as i:
                for par in range(2):
                    k = i * 2 + par
                    add_in(k, par, i)
                    stage_w(k + 2, par, k + 1)
            for k in (K - 2, K - 1):
                add_in(k, k % 2, K // 2 - 1)

        @block.scalar
        def _(act):
            def copy(o, i, scale=1.0):
                return nc.scalar.activation(o, i, ACT.Copy, scale=scale)

            def sqrt_var(g):
                act.wait_ge(var_ready, g + 1)
                nc.scalar.activation(std[:], veps[:], ACT.Sqrt).then_inc(std_ready, 1)

            def front(g, par, used):
                for h in range(2):
                    act.wait_ge(tb_full, g * 5 + (h + 1))
                    if used and not (isinstance(g, int) and g < 2):
                        act.wait_ge(mb_full[NB - 1], g * B - B)
                    copy(xnT[par][:, :, 2 * h:2 * h + 2, :],
                         tb[:].rearrange("p (t c) m -> p c t m", c=DC)).then_inc(tb_copied, 1)
                for t in range(B):
                    act.wait_ge(qkv_ready, g * B + (t + 1))
                    nc.scalar.activation(ksq[:, t], qkv[:, t, H:2 * H], ACT.Square,
                                         accum_out=ss[:, t:t + 1]).then_inc(squares_done, 1)
                act.wait_ge(squares_done, g * B + B)
                nc.scalar.activation(nrm[:], ss[:], ACT.Sqrt).then_inc(norm_ready, 1)
                act.wait_ge(logits_shifted, g + 1)
                nc.scalar.activation(gex[:], gd[:], ACT.Exp).then_inc(exp_ready, 1)

            def moe(k, par, tiles, seen):
                act.wait_ge(gates_ready, k + 1)
                for t in tiles:
                    n = k * B + t
                    if seen or t >= 2:
                        act.wait_ge(tile_summed, n - 1)
                    for b, q in enumerate((1, 3)):
                        act.wait_ge(mb_full[q], n + 1)
                        for h in range(2):
                            e = 2 * q + h
                            ins = copy(tmp[t % 2][:, b, h], mb[q][:, h], gates[par][:, t, e:e + 1])
                        ins.then_inc(mb_used[q], 1)

            def back(g, par, used, stored=None):
                act.wait_ge(tb_full, g * 5 + 3)
                if used:
                    act.wait_ge(qb_full[1], g * 3)
                copy(gT[:], tb[0:E + 1]).then_inc(tb_copied, 1)
                for h in range(2):
                    act.wait_ge(tb_full, g * 5 + (4 + h))
                    uq = tb[:].rearrange("p (t a) m -> p a t m", a=2)
                    tiles = bass.ds(g * B + 2 * h, 2)
                    copy(GR[:, tiles, P:2 * P], uq[:, 0])
                    copy(QT[:, tiles, :], uq[:, 1]).then_inc(tb_copied, 1)
                for h in range(2):
                    act.wait_ge(qb_full[h], g * 3 + 3)
                    if stored is not None:
                        act.wait_ge(part_stored[par], stored * 16)
                    copy(acc[par][:, 2 * h:2 * h + 2, :],
                         qb[h][:].rearrange("p (t n) -> p t n", t=2)).then_inc(acc_ready, 1)

            sqrt_var(0)
            front(0, 0, False)
            sqrt_var(1)
            back(0, 0, False)

            def step(k, par, stored):
                front(k + 1, 1 - par, True)
                moe(k, par, (0, 1), True)
                sqrt_var(k + 2)
                moe(k, par, (2, 3), True)
                back(k + 1, 1 - par, True, stored)

            front(1, 1, True)
            moe(0, 0, (0, 1), False)
            sqrt_var(2)
            moe(0, 0, (2, 3), False)
            back(1, 1, True)
            step(1, 1, 1)
            with act.Fori(1, K // 2 - 1) as i:
                for par in range(2):
                    step(i * 2 + par, par, i + par)
            front(K - 1, 1, True)
            moe(K - 2, 0, range(B), True)
            back(K - 1, 1, True, K // 2 - 1)
            moe(K - 1, 1, range(B), True)
            act.wait_ge(mb_used[3], NP)
            nc.scalar.sem_inc(stage1_over, 1)
            act.wait_ge(stage1_over, 4)
            for par in range(2):
                act.wait_ge(part_stored[par], 16 * (K // 2))

            def products(s, k, done):
                act.wait_ge(au_full[s], done + 2)
                copy(AUT[s][:], pT[s][:]).then_inc(au_ready[s], 1)
                act.wait_ge(g_full[s], done + 1)
                copy(GR[:, grp(k), P:2 * P], pX[s][:]).then_inc(ua_kept[s], 1)

            for s in range(NS):
                nc.scalar.sem_inc(ua_kept[s], 1)
            products(0, 0, 0)
            with act.Fori(0, (K - 1) // NS) as i:
                for it in range(NIT):
                    for s in range(NS):
                        act.wait_ge(x_full[s], i * NIT + (it + 1))
                        copy(X[s][:], pX[s][:], scales[it + 1]).then_inc(x_ready[s], 1)
                for s in range(NS):
                    act.wait_ge(au_full[s], i + (2 + (s == 0)))
                    copy(AUT[s][:], pT[s][:]).then_inc(au_ready[s], 1)
                for s in range(NS):
                    act.wait_ge(g_full[s], i + (1 + (s == 0)))
                    copy(GR[:, grp(i * NS + (s + 1)), P:2 * P], pX[s][:]).then_inc(ua_kept[s], 1)

            for j in range(NJ):
                rows = slice(BLK * j, BLK * j + BLK)
                c0 = BLK * (j + 1)
                act.wait_ge(y_transposed, j + 1)
                act.wait_ge(yt_cleared, 2 * j + 2)

                def stage_yt(g, par):
                    copy(YT[par][rows], pY[0:BLK, :, grp(g)].rearrange("c i b -> c b i")).then_inc(yt_ready, 1)

                def keep_panel(g):
                    act.wait_ge(panel_full, g + (j * K + 1))
                    copy(GR[rows, grp(g), c0:2 * P], pP[0:BLK, :, c0:2 * P]).then_inc(panel_kept, 1)

                stage_yt(0, 0)
                stage_yt(1, 1)
                with act.Fori(0, K // 2 - 1) as i:
                    for par in range(2):
                        g = i * 2 + par
                        keep_panel(g)
                        stage_yt(g + 2, par)
                keep_panel(K - 2)
                keep_panel(K - 1)

            act.wait_ge(update_done, (NJ - 1) * K)
            act.wait_ge(consts_ready, 8)

            def keep_wt(k):
                act.wait_ge(wt_full, k + 1)
                copy(WT[:], pWT[:]).then_inc(wt_ready, 1)

            def keep_ot(k):
                act.wait_ge(ot_full, k + 1)
                copy(OT[:], pOT[:]).then_inc(ot_ready, 1)

            def keep_m(k):
                act.wait_ge(m_full, k + 1)
                copy(MT[:], pM[:]).then_inc(m_kept, 1)

            keep_wt(0)
            with act.Fori(0, K - 1) as k:
                keep_wt(k + 1)
                keep_ot(k)
                keep_m(k)
            keep_ot(K - 1)

        @block.vector
        def _(dve):
            st = Steps(dve, dve_step)
            v = nc.vector
            v.memset(psS[:], 0.0).then_inc(prefix_kept, 1)

            def stats_a(g, par, i):
                dve.wait_ge(x_loaded[par], i * 16 + 16)
                for t in range(B):
                    ins = v.bn_stats(bnst[:, t], xbuf[par][:, t])
                st.done(ins)
                st.wait()
                v.tensor_tensor(mdiff[:], bnst[:, :, 1], bnst[:, :, 4], ALU.subtract)
                st.done(v.tensor_tensor(msum[:], bnst[:, :, 1:3], bnst[:, :, 4:6], ALU.add))
                st.wait()
                v.tensor_scalar(mean[:], msum[:, :, 0], 0.5, None, ALU.mult)
                st.done(v.scalar_tensor_tensor(mdiff[:], mdiff[:], 0.25, mdiff[:], ALU.mult, ALU.mult))
                st.wait()
                st.done(v.scalar_tensor_tensor(veps[:], msum[:, :, 1], 1.0 / D, mdiff[:], ALU.mult, ALU.add))
                st.wait()
                v.tensor_scalar(veps[:], veps[:], LN_EPS, None, ALU.add).then_inc(var_ready, 1)

            def stats_b(g, par):
                dve.wait_ge(std_ready, g + 1)
                st.done(v.reciprocal(rstd[:], std[:]))
                st.wait()
                for t in range(B):
                    ins = v.tensor_scalar(xn[:, t], xbuf[par][:, t], mean[:, t:t + 1], rstd[:, t:t + 1],
                                          ALU.subtract, ALU.mult)
                ins.then_inc(xn_ready, 1)

            def bc(a):
                return a.unsqueeze(2).broadcast_to([P, B, E])

            def post(g, par, used):
                if used:
                    dve.wait_ge(tb_full, g * 5)
                    dve.wait_ge(v_kept, g)
                    dve.wait_ge(norm_ready, g)
                for t in range(B):
                    dve.wait_ge(qb_full[t % 2], g * 3 + (t // 2 + 1))
                    v.tensor_tensor(qkv[:, t], qb[t % 2][:, 0:NQ], bias_bc[:], ALU.add).then_inc(qkv_ready, 1)
                dve.wait_ge(qkv_ready, g * B + B)
                lg = qkv[:, :, 3 * H:NQ]
                revb = rev[:].unsqueeze(1).broadcast_to([P, B, E])
                st.done(v.tensor_reduce(gm[:], lg, AX, ALU.max))
                st.wait()
                v.tensor_tensor(gd[:], lg, bc(gm[:]), ALU.subtract).then_inc(logits_shifted, 1)
                dve.wait_ge(logits_shifted, g + 1)
                st.done(v.scalar_tensor_tensor(g1[:], gd[:], 0.0, revb, ALU.is_equal, ALU.mult))
                st.wait()
                st.done(v.tensor_reduce(gm[:], g1[:], AX, ALU.max))
                st.wait()
                st.done(v.tensor_tensor(g1[:], g1[:], bc(gm[:]), ALU.is_equal))
                st.wait()
                st.done(v.scalar_tensor_tensor(g2[:], g1[:], -3.0e38, gd[:], ALU.mult, ALU.add))
                st.wait()
                st.done(v.tensor_reduce(gm[:], g2[:], AX, ALU.max))
                st.wait()
                st.done(v.tensor_tensor(g3[:], g2[:], bc(gm[:]), ALU.is_equal))
                st.wait()
                st.done(v.tensor_tensor(g3[:], g3[:], revb, ALU.mult))
                st.wait()
                st.done(v.tensor_reduce(gm[:], g3[:], AX, ALU.max))
                st.wait()
                st.done(v.tensor_tensor(g3[:], g3[:], bc(gm[:]), ALU.is_equal))
                st.wait()
                st.done(v.tensor_tensor(g1[:], g1[:], g3[:], ALU.add))
                st.wait()
                dve.wait_ge(exp_ready, g + 1)
                st.done(v.tensor_tensor(g1[:], g1[:], gex[:], ALU.mult))
                st.wait()
                st.done(v.tensor_reduce(gm[:], g1[:], AX, ALU.add))
                st.wait()
                st.done(v.reciprocal(rn[:], gm[:]))
                st.wait()
                if used and not (isinstance(g, int) and g < 2):
                    dve.wait_ge(mb_used[3], g * B - B)
                v.tensor_tensor(gates[par][:, :, 0:E], g1[:], bc(rn[:]), ALU.mult).then_inc(gates_ready, 1)
                for t in range(B):
                    ins = v.scalar_tensor_tensor(kq[:, t], qkv[:, t, 0:H], 1.0, qkv[:, t, H:2 * H], ALU.mult,
                                                 ALU.mult, accum_out=sdot[:, bass.ds(g * B + t, 1)])
                dve.wait_ge(norm_ready, g + 1)
                st.done(v.tensor_scalar(nrme[:], nrm[:], NORM_EPS, None, ALU.add))
                dve.wait_ge(gates_ready, g + 1)
                st.wait()
                st.done(v.reciprocal(rn[:], nrme[:]))
                st.wait()
                if used:
                    dve.wait_ge(gram_done, g)
                v.tensor_tensor(U[:], qkv[:, :, H:2 * H], rn[:].unsqueeze(2).broadcast_to([P, B, H]),
                                ALU.mult).then_inc(u_ready, 1)

            POST, STATS = 16, 5

            def moe(k, par, tiles):
                dve.wait_ge(gates_ready, k + 1)
                dve.wait_ge(acc_ready, k * 2 + 2)
                for t in tiles:
                    n = k * B + t
                    for q in (0, 2):
                        dve.wait_ge(mb_full[q], n + 1)
                        for h in range(2):
                            e = 2 * q + h
                            ins = v.scalar_tensor_tensor(acc[par][:, t], mb[q][:, h], gates[par][:, t, e:e + 1],
                                                         acc[par][:, t], ALU.mult, ALU.add)
                            if h == 0:
                                st.done(ins)
                                st.wait()
                        ins.then_inc(mb_used[q], 1)
                        if q == 0:
                            dve.wait_ge(mb_used[0], n + 1)

            MOE = 2 * B

            def keep_prefix(g):
                dve.wait_ge(gram_done, g + 1)
                v.tensor_tensor(GR[:, grp(g + 1), 0:P], psS[:],
                                ident[:].unsqueeze(1).broadcast_to([P, B, P]), ALU.add).then_inc(prefix_kept, 1)

            dve.wait_ge(consts_ready, 3)
            stats_a(0, 0, 0)
            stats_b(0, 0)
            dve.wait_ge(weights_loaded, 80)
            post(0, 0, False)
            stats_a(1, 1, 0)
            dve.wait_ge(tb_full, 2)
            stats_b(1, 1)
            keep_prefix(0)

            def step(k, par, i):
                post(k + 1, 1 - par, True)
                stats_a(k + 2, par, i + 1)
                moe(k, par, (0, 1))
                dve.wait_ge(tb_full, k * 5 + 7)
                stats_b(k + 2, par)
                moe(k, par, (2, 3))
                keep_prefix(k + 1)

            step(0, 0, 0)
            step(1, 1, 0)
            with dve.Fori(0, K // 2 - 2) as i:
                st.loop(i, 2 * (POST + STATS + MOE))
                for par in range(2):
                    step(i * 2 + (2 + par), par, i + 1)
                st.end(K // 2 - 2, 2 * (POST + STATS + MOE))
            post(K - 1, 1, True)
            moe(K - 2, 0, range(B))
            moe(K - 1, 1, range(B))
            dve.wait_ge(mb_used[2], NP)
            v.sem_inc(stage1_over, 1)
            dve.wait_ge(stage1_over, 4)
            for par in range(2):
                dve.wait_ge(part_stored[par], 16 * (K // 2))
            dve.wait_ge(consts_ready, 7)

            twoIb = twoI[:].unsqueeze(1).broadcast_to([P, B, P])
            firstIb = firstI[:].unsqueeze(1).broadcast_to([P, B, P])
            identb = ident[:].unsqueeze(1).broadcast_to([P, B, P])

            def keep_g(s, k, done):
                dve.wait_ge(g_full[s], done)
                v.tensor_tensor(GR[:, grp(k), 0:P], pT[s][:], identb, ALU.add).then_inc(g_kept[s], 1)

            for s in range(NS):
                v.sem_inc(g_kept[s], 1)
            keep_g(0, 0, 1)
            with dve.Fori(0, (K - 1) // NS) as i:
                for s in range(NS):
                    dve.wait_ge(s_staged[s], i + 1)
                    dve.wait_ge(au_full[s], i + (1 + (s == 0)))
                    v.scalar_tensor_tensor(X[s][:], Sst[s][:], -scales[0] * start * start, firstIb,
                                           ALU.mult, ALU.add).then_inc(x_init[s], 1)
                for it in range(NIT):
                    for s in range(NS):
                        dve.wait_ge(t_full[s], i * NIT + (it + 2))
                        v.scalar_tensor_tensor(Vn[s][:], pT[s][:], -1.0, twoIb,
                                               ALU.mult, ALU.add).then_inc(v_ready[s], 1)
                for s in range(NS):
                    keep_g(s, i * NS + (s + 1), i + (1 + (s == 0)))

            for j in range(NJ):
                rows = slice(BLK * j, BLK * j + BLK)
                c0 = BLK * (j + 1)
                dve.wait_ge(blocks_gathered, j + 1)
                if j:
                    dve.wait_ge(y_transposed, j)
                st.done(v.tensor_copy(work[:], pWork))
                st.wait()
                for c in range(BLK):
                    st.done(v.reciprocal(RD[:, c:c + 1], work[:, c, c:c + 1]))
                    if c < BLK - 1:
                        st.wait()
                        st.done(v.tensor_scalar(nm[:, c + 1:BLK], work[:, c + 1:BLK, c], RD[:, c:c + 1], -1.0,
                                                ALU.mult, ALU.mult))
                    st.wait()
                    st.done(v.tensor_copy(work[:, c:BLK, c], unit[:, 0:BLK - c]))
                    st.wait()
                    if c < BLK - 1:
                        r = BLK - 1 - c
                        st.done(v.tensor_tensor(prod[:, 0:r], work[:, c:c + 1, :].broadcast_to([NP, r, BLK]),
                                                nm[:, c + 1:BLK].unsqueeze(2).broadcast_to([NP, r, BLK]), ALU.mult))
                        st.wait()
                        st.done(v.tensor_tensor(work[:, c + 1:BLK], work[:, c + 1:BLK], prod[:, 0:r], ALU.add))
                        st.wait()
                v.tensor_tensor(work[:], work[:], keep[:], ALU.mult).then_inc(blocks_factored, 1)
                dve.wait_ge(y_transposed, j + 1)
                v.tensor_copy(RDall[rows], pU[0:BLK, 0, 0:NP]).then_inc(rd_kept, 1)
                if j < NJ - 1:
                    hi = slice(0, P) if j == 0 else slice(c0, P)
                    with dve.Fori(0, K) as g:
                        dve.wait_ge(update_full, g + (j * K + 1))
                        v.tensor_tensor(GR[hi, grp(g), c0:2 * P], GR[hi, grp(g), c0:2 * P],
                                        pU[hi, :, c0:2 * P], ALU.subtract).then_inc(update_done, 1)

            dve.wait_ge(panel_kept, NJ * K)
            dve.wait_ge(consts_ready, 8)
            dve.wait_ge(rd_kept, NJ)
            v.memset(pM[:], 0.0).then_inc(m_zeroed, 1)
            v.memset(MT[:], 0.0).then_inc(m_zeroed, 1)
            st.done(v.tensor_tensor(SD[:], sdot[:], RDall[:], ALU.mult))
            st.wait()
            upperb = upper[:].unsqueeze(1).broadcast_to([P, B, P])

            def scale_v(k, done):
                if done is not None:
                    dve.wait_ge(m_full, done)
                v.tensor_tensor(Vs[:], V_all[:, grp(k), :], SD[:, grp(k)].unsqueeze(2).broadcast_to([P, B, H]),
                                ALU.mult).then_inc(vs_ready, 1)

            def mask_pt(k):
                dve.wait_ge(pt_full, k + 1)
                v.tensor_tensor(PTm[:], pPT[:], upperb, ALU.mult).then_inc(pt_masked, 1)

            def finish(k, par, i):
                dve.wait_ge(out_full, k + 1)
                dve.wait_ge(in_summed, k + 1)
                if i is not None:
                    dve.wait_ge(out_stored[par], i * 16)
                v.tensor_tensor(obuf[par][:], pOut[:], pin[par][:], ALU.add).then_inc(out_ready, 1)

            scale_v(0, None)
            mask_pt(0)
            for k in (0, 1):
                scale_v(k + 1, k + 1)
                mask_pt(k + 1)
                finish(k, k, None)
            with dve.Fori(1, K // 2 - 1) as i:
                for par in range(2):
                    k = i * 2 + par
                    scale_v(k + 1, k + 1)
                    mask_pt(k + 1)
                    finish(k, par, i)
            scale_v(K - 1, K - 1)
            mask_pt(K - 1)
            finish(K - 2, 0, K // 2 - 1)
            finish(K - 1, 1, K // 2 - 1)

        @block.tensor
        def _(pe):
            mm = nc.tensor.matmul
            tr = nc.tensor.transpose

            def front(g, par, used):
                pe.wait_ge(xn_ready, g + 1)
                for h in range(2):
                    if used or h:
                        pe.wait_ge(tb_copied, g * 5 + h)
                    for t in range(2):
                        for c in range(DC):
                            ins = tr(tb[:, 2 * t + c], xn[:, 2 * h + t, c * P:(c + 1) * P], ident[:])
                    ins.then_inc(tb_full, 1)
                for t in range(B):
                    if t % 2 == 0:
                        pe.wait_ge(tb_copied, g * 5 + (1 + t // 2))
                    if t >= 2:
                        pe.wait_ge(qkv_ready, g * B + (t - 1))
                    elif used:
                        pe.wait_ge(acc_ready, g * 2 + (t - 1))
                    for c in range(DC):
                        ins = mm(qb[t % 2][:, 0:NQ], xnT[par][:, c, t], wq_sb[:, c], start=(c == 0), stop=(c == DC - 1))
                    ins.then_inc(qb_full[t % 2], 1)

            def back(g, par, gram):
                pe.wait_ge(gates_ready, g + 1)
                pe.wait_ge(tb_copied, g * 5 + 2)
                for t in range(B):
                    ins = tr(tb[0:E + 1, t], gates[par][:, t], ident[:])
                ins.then_inc(tb_full, 1)
                pe.wait_ge(u_ready, g + 1)
                for h in range(2):
                    pe.wait_ge(tb_copied, g * 5 + (3 + h))
                    for t in range(2):
                        tr(tb[:, 2 * t], U[:, 2 * h + t], ident[:])
                        ins = tr(tb[:, 2 * t + 1], qkv[:, 2 * h + t, 0:H], ident[:])
                    ins.then_inc(tb_full, 1)
                    if h == 0 and gram:
                        pe.wait_ge(prefix_kept, g + 1)
                        for b in range(B):
                            ins = mm(psS[:, b], U[:, b], U[:, b], start=False, stop=True, skip_group_check=True)
                        ins.then_inc(gram_done, 1)
                for h in range(2):
                    pe.wait_ge(qkv_ready, g * B + (3 + h))
                    for t in range(2):
                        ins = mm(qb[h][:, t * D:(t + 1) * D], gT[:, 2 * h + t], bebo_sb[:], start=True, stop=True)
                    ins.then_inc(qb_full[h], 1)

            def moe(k, par, used):
                for t in range(B):
                    for q in range(NB):
                        if used or t:
                            pe.wait_ge(mb_used[q], k * B + t)
                        for c in range(DC):
                            ins = mm(mb[q][:].rearrange("p h n -> p (h n)"), xnT[par][:, c, t],
                                     we_sb[:, c, q * 512:(q + 1) * 512], start=(c == 0), stop=(c == DC - 1))
                        ins.then_inc(mb_full[q], 1)

            pe.wait_ge(consts_ready, 3)
            pe.wait_ge(weights_loaded, 80)
            front(0, 0, False)
            back(0, 0, True)
            front(1, 1, True)
            moe(0, 0, False)
            back(1, 1, True)
            front(2, 0, True)
            moe(1, 1, True)
            back(2, 0, True)
            with pe.Fori(1, K // 2 - 1) as i:
                for par in range(2):
                    k = i * 2 + par
                    front(k + 1, 1 - par, True)
                    moe(k, par, True)
                    back(k + 1, 1 - par, True)
            front(K - 1, 1, True)
            moe(K - 2, 0, True)
            back(K - 1, 1, False)
            moe(K - 1, 1, True)
            pe.wait_ge(mb_full[NB - 1], NP)
            nc.tensor.sem_inc(stage1_over, 1)
            pe.wait_ge(stage1_over, 4)
            for par in range(2):
                pe.wait_ge(part_stored[par], 16 * (K // 2))

            def au(s, k, lhs):
                for b in range(B):
                    ins = mm(pT[s][:, b], lhs(b), GR[:, bass.ds(k * B + b, 1), P:2 * P].squeeze(1), start=True, stop=True)
                ins.then_inc(au_full[s], 1)

            def gmat(s, k, done):
                pe.wait_ge(au_ready[s], done)
                for b in range(B):
                    tr(pX[s][:, b], AUT[s][:, b], ident[:])
                for b in range(B):
                    ins = mm(pT[s][:, b], AUT[s][:, b], GR[:, bass.ds(k * B + b, 1), P:2 * P].squeeze(1), start=True, stop=True)
                ins.then_inc(g_full[s], 1)

            for s in range(NS):
                nc.tensor.sem_inc(t_full[s], 1)
                nc.tensor.sem_inc(au_full[s], 1)
            pe.wait_ge(tb_copied, 5 * K)
            au(0, 0, lambda b: ident[:])
            gmat(0, 0, 1)
            with pe.Fori(0, (K - 1) // NS) as i:
                for it in range(NIT):
                    for s in range(NS):
                        if it == 0:
                            pe.wait_ge(x_init[s], i + 1)
                            pe.wait_ge(g_kept[s], i + (1 + (s == 0)))
                            pe.wait_ge(ua_kept[s], i + (1 + (s == 0)))
                        else:
                            pe.wait_ge(x_ready[s], i * NIT + it)
                        for b in range(B):
                            ins = mm(pT[s][:, b], Sst[s][:, b], X[s][:, b], start=True, stop=True)
                        ins.then_inc(t_full[s], 1)
                    for s in range(NS):
                        pe.wait_ge(v_ready[s], i * NIT + (it + 1))
                        for b in range(B):
                            ins = mm(pX[s][:, b], X[s][:, b], Vn[s][:, b], start=True, stop=True)
                        ins.then_inc(x_full[s], 1)
                for s in range(NS):
                    pe.wait_ge(x_ready[s], i * NIT + NIT)
                    au(s, i * NS + (s + 1), lambda b, s=s: X[s][:, b])
                for s in range(NS):
                    gmat(s, i * NS + (s + 1), i + (1 + (s == 0)))

            for s in range(NS):
                pe.wait_ge(g_kept[s], (K - 1) // NS + (1 + (s == 0)))
                pe.wait_ge(ua_kept[s], (K - 1) // NS + (1 + (s == 0)))
            for j in range(NJ):
                rows = slice(BLK * j, BLK * j + BLK)
                c0 = BLK * (j + 1)
                if j:
                    pe.wait_ge(update_done, j * K)
                for c in range(BLK):
                    ins = tr(pWork[:, c], GR[rows, :, BLK * j + c], ident[rows, rows])
                ins.then_inc(blocks_gathered, 1)
                pe.wait_ge(blocks_factored, j + 1)
                if j:
                    pe.wait_ge(panel_kept, j * K)
                for r in range(BLK):
                    tr(pY[0:BLK, r], work[:, r], ident[0:NP, 0:NP])
                tr(pU[0:BLK, 0, 0:NP], RD[:], ident[0:NP, 0:NP]).then_inc(y_transposed, 1)

                def panel(g, par, seen):
                    pe.wait_ge(yt_ready, g + (j * K + 1))
                    if seen:
                        pe.wait_ge(panel_kept, g + j * K)
                    for b in range(B):
                        ins = mm(pP[0:BLK, b, c0:2 * P], YT[par][:, b],
                                 GR[:, bass.ds(g * B + b, 1), c0:2 * P].squeeze(1), start=True, stop=True)
                    ins.then_inc(panel_full, 1)

                def trail(g, par, seen):
                    pe.wait_ge(lt_ready, g + (j * K + 1))
                    pe.wait_ge(rd_kept, j + 1)
                    if seen:
                        pe.wait_ge(update_done, g + j * K)
                    for b in range(B):
                        ins = mm(pU[:, b, c0:2 * P], LT[par][:, b],
                                 GR[:, bass.ds(g * B + b, 1), c0:2 * P].squeeze(1), start=True, stop=True)
                    ins.then_inc(update_full, 1)

                last = j == NJ - 1
                panel(0, 0, False)
                panel(1, 1, True)
                if not last:
                    trail(0, 0, False)
                panel(2, 0, True)
                if not last:
                    trail(1, 1, True)
                with pe.Fori(1, K // 2 - 1) as i:
                    for par in range(2):
                        g = i * 2 + par
                        panel(g + 1, 1 - par, True)
                        if not last:
                            trail(g, par, True)
                panel(K - 1, 1, True)
                if not last:
                    trail(K - 2, 0, True)
                    trail(K - 1, 1, True)

            def q_of(k, b):
                return QT[:, bass.ds(k * B + b, 1), :].squeeze(1)

            def w_transpose(k, par):
                pe.wait_ge(w_staged, k + 1)
                for b in range(B):
                    ins = tr(pWT[:, b], Wst[par][:, b], ident[:])
                ins.then_inc(wt_full, 1)

            def pt(k):
                pe.wait_ge(wt_ready, k + 1)
                for b in range(B):
                    ins = mm(pPT[:, b], WT[:, b], q_of(k, b), start=True, stop=True)
                ins.then_inc(pt_full, 1)

            def ot(k, seen):
                pe.wait_ge(vs_ready, k + 1)
                pe.wait_ge(pt_masked, k + 1)
                if seen:
                    pe.wait_ge(m_kept, k)
                    pe.wait_ge(ot_ready, k)
                for b in range(B):
                    mm(pOT[:, b], MT[:, b], q_of(k, b), start=True, stop=False)
                    ins = mm(pOT[:, b], Vs[:, b], PTm[:, b], start=False, stop=True)
                ins.then_inc(ot_full, 1)

            def m_update(k, par):
                for b in range(B):
                    ins = mm(pM[:, b], Wst[par][:, b], Vs[:, b], start=False, stop=True, skip_group_check=True)
                ins.then_inc(m_full, 1)

            def project(k, seen):
                pe.wait_ge(ot_ready, k + 1)
                if seen:
                    pe.wait_ge(out_ready, k)
                for b in range(B):
                    ins = mm(pOut[:, b], OT[:, b], wo_sb[:], start=True, stop=True)
                ins.then_inc(out_full, 1)

            pe.wait_ge(panel_kept, NJ * K)
            pe.wait_ge(update_done, (NJ - 1) * K)
            pe.wait_ge(m_zeroed, 2)
            w_transpose(0, 0)
            pt(0)

            def step(k, par, seen):
                w_transpose(k + 1, 1 - par)
                ot(k, seen)
                m_update(k, par)
                pt(k + 1)
                project(k, seen)

            step(0, 0, False)
            step(1, 1, True)
            with pe.Fori(1, K // 2 - 1) as i:
                for par in range(2):
                    step(i * 2 + par, par, True)
            step(K - 2, 0, True)
            ot(K - 1, True)
            project(K - 1, True)


_OUT = ((4, 2048, 256), "float32")


def kernel(**inputs):
    import numpy as np
    import concourse.bacc as bacc
    from concourse.bass_utils import run_bass_kernel_spmd

    a = {name: np.asarray(value) for name, value in inputs.items()}
    E, O, D = a["L0_ffn_We"].shape
    arrays = {
        "x": a["L0_attn_x"],
        "wqkvg": np.concatenate([a["L0_attn_Wq"].T, a["L0_attn_Wk"].T, a["L0_attn_Wv"].T, a["L0_ffn_Wg"]], axis=1),
        "bias_row": np.concatenate([a["L0_attn_bq"], a["L0_attn_bk"], a["L0_attn_bv"], a["L0_ffn_bg"]]),
        "we": a["L0_ffn_We"].transpose(2, 0, 1).reshape(D, E * O),
        "be_bo": np.concatenate([a["L0_ffn_be"], a["L0_attn_bo"][None]], axis=0),
        "wo": a["L0_attn_Wo"].T,
    }
    nc = bacc.Bacc("TRN2", target_bir_lowering=False, num_devices=1)
    ins, args = {}, []
    for name, value in arrays.items():
        value = np.ascontiguousarray(value)
        ins[f"in_{name}"] = value
        args.append(nc.dram_tensor(f"in_{name}", value.shape, mybir.dt.from_np(value.dtype), kind="ExternalInput").ap())
    shape, dtype = _OUT
    args.append(nc.dram_tensor("out_0", shape, mybir.dt.from_np(np.dtype(dtype)), kind="ExternalOutput").ap())
    build(nc, *args)
    r = run_bass_kernel_spmd(nc, [ins], core_ids=[0])
    return r.results[0]["out_0"]
```

```python
from contextlib import ExitStack

import concourse.bass as bass
from concourse import mybir

F32 = mybir.dt.float32
F32R = mybir.dt.float32r
BF16 = mybir.dt.bfloat16
F16 = mybir.dt.float16
ALU = mybir.AluOpType
ACT = mybir.ActivationFunctionType
AX = mybir.AxisListType.X

P = 128
LN_EPS = 1e-5
NORM_EPS = 1e-6
BLK = 32


def newton_scales(largest):
    r = (largest - 1.0) / (largest + 1.0)
    start = 2.0 / (1.0 + largest)
    scales = []
    while r * r > 1e-7:
        scales.append(2.0 / (2.0 - r * r))
        r = r * r / (2.0 - r * r)
    return start, scales + [1.0]


class Steps:

    def __init__(self, eng, sem):
        self.eng, self.sem, self.base, self.n = eng, sem, 0, 0

    def done(self, ins):
        ins.then_inc(self.sem, 1)
        self.n += 1

    def wait(self):
        self.eng.wait_ge(self.sem, self.base + self.n)

    def loop(self, i, per):
        self.start = self.base + self.n
        self.base, self.n = self.start + i * per, 0

    def end(self, rounds, per):
        assert self.n == per, (self.n, per)
        self.base, self.n = self.start + rounds * per, 0


def build(nc, x, wqkvg, bias_row, we, be_bo, wo, out):
    B, T, D = x.shape
    H = wo.shape[0]
    E = be_bo.shape[0] - 1
    DC = D // P
    K = T // P
    NP = B * K
    NQ = 3 * H + E
    NB = E * D // 512
    HALF = P // 2
    NJ = HALF // BLK

    x_v = x.rearrange("b (k p) d -> k p b d", p=P)
    out_v = out.rearrange("b (k p) d -> k p b d", p=P)
    part_dram = nc.dram_tensor("part_dram", [K, P, B, D], F32, kind="Internal").ap()
    v_dram = nc.dram_tensor("v_dram", [K, P, B, H], F32, kind="Internal").ap()
    M1 = K
    MJ = (2 * K - M1) // NJ
    SLOT = BLK // MJ
    assert (2 * K - M1) % NJ == 0 and M1 % 2 == 0 and MJ % 2 == 0 and SLOT == 4

    start, scales = newton_scales(1.0 + P * (K - 1))
    NIT = len(scales) - 1
    start64, scales64 = newton_scales(1.0 + HALF)
    NIT64 = len(scales64) - 1
    LOW, LOW64 = NIT - 3, NIT64 - 2
    GROWS = B * 3 * (E + 1)
    X16 = 64.0
    NS = 4
    NR, NR64 = K // NS, K // NS // 2
    STEPS1 = NR * NIT

    assert B == 4 and D == 2 * H and H == P and NB == 4 and K % (2 * NS) == 0 and LOW > 0 and LOW64 > 0

    with ExitStack() as ctx:
        def sem(name):
            return ctx.enter_context(nc.semaphore(name))

        def sb_in(stack):
            return lambda name, shape, dt=F32: stack.enter_context(nc.sbuf_tensor(name, shape, dt))

        def ps_in(stack):
            return lambda name, shape: stack.enter_context(nc.psum_tensor(name, shape, F32))

        sb = sb_in(ctx)
        GR = sb("GR", [P, NP, 2 * P])
        QT = sb("QT", [P, NP, P])
        sdot = sb("sdot", [P, NP])
        RDall = sb("RDall", [P, NP])
        ident = sb("ident", [P, P])
        mean = sb("mean", [P, NP])
        rstd = sb("rstd", [P, NP])
        gates = sb("gates", [P, NP, E + 1])

        with ExitStack() as sm:
            sb = sb_in(sm)
            we_hi = sb("we_hi", [P, DC, E * D], F32R)
            we_lo = sb("we_lo", [P, DC, E * D], F32R)
            xm = [sb(f"xm{i}", [P, 2, D]) for i in range(2)]
            xh = [sb(f"xh{i}", [P, DC, 2, P], F32R) for i in range(2)]
            xl = [sb(f"xl{i}", [P, DC, 2, P], F32R) for i in range(2)]
            acc = [sb(f"acc{i}", [P, 2, D]) for i in range(2)]
            tmp = [sb(f"tmp{i}", [P, 2, 2, D]) for i in range(2)]

            with ExitStack() as s1:
                sb = sb_in(s1)
                ps = ps_in(s1)
                wq_hi = sb("wq_hi", [P, DC, NQ], F32R)
                wq_lo = sb("wq_lo", [P, DC, NQ], F32R)
                bias_bc = sb("bias_bc", [P, NQ])
                rev = sb("rev", [P, E])
                xbuf = [sb(f"xbuf{i}", [P, B, D]) for i in range(2)]
                qh = sb("qh", [P, DC, B, P], F32R)
                ql = sb("ql", [P, DC, B, P], F32R)
                qkv = sb("qkv", [P, B, NQ])
                bnst = sb("bnst", [P, B, 6])
                mdiff = sb("mdiff", [P, B])
                msum = sb("msum", [P, B, 2])
                veps = sb("veps", [P, B])
                std = sb("std", [P, B])
                ksq = sb("ksq", [P, B, H], BF16)
                kq = sb("kq", [P, B, H], BF16)
                ss = sb("ss", [P, B])
                nrm = sb("nrm", [P, B])
                nrme = sb("nrme", [P, B])
                rn = sb("rn", [P, B])
                gsum = sb("gsum", [P, B])
                gd = sb("gd", [P, B, E])
                gex = sb("gex", [P, B, E])
                gm = sb("gm", [P, B])
                g1 = sb("g1", [P, B, E])
                g2 = sb("g2", [P, B, E])
                g3 = sb("g3", [P, B, E])

                tb = ps("tb", [P, 4, P])
                qb = [ps(f"qb{i}", [P, 512]) for i in range(2)]
                psS = ps("psS", [P, B, P])
                mb = [ps(f"mb{i}", [P, 2, D]) for i in range(NB)]

            we_land = GR[:, NP - 16:NP, :].rearrange("p a n -> p (a n)").rearrange("p (c n) -> p c n", c=DC)
            wq_land = GR[:, NP - 20:NP - 16, :].rearrange("p a n -> p (a n)")[:, 0:DC * NQ]\
                .rearrange("p (c n) -> p c n", c=DC)

            with ExitStack() as s2f:
                sb = sb_in(s2f)
                X = [sb(f"X{i}", [P, B, P]) for i in range(NS)]
                Vn = [sb(f"Vn{i}", [P, B, P]) for i in range(NS)]
            with ExitStack() as s2:
                sb = sb_in(s2)
                ps = ps_in(s2)
                Xr = [sb(f"Xr{i}", [P, 2, B, P], F16)[:, 0] for i in range(NS)]
                Vr = [sb(f"Vr{i}", [P, 2, B, P], F16)[:, 0] for i in range(NS)]
                Sst = [sb(f"Sst{i}", [P, B, P]) for i in range(NS)]
                Sr = [sb(f"Sr{i}", [P, B, P], F16) for i in range(NS)]
                twoI = sb("twoI", [P, P])
                firstI = sb("firstI", [P, P])
                firstI64 = sb("firstI64", [P, P])
                Xodd = [sb(f"Xodd{i}", [HALF, B, HALF]) for i in range(NS)]
                Fst = [t[0:HALF].rearrange("r b (h c) -> r (b h) c", h=2).rearrange("r (h b) c -> r h b c", h=2)
                       for t in Vn]
                pT = [ps(f"pT{i}", [P, B, P]) for i in range(NS)]
                pX = [ps(f"pX{i}", [P, B, P]) for i in range(NS)]
            with ExitStack() as s2b:
                ps = ps_in(s2b)
                pF = [ps(f"pF{i}", [P, 2, B, HALF]) for i in range(NS)]
                pV = [ps(f"pV{i}", [P, B, 2 * P]) for i in range(2)]

            with ExitStack() as s3b:
                sb = sb_in(s3b)
                work = sb("work", [P, BLK, BLK])
                prod = sb("prod", [P, BLK, BLK])
                below = sb("below", [P, BLK, BLK])
                RD = sb("RD", [P, BLK])
                YTs = sb("YTs", [P, NP, BLK])
                YT = [sb(f"YT{i}", [P, B, P]) for i in range(2)]
                LT = [sb(f"LT{i}", [P, B, P]) for i in range(2)]
            with ExitStack() as s3:
                ps = ps_in(s3)
                pP = ps("pP", [P, B, 2 * P])
                pU = ps("pU", [P, B, 2 * P])
                pYb = ps("pYb", [P, BLK // 2, P])
                pWork = pP[:].rearrange("p b n -> p (b n)").rearrange("p (c r) -> p c r", c=BLK)

            with ExitStack() as s3c:
                pYa = ps_in(s3c)("pYa", [P, BLK // 2, P])

        with ExitStack() as s4:
            sb = sb_in(s4)
            ps = ps_in(s4)
            YTs4 = sb("YTs4", [P, NP, BLK])
            YT4 = [sb(f"YTl{i}", [P, B, P]) for i in range(2)]
            Wst = [sb(f"Wst{i}", [P, B, P]) for i in range(2)]
            WT = sb("WT", [P, B, P])
            wo_sb = sb("wo_sb", [P, D])
            g_hi = sb("g_hi", [P, NP, E + 1], F32R)
            g_parts = sb("g_parts", [P, NP, 3, E + 1])
            be_land = sb("be_land", [GROWS, D])
            be_hi = sb("be_hi", [GROWS, D], F32R)
            be_lo = sb("be_lo", [GROWS, D])
            mask_hi = sb("mask_hi", [P, B])
            mask_lo = sb("mask_lo", [P, B])
            bebo4 = sb("bebo4", [GROWS, B, D], F32R)
            gst = sb("gst", [P, P])
            gT = sb("gT", [P, P], F32R)
            Vs = sb("Vs", [P, B, H])
            SD = sb("SD", [P, NP])
            upper = sb("upper", [P, P])
            PTm = sb("PTm", [P, B, P])
            MT = sb("MT", [P, B, H])
            OT = sb("OT", [P, B, P])
            xin = [sb(f"xin{i}", [P, B, D]) for i in range(2)]
            pin = [sb(f"pin{i}", [P, B, D]) for i in range(2)]
            vin = [sb(f"vin{i}", [P, B, H]) for i in range(2)]
            obuf = [sb(f"obuf{i}", [P, B, D]) for i in range(2)]
            pWT = ps("pWT", [P, B, P])
            pPT = ps("pPT", [P, B, P])
            pOT = ps("pOT", [P, B, P])
            pM = ps("pM", [P, B, H])
            pOut = ps("pOut", [P, B, D])
            pG = ps("pG", [P, 512])
            pW = ps("pW", [P, B, P])

        wq_loaded = sem("wq_loaded")
        we_loaded = sem("we_loaded")
        wq_split = sem("wq_split")
        we_hi_ready = sem("we_hi_ready")
        we_split = sem("we_split")
        consts_ready = sem("consts_ready")
        pool_step = sem("pool_step")
        dve_step = sem("dve_step")
        x_loaded = [sem(f"x_loaded{i}") for i in range(2)]
        var_ready = sem("var_ready")
        std_ready = sem("std_ready")
        xn_ready = sem("xn_ready")
        xT_full = sem("xT_full")
        xT_hi = sem("xT_hi")
        xT_lo = sem("xT_lo")
        uq_full = sem("uq_full")
        uq_kept = sem("uq_kept")
        qb_full = [sem(f"qb_full{i}") for i in range(2)]
        qkv_ready = sem("qkv_ready")
        squares_done = sem("squares_done")
        norm_ready = sem("norm_ready")
        logits_shifted = sem("logits_shifted")
        exp_ready = sem("exp_ready")
        gates_ready = sem("gates_ready")
        u_ready = sem("u_ready")
        v_stored = sem("v_stored")
        gram_done = sem("gram_done")
        prefix_kept = sem("prefix_kept")
        stage1_over = sem("stage1_over")

        xm_loaded = [sem(f"xm_loaded{i}") for i in range(2)]
        xm_ready = sem("xm_ready")
        xmT_full = sem("xmT_full")
        xm_hi = sem("xm_hi")
        xm_lo = sem("xm_lo")
        mb_full = [sem(f"mb_full{i}") for i in range(NB)]
        mb_used = [sem(f"mb_used{i}") for i in range(NB)]
        tile_summed = sem("tile_summed")
        part_stored = [sem(f"part_stored{i}") for i in range(2)]

        s_staged = [sem(f"s_staged{i}") for i in range(NS)]
        x_init = [sem(f"x_init{i}") for i in range(NS)]
        t_full = [sem(f"t_full{i}") for i in range(NS)]
        v_ready = [sem(f"v_ready{i}") for i in range(NS)]
        x_full = [sem(f"x_full{i}") for i in range(NS)]
        x_ready = [sem(f"x_ready{i}") for i in range(NS)]
        au_full = [sem(f"au_full{i}") for i in range(NS)]
        au_ready = [sem(f"au_ready{i}") for i in range(NS)]
        g_full = [sem(f"g_full{i}") for i in range(NS)]
        g_kept = [sem(f"g_kept{i}") for i in range(NS)]
        ua_kept = [sem(f"ua_kept{i}") for i in range(NS)]

        s16_staged = [sem(f"s16_staged{i}") for i in range(NS)]
        s64_staged = sem("s64_staged")
        xodd_ready = sem("xodd_ready")
        f_full = sem("f_full")
        f_ready = sem("f_ready")
        half_full = sem("half_full")
        half_done = sem("half_done")
        consts3 = sem("consts3")
        blocks_gathered = sem("blocks_gathered")
        blocks_copied = sem("blocks_copied")
        blocks_factored = sem("blocks_factored")
        y_full = sem("y_full")
        y_kept = sem("y_kept")
        y_rd_kept = sem("y_rd_kept")
        rd_kept = sem("rd_kept")
        yt_ready = sem("yt_ready")
        panel_full = sem("panel_full")
        panel_kept = sem("panel_kept")
        lt_ready = sem("lt_ready")
        update_full = sem("update_full")
        update_done = sem("update_done")

        yt4_set = sem("yt4_set")
        w_full = sem("w_full")
        w_staged = sem("w_staged")
        gates_split = sem("gates_split")
        be_ready = sem("be_ready")
        out_weights_loaded = sem("out_weights_loaded")
        gates_staged = sem("gates_staged")
        gt_full = sem("gt_full")
        gt_ready = sem("gt_ready")
        wt_full = sem("wt_full")
        wt_ready = sem("wt_ready")
        vs_ready = sem("vs_ready")
        pt_full = sem("pt_full")
        pt_masked = sem("pt_masked")
        ot_full = sem("ot_full")
        ot_ready = sem("ot_ready")
        m_full = sem("m_full")
        m_zeroed = sem("m_zeroed")
        m_kept = sem("m_kept")
        out_full = sem("out_full")
        in_loaded = [sem(f"in_loaded{i}") for i in range(2)]
        in_summed = sem("in_summed")
        v_loaded = [sem(f"v_loaded{i}") for i in range(2)]
        out_ready = sem("out_ready")
        out_stored = [sem(f"out_stored{i}") for i in range(2)]

        block = ctx.enter_context(nc.Block())

        def within(g, n):
            return not isinstance(g, int) or g < n

        def steps_beside_stage1(eng, step, loop=lambda i: None, end=lambda: None):
            step(0, 0, 0)
            step(1, 1, 0)
            with eng.Fori(1, M1 // 2 - 2) as i:
                loop(i - 1)
                for par in range(2):
                    step(i * 2 + par, par, i)
                end()
            for k in range(M1 - 4, M1):
                step(k, k % 2, k // 2)

        def grp(k):
            return bass.ds(k * B, B)

        CONSTS = 9

        @block.sync
        def _(sp):
            def load_x(k, par):
                sp.dma_start(xbuf[par][:], x_v[k]).then_inc(x_loaded[par], 16)

            def load_xm(k, par):
                sp.dma_start(xm[par][:], x_v[k][:, 2 * par:2 * par + 2]).then_inc(xm_loaded[par], 16)

            def store_part(m, k, par):
                sp.wait_ge(tile_summed, m * 2 + 2)
                sp.dma_start(part_dram[k][:, 2 * par:2 * par + 2], acc[par][:]).then_inc(part_stored[par], 16)

            def store_v(g):
                sp.wait_ge(qkv_ready, g * B + B)
                sp.dma_start(v_dram[g], qkv[:, :, 2 * H:3 * H]).then_inc(v_stored, 16)

            load_x(0, 0)
            sp.dma_start(wq_land, wqkvg.rearrange("(c p) n -> p c n", p=P)).then_inc(wq_loaded, 16)
            sp.dma_start(bias_bc[:], bias_row.partition_broadcast(P)).then_inc(wq_loaded, 16)
            load_x(1, 1)
            load_xm(0, 0)
            load_xm(0, 1)
            sp.dma_start(we_land, we.rearrange("(c p) n -> p c n", p=P)).then_inc(we_loaded, 16)
            store_v(0)
            for g in range(2):
                sp.wait_ge(xT_full, 2 * g + 2)
                load_x(g + 2, g)
            sp.wait_ge(xmT_full, 1)
            load_xm(1, 0)

            def step(k, par, i):
                if within(k + 1, K):
                    store_v(k + 1)
                if within(k + 4, K):
                    sp.wait_ge(xT_full, k * 2 + 6)
                    load_x(k + 4, par)
                if within(k + 3, 2 * K):
                    sp.wait_ge(xmT_full, k + 2)
                    load_xm(i + 1 + par, 1 - par)
                store_part(k, i, par)

            steps_beside_stage1(sp, step)
            for m in range(M1, 2 * K):
                step(m, m % 2, m // 2)

            for par in range(2):
                sp.wait_ge(part_stored[par], 16 * K)
            sp.wait_ge(v_stored, 16 * K)
            sp.wait_ge(y_full, 3 * NJ)

            def load_v(k, par):
                sp.dma_start(vin[par][:], v_dram[k]).then_inc(v_loaded[par], 16)

            def load_in(k, par):
                sp.dma_start(xin[par][:], x_v[k]).then_inc(in_loaded[par], 16)
                sp.dma_start(pin[par][:], part_dram[k]).then_inc(in_loaded[par], 16)

            def store_out(k, par):
                sp.wait_ge(out_ready, k + 1)
                sp.dma_start(out_v[k], obuf[par][:]).then_inc(out_stored[par], 16)

            load_v(0, 0)
            load_v(1, 1)
            sp.dma_start(wo_sb[:], wo).then_inc(out_weights_loaded, 16)
            for n in range(B * 3):
                sp.dma_start(be_land[(E + 1) * n:(E + 1) * (n + 1), :], be_bo).then_inc(out_weights_loaded, 16)
            load_in(0, 0)
            load_in(1, 1)
            with sp.Fori(0, K // 2 - 1) as i:
                for par in range(2):
                    k = i * 2 + par
                    sp.wait_ge(vs_ready, k + 1)
                    load_v(k + 2, par)
                    store_out(k, par)
                    load_in(k + 2, par)
            for k in range(K - 2, K):
                store_out(k, k % 2)
            for par in range(2):
                sp.wait_ge(out_stored[par], 16 * (K // 2))

        @block.gpsimd
        def _(pool):
            st = Steps(pool, pool_step)
            st.done(nc.gpsimd.memset(ident[:], 0.0))
            st.wait()
            nc.gpsimd.affine_select(out=ident[:], in_=ident[:], compare_op=ALU.not_equal, fill=1.0, base=0,
                                    pattern=[[-1, P]], channel_multiplier=1).then_inc(consts_ready, 1)
            for e in range(E):
                nc.gpsimd.memset(rev[:, e:e + 1], float(E - e))
            nc.gpsimd.memset(gates[:], 1.0).then_inc(consts_ready, 1)
            pool.wait_ge(consts_ready, 2)
            nc.gpsimd.tensor_copy(GR[:, 0:B, 0:P], ident[:].unsqueeze(1).broadcast_to([P, B, P]))\
                .then_inc(consts_ready, 1)

            def sum_tiles(m, par):
                for t in range(2):
                    n = m * 2 + t
                    four = tmp[t]
                    pool.wait_ge(mb_used[3], n + 1)
                    st.done(nc.gpsimd.tensor_tensor(four[:, 0], four[:, 0], four[:, 1], ALU.add))
                    st.wait()
                    st.done(nc.gpsimd.tensor_tensor(four[:, 0, 0], four[:, 0, 0], four[:, 0, 1], ALU.add))
                    st.wait()
                    pool.wait_ge(mb_used[2], n + 1)
                    nc.gpsimd.tensor_tensor(acc[par][:, t], four[:, 0, 0], acc[par][:, t], ALU.add)\
                        .then_inc(tile_summed, 1)

            with pool.Fori(0, M1 // 2) as i:
                st.loop(i, 8)
                for par in range(2):
                    sum_tiles(i * 2 + par, par)
                st.end(M1 // 2, 8)

            pool.wait_ge(stage1_over, 3)
            pool.wait_ge(v_stored, 16 * K)
            nc.gpsimd.tensor_scalar(twoI[:], ident[:], 2.0, None, ALU.mult).then_inc(consts_ready, 1)
            nc.gpsimd.tensor_scalar(firstI[:], ident[:], X16 * 2.0 * start * scales[0], None, ALU.mult).then_inc(consts_ready, 1)
            nc.gpsimd.tensor_scalar(firstI64[:], ident[:], X16 * 2.0 * start64 * scales64[0], None, ALU.mult)\
                .then_inc(consts_ready, 1)

            def stage_s(k, s, to, staged):
                nc.gpsimd.tensor_copy(to[s][:], GR[:, grp(k), 0:P]).then_inc(staged[s], 1)

            for s in range(NS):
                stage_s(s, s, Sr, s16_staged)
            with pool.Fori(0, NR - 1) as i:
                for s in range(NS):
                    pool.wait_ge(t_full[s], i * NIT + 1)
                    stage_s(i * NS + s, s, Sst, s_staged)
                for s in range(NS):
                    pool.wait_ge(t_full[s], i * NIT + (LOW + 1))
                    stage_s(i * NS + (NS + s), s, Sr, s16_staged)
            for s in range(NS):
                pool.wait_ge(t_full[s], (NR - 1) * NIT + 1)
                stage_s((NR - 1) * NS + s, s, Sst, s_staged)

            pool.wait_ge(half_done, K)

            st.done(nc.gpsimd.memset(below[:], 1.0))
            st.wait()
            nc.gpsimd.affine_select(out=below[:], in_=below[:], compare_op=ALU.is_gt, fill=0.0, base=0,
                                    pattern=[[1, BLK], [-1, BLK]], channel_multiplier=0).then_inc(consts3, 1)
            def block_rows(j, h):
                return slice(HALF * h + BLK * j, HALF * h + BLK * (j + 1))

            for j in range(NJ):
                if j:
                    pool.wait_ge(panel_full, j * K)
                    pool.wait_ge(update_full, j * K)
                last = j == NJ - 1
                for par in range(0 if last else 2):
                    st.done(nc.gpsimd.tensor_copy(YT[par][:], ident[:].unsqueeze(1).broadcast_to([P, B, P])))
                    st.done(nc.gpsimd.memset(LT[par][:], 0.0))
                for m in range(M1 + j * MJ, M1 + j * MJ + MJ):
                    sum_tiles(m, m % 2)
                pool.wait_ge(tile_summed, 2 * (m + 1))
                if last:
                    break
                pool.wait_ge(y_kept, j + 1)
                pool.wait_ge(y_rd_kept, 2 * (j + 1))

                def stage_yt(g, par):
                    for h in range(2):
                        rows = block_rows(j, h)
                        nc.gpsimd.tensor_copy(YT[par][rows, :, rows], YTs[rows, grp(g), :]).then_inc(yt_ready, 1)
                        pool.wait_ge(yt_ready, g * 2 + (2 * j * K + h + 1))

                def make_lt(g, par):
                    pool.wait_ge(panel_kept, g + (j * K + 1))
                    for h in range(2):
                        rows = block_rows(j, h)
                        cols = block_rows(j + 1, h)
                        nc.gpsimd.tensor_tensor(LT[par][rows, :, cols], GR[rows, grp(g), cols],
                                                RDall[rows, grp(g)].unsqueeze(2).broadcast_to([BLK, B, BLK]),
                                                ALU.mult).then_inc(lt_ready, 1)
                        pool.wait_ge(lt_ready, g * 2 + (2 * j * K + h + 1))

                def step(g, par):
                    pool.wait_ge(panel_full, g + (j * K + 1))
                    stage_yt(g + 2, par)
                    if not (isinstance(g, int) and g < 2):
                        pool.wait_ge(update_full, g + (j * K - 1))
                    make_lt(g, par)

                stage_yt(0, 0)
                stage_yt(1, 1)
                step(0, 0)
                step(1, 1)
                with pool.Fori(1, K // 2 - 1) as i:
                    for par in range(2):
                        step(i * 2 + par, par)
                for g in (K - 2, K - 1):
                    pool.wait_ge(update_full, g + j * K - 1)
                    make_lt(g, g % 2)

            pool.wait_ge(y_full, 3 * NJ)
            pool.wait_ge(y_kept, NJ)
            pool.wait_ge(y_rd_kept, 2 * NJ)
            pool.wait_ge(yt4_set, 2)

            def stage_yt4(g, par, done):
                if done is not None:
                    pool.wait_ge(w_full, done)
                for h in range(2):
                    rows = block_rows(NJ - 1, h)
                    nc.gpsimd.tensor_copy(YT4[par][rows, :, rows], YTs4[rows, grp(g), :]).then_inc(yt_ready, 1)
                    pool.wait_ge(yt_ready, g * 2 + (2 * (NJ - 1) * K + h + 1))

            stage_yt4(0, 0, None)
            stage_yt4(1, 1, None)
            for par in range(2):
                pool.wait_ge(part_stored[par], 16 * K)
            st.done(nc.gpsimd.memset(upper[:], 1.0))
            st.done(nc.gpsimd.memset(mask_hi[:], 1.0))
            st.done(nc.gpsimd.memset(mask_lo[:], 1.0))
            st.done(nc.gpsimd.memset(gst[:], 0.0))
            st.wait()
            nc.gpsimd.affine_select(out=upper[:], in_=upper[:], compare_op=ALU.is_ge, fill=0.0, base=0,
                                    pattern=[[1, P]], channel_multiplier=-1).then_inc(consts_ready, 1)
            for mask, lo, hi in ((mask_hi, 0, 2), (mask_lo, 2, 3)):
                step = 3 * (E + 1)
                st.done(nc.gpsimd.affine_select(out=mask[:], in_=mask[:], compare_op=ALU.is_ge, fill=0.0,
                                                base=-lo * (E + 1), pattern=[[-step, B]], channel_multiplier=1))
                st.wait()
                nc.gpsimd.affine_select(out=mask[:], in_=mask[:], compare_op=ALU.is_ge, fill=0.0,
                                        base=hi * (E + 1) - 1, pattern=[[step, B]], channel_multiplier=-1)\
                    .then_inc(consts_ready, 1)

            def stage_gates(k):
                if not (isinstance(k, int) and k == 0):
                    pool.wait_ge(gt_full, k)
                nc.gpsimd.tensor_copy(gst[:, 0:GROWS].rearrange("p (b f) -> p b f", b=B),
                                      g_parts[:, grp(k)].rearrange("p b a e -> p b (a e)")).then_inc(gates_staged, 1)

            def add_in(k, par, i):
                pool.wait_ge(in_loaded[par], i * 32 + 32)
                nc.gpsimd.tensor_tensor(pin[par][:], pin[par][:], xin[par][:], ALU.add).then_inc(in_summed, 1)

            pool.wait_ge(gates_split, 2)
            stage_gates(0)
            pool.wait_ge(gates_staged, 1)
            with pool.Fori(0, K // 2 - 1) as i:
                for par in range(2):
                    k = i * 2 + par
                    stage_yt4(k + 2, par, k + 1)
                    stage_gates(k + 1)
                    add_in(k, par, i)
                    pool.wait_ge(gates_staged, k + 2)
                    pool.wait_ge(in_summed, k + 1)
            stage_gates(K - 1)
            for k in (K - 2, K - 1):
                add_in(k, k % 2, K // 2 - 1)

        @block.scalar
        def _(act):
            def copy(o, i, scale=1.0):
                return nc.scalar.activation(o, i, ACT.Copy, scale=scale)

            def sqrt_var(g):
                act.wait_ge(var_ready, g + 1)
                nc.scalar.activation(std[:], veps[:], ACT.Sqrt).then_inc(std_ready, 1)

            def xm_high(m, par, used):
                act.wait_ge(xmT_full, m + 1)
                if used:
                    act.wait_ge(mb_full[NB - 1], m * 2 - 2)
                copy(xh[par][:], tb[:].rearrange("p (t c) m -> p c t m", c=DC)).then_inc(xm_hi, 1)

            def x_high(g, h):
                act.wait_ge(xT_full, g * 2 + (h + 1))
                if not (isinstance(g, int) and g == 0):
                    act.wait_ge(qb_full[1], g * 2)
                copy(qh[:, :, 2 * h:2 * h + 2, :],
                     tb[:].rearrange("p (t c) m -> p c t m", c=DC)).then_inc(xT_hi, 1)

            def norms(g):
                for t in range(B):
                    act.wait_ge(qkv_ready, g * B + (t + 1))
                    nc.scalar.activation(ksq[:, t], qkv[:, t, H:2 * H], ACT.Square,
                                         accum_out=ss[:, t:t + 1]).then_inc(squares_done, 1)
                act.wait_ge(squares_done, g * B + B)
                nc.scalar.activation(nrm[:], ss[:], ACT.Sqrt).then_inc(norm_ready, 1)

            def exps(g):
                act.wait_ge(logits_shifted, g + 1)
                nc.scalar.activation(gex[:], gd[:], ACT.Exp).then_inc(exp_ready, 1)

            def experts(m, t, b):
                n = m * 2 + t
                q = 2 * b + 1
                if b == 0 and not (isinstance(m, int) and m == 0):
                    act.wait_ge(tile_summed, n - 1)
                act.wait_ge(mb_full[q], n + 1)
                for h in range(2):
                    e = 2 * q + h
                    ins = copy(tmp[t][:, b, h], mb[q][:, h], gates[:, bass.ds(n, 1), e:e + 1].squeeze(1))
                ins.then_inc(mb_used[q], 1)

            def keep_uq(g, h):
                act.wait_ge(uq_full, g * 2 + (h + 1))
                uq = tb[:].rearrange("p (t a) m -> p a t m", a=2)
                tiles = bass.ds(g * B + 2 * h, 2)
                copy(GR[:, tiles, P:2 * P], uq[:, 0])
                copy(QT[:, tiles, :], uq[:, 1]).then_inc(uq_kept, 1)

            sqrt_var(0)
            act.wait_ge(we_loaded, 16)
            copy(we_hi[:], we_land).then_inc(we_hi_ready, 1)
            x_high(0, 0)
            x_high(0, 1)
            xm_high(0, 0, False)
            sqrt_var(1)
            norms(0)
            x_high(1, 0)
            x_high(1, 1)
            exps(0)
            keep_uq(0, 0)
            keep_uq(0, 1)
            sqrt_var(2)

            def step(k, par, i):
                g = k + 1
                if within(g, K):
                    if within(k + 2, K):
                        x_high(k + 2, 0)
                    norms(g)
                    exps(g)
                    if within(k + 2, K):
                        x_high(k + 2, 1)
                act.wait_ge(gates_ready, k + 1)
                experts(k, 0, 0)
                xm_high(k + 1, 1 - par, not (isinstance(k, int) and k == 0))
                experts(k, 0, 1)
                if within(k + 3, K):
                    sqrt_var(k + 3)
                if within(g, K):
                    keep_uq(g, 0)
                experts(k, 1, 0)
                if within(g, K):
                    keep_uq(g, 1)
                experts(k, 1, 1)

            steps_beside_stage1(act, step)
            act.wait_ge(uq_kept, 2 * K)
            nc.scalar.sem_inc(stage1_over, 1)
            act.wait_ge(stage1_over, 3)
            act.wait_ge(v_stored, 16 * K)

            def newton(before, nit, low, scales):
                for it in range(nit):
                    x = Xr if it < low - 1 else X
                    scale = scales[it + 1] * (0.5 / X16 if it == low - 1 else 1.0)
                    for s in range(NS):
                        act.wait_ge(x_full[s], before + (it + 1))
                        copy(x[s][:], pX[s][:], scale).then_inc(x_ready[s], 1)

            for s in range(NS):
                nc.scalar.sem_inc(ua_kept[s], 1)
            with act.Fori(0, NR) as i:
                newton(i * NIT, NIT, LOW, scales)
                for s in range(NS):
                    act.wait_ge(au_full[s], i + 2)
                    copy(Vn[s][:], pT[s][:]).then_inc(au_ready[s], 1)
                for s in range(NS):
                    act.wait_ge(g_full[s], i + 1)
                    copy(GR[:, grp(i * NS + s), P:2 * P], pX[s][:]).then_inc(ua_kept[s], 1)

            for r in range(NR64):
                newton(STEPS1 + r * NIT64, NIT64, LOW64, scales64)
                for s in range(NS):
                    act.wait_ge(x_ready[s], STEPS1 + (r + 1) * NIT64)
                    copy(Xodd[s][:], X[s][HALF:P, :, HALF:P]).then_inc(xodd_ready, 1)
                for s in range(NS):
                    act.wait_ge(f_full, r * NS + s + 1)
                    copy(Fst[s], pF[s][0:HALF]).then_inc(f_ready, 1)

            for j in range(NJ):
                for m in range(M1 + j * MJ, M1 + j * MJ + MJ):
                    if m + 1 < 2 * K:
                        xm_high(m + 1, (m + 1) % 2, True)
                    experts(m, 0, 0)
                    experts(m, 0, 1)
                    experts(m, 1, 0)
                    experts(m, 1, 1)
                last = j == NJ - 1
                if last:
                    act.wait_ge(mb_full[NB - 1], 4 * K)
                    for par in range(2):
                        copy(YT4[par][:], ident[:].unsqueeze(1).broadcast_to([P, B, P])).then_inc(yt4_set, 1)
                yts = YTs4 if last else YTs
                act.wait_ge(y_full, 3 * j + 1)
                for h in range(2):
                    rows = slice(HALF * h + BLK * j, HALF * h + BLK * (j + 1))
                    ins = copy(yts[rows, :, 0:BLK // 2].rearrange("c p i -> c i p"),
                               pYb[0:BLK, :, h * HALF:(h + 1) * HALF])
                ins.then_inc(y_kept, 1)

                if last:
                    break

                def keep_panel(g):
                    act.wait_ge(panel_full, g + (j * K + 1))
                    copy(GR[:, grp(g), BLK * (j + 1):2 * P], pP[:, :, BLK * (j + 1):2 * P]).then_inc(panel_kept, 1)

                with act.Fori(0, K) as g:
                    keep_panel(g)

            act.wait_ge(y_full, 3 * NJ)
            act.wait_ge(y_rd_kept, 2 * NJ)
            for par in range(2):
                act.wait_ge(part_stored[par], 16 * K)

            def keep_w(k, par, done):
                act.wait_ge(w_full, k + 1)
                if done is not None:
                    act.wait_ge(m_full, done)
                copy(Wst[par][:], pW[:]).then_inc(w_staged, 1)

            def keep_wt(k):
                act.wait_ge(wt_full, k + 1)
                copy(WT[:], pWT[:]).then_inc(wt_ready, 1)

            def keep_ot(k):
                act.wait_ge(ot_full, k + 1)
                copy(OT[:], pOT[:]).then_inc(ot_ready, 1)

            def keep_m(k):
                act.wait_ge(m_full, k + 1)
                copy(MT[:], pM[:]).then_inc(m_kept, 1)

            def keep_gt(k):
                act.wait_ge(gt_full, k + 1)
                if not (isinstance(k, int) and k == 0):
                    act.wait_ge(out_full, k)
                copy(gT[:], pG[:, 0:P]).then_inc(gt_ready, 1)

            keep_w(0, 0, None)
            keep_w(1, 1, None)
            keep_wt(0)
            keep_gt(0)

            def step(k, par):
                keep_wt(k + 1)
                keep_ot(k)
                keep_m(k)
                if within(k + 2, K):
                    keep_w(k + 2, par, k + 1)
                keep_gt(k + 1)

            step(0, 0)
            step(1, 1)
            with act.Fori(1, K // 2 - 1) as i:
                for par in range(2):
                    step(i * 2 + par, par)
            step(K - 2, 0)
            keep_ot(K - 1)

        @block.vector
        def _(dve):
            st = Steps(dve, dve_step)
            v = nc.vector
            v.memset(psS[:], 0.0).then_inc(prefix_kept, 1)

            def split_low(lo, whole, hi):
                return v.tensor_tensor(lo, whole, hi.bitcast(F32), ALU.subtract)

            def stats_a(g, par, i):
                dve.wait_ge(x_loaded[par], i * 16 + 16)
                for t in range(B):
                    ins = v.bn_stats(bnst[:, t], xbuf[par][:, t])
                st.done(ins)
                st.wait()
                v.tensor_tensor(mdiff[:], bnst[:, :, 1], bnst[:, :, 4], ALU.subtract)
                st.done(v.tensor_tensor(msum[:], bnst[:, :, 1:3], bnst[:, :, 4:6], ALU.add))
                st.wait()
                v.tensor_scalar(mean[:, grp(g)], msum[:, :, 0], 0.5, None, ALU.mult)
                st.done(v.scalar_tensor_tensor(mdiff[:], mdiff[:], 0.25, mdiff[:], ALU.mult, ALU.mult))
                st.wait()
                st.done(v.scalar_tensor_tensor(veps[:], msum[:, :, 1], 1.0 / D, mdiff[:], ALU.mult, ALU.add))
                st.wait()
                v.tensor_scalar(veps[:], veps[:], LN_EPS, None, ALU.add).then_inc(var_ready, 1)

            def normalise(xt, n):
                one = bass.ds(n, 1)
                return v.tensor_scalar(xt, xt, mean[:, one], rstd[:, one], ALU.subtract, ALU.mult)

            def stats_b(g, par):
                dve.wait_ge(std_ready, g + 1)
                st.done(v.reciprocal(rstd[:, grp(g)], std[:]))
                st.wait()
                for t in range(B):
                    ins = normalise(xbuf[par][:, t], g * B + t)
                ins.then_inc(xn_ready, 1)

            def norm_pair(m, par, i):
                dve.wait_ge(xm_loaded[par], i * 16 + 16)
                for t in range(2):
                    ins = normalise(xm[par][:, t], m * 2 + t)
                ins.then_inc(xm_ready, 1)

            def xm_low(m, par, used):
                dve.wait_ge(xm_hi, m + 1)
                if used:
                    dve.wait_ge(mb_full[NB - 1], m * 2 - 2)
                split_low(xl[par][:], tb[:].rearrange("p (t c) m -> p c t m", c=DC), xh[par][:]).then_inc(xm_lo, 1)

            def experts(m, par, t, q, i):
                n = m * 2 + t
                dve.wait_ge(mb_full[q], n + 1)
                if q == 0 and t == 0 and i is not None:
                    dve.wait_ge(part_stored[par], i * 16)
                for h in range(2):
                    e = 2 * q + h
                    gate = gates[:, bass.ds(n, 1), e:e + 1].squeeze(1)
                    if e == 0:
                        ins = v.tensor_scalar(acc[par][:, t], mb[q][:, h], gate, None, ALU.mult)
                    else:
                        ins = v.scalar_tensor_tensor(acc[par][:, t], mb[q][:, h], gate, acc[par][:, t],
                                                     ALU.mult, ALU.add)
                    if h == 0:
                        st.done(ins)
                        st.wait()
                ins.then_inc(mb_used[q], 1)
                if q == 0:
                    dve.wait_ge(mb_used[0], n + 1)

            def bc(a):
                return a.unsqueeze(2).broadcast_to([P, B, E])

            def x_low(g, h):
                dve.wait_ge(xT_hi, g * 2 + (h + 1))
                split_low(ql[:, :, 2 * h:2 * h + 2, :], tb[:].rearrange("p (t c) m -> p c t m", c=DC),
                          qh[:, :, 2 * h:2 * h + 2, :]).then_inc(xT_lo, 1)

            def keep_qkv(g, t):
                if t == 0 and not (isinstance(g, int) and g == 0):
                    dve.wait_ge(uq_full, g * 2)
                    dve.wait_ge(gram_done, g)
                    dve.wait_ge(v_stored, g * 16)
                dve.wait_ge(qb_full[t % 2], g * 2 + (t // 2 + 1))
                v.tensor_tensor(qkv[:, t], qb[t % 2][:, 0:NQ], bias_bc[:], ALU.add).then_inc(qkv_ready, 1)

            def shift_logits(g):
                dve.wait_ge(qkv_ready, g * B + B)
                lg = qkv[:, :, 3 * H:NQ]
                st.done(v.tensor_reduce(gm[:], lg, AX, ALU.max))
                st.wait()
                v.tensor_tensor(gd[:], lg, bc(gm[:]), ALU.subtract).then_inc(logits_shifted, 1)
                for t in range(B):
                    v.scalar_tensor_tensor(kq[:, t], qkv[:, t, 0:H], 1.0, qkv[:, t, H:2 * H], ALU.mult,
                                           ALU.mult, accum_out=sdot[:, bass.ds(g * B + t, 1)])

            def make_u(g):
                dve.wait_ge(norm_ready, g + 1)
                st.done(v.tensor_scalar(nrme[:], nrm[:], NORM_EPS, None, ALU.add))
                st.wait()
                st.done(v.reciprocal(rn[:], nrme[:]))
                st.wait()
                v.tensor_tensor(qkv[:, :, H:2 * H], qkv[:, :, H:2 * H],
                                rn[:].unsqueeze(2).broadcast_to([P, B, H]), ALU.mult).then_inc(u_ready, 1)

            def choose(g):
                revb = rev[:].unsqueeze(1).broadcast_to([P, B, E])
                dve.wait_ge(logits_shifted, g + 1)
                st.done(v.scalar_tensor_tensor(g1[:], gd[:], 0.0, revb, ALU.is_equal, ALU.mult))
                st.wait()
                st.done(v.tensor_reduce(gm[:], g1[:], AX, ALU.max))
                st.wait()
                st.done(v.tensor_tensor(g1[:], g1[:], bc(gm[:]), ALU.is_equal))
                st.wait()
                st.done(v.scalar_tensor_tensor(g2[:], g1[:], -3.0e38, gd[:], ALU.mult, ALU.add))
                st.wait()
                st.done(v.tensor_reduce(gm[:], g2[:], AX, ALU.max))
                st.wait()
                st.done(v.tensor_tensor(g3[:], g2[:], bc(gm[:]), ALU.is_equal))
                st.wait()
                st.done(v.tensor_tensor(g3[:], g3[:], revb, ALU.mult))
                st.wait()
                st.done(v.tensor_reduce(gm[:], g3[:], AX, ALU.max))
                st.wait()
                st.done(v.tensor_tensor(g3[:], g3[:], bc(gm[:]), ALU.is_equal))
                st.wait()
                st.done(v.tensor_tensor(g1[:], g1[:], g3[:], ALU.add))
                st.wait()
                dve.wait_ge(exp_ready, g + 1)
                st.done(v.tensor_tensor(g1[:], g1[:], gex[:], ALU.mult))
                st.wait()
                st.done(v.tensor_reduce(gsum[:], g1[:], AX, ALU.add))
                st.wait()
                st.done(v.reciprocal(gm[:], gsum[:]))
                st.wait()
                v.tensor_tensor(gates[:, grp(g), 0:E], g1[:], bc(gm[:]), ALU.mult).then_inc(gates_ready, 1)

            def keep_prefix(g):
                dve.wait_ge(gram_done, g + 1)
                v.tensor_tensor(GR[:, grp(g + 1), 0:P], psS[:],
                                ident[:].unsqueeze(1).broadcast_to([P, B, P]), ALU.add).then_inc(prefix_kept, 1)

            dve.wait_ge(consts_ready, 2)
            stats_a(0, 0, 0)
            dve.wait_ge(wq_loaded, 32)
            st.done(v.tensor_copy(wq_hi[:], wq_land))
            st.wait()
            split_low(wq_lo[:], wq_land, wq_hi[:]).then_inc(wq_split, 1)
            stats_b(0, 0)
            norm_pair(0, 0, 0)
            stats_a(1, 1, 0)
            x_low(0, 0)
            x_low(0, 1)
            xm_low(0, 0, False)
            stats_b(1, 1)
            norm_pair(1, 1, 0)
            for t in range(B):
                keep_qkv(0, t)
            shift_logits(0)
            make_u(0)
            x_low(1, 0)
            x_low(1, 1)
            dve.wait_ge(we_hi_ready, 1)
            split_low(we_lo[:], we_land, we_hi[:]).then_inc(we_split, 1)
            choose(0)
            stats_a(2, 0, 1)
            stats_b(2, 0)

            def step(k, par, i):
                g = k + 1
                more = within(g, K)
                if more:
                    keep_qkv(g, 0)
                    keep_qkv(g, 1)
                    keep_prefix(k)
                    keep_qkv(g, 2)
                    keep_qkv(g, 3)
                    shift_logits(g)
                    if within(k + 2, K):
                        x_low(k + 2, 0)
                experts(k, par, 0, 0, None if isinstance(k, int) and k < 2 else i)
                if more:
                    make_u(g)
                if within(k + 2, K):
                    x_low(k + 2, 1)
                if within(k + 3, K):
                    stats_a(k + 3, 1 - par, i + 1 + par)
                xm_low(k + 1, 1 - par, not (isinstance(k, int) and k == 0))
                experts(k, par, 0, 2, None)
                experts(k, par, 1, 0, None)
                if within(k + 3, K):
                    stats_b(k + 3, 1 - par)
                if more:
                    choose(g)
                norm_pair(k + 2, par, i + 1)
                experts(k, par, 1, 2, None)

            PER = 2 * (3 + 5 + 13 + 4)
            steps_beside_stage1(dve, step, lambda i: st.loop(i, PER), lambda: st.end(M1 // 2 - 3, PER))
            dve.wait_ge(u_ready, K)
            v.sem_inc(stage1_over, 1)
            dve.wait_ge(stage1_over, 3)
            dve.wait_ge(v_stored, 16 * K)
            dve.wait_ge(consts_ready, CONSTS - 3)

            def bc_b(a):
                return a[:].unsqueeze(1).broadcast_to([P, B, P])

            def make_v(before, nit, low):
                for it in range(nit):
                    for s in range(NS):
                        dve.wait_ge(t_full[s], before + (it + 2))
                        o = (Vr if it < low else Vn)[s][:]
                        v.scalar_tensor_tensor(o, pT[s][:], -1.0 / X16 if it < low else -1.0, bc_b(twoI), ALU.mult, ALU.add)\
                            .then_inc(v_ready[s], 1)

            for s in range(NS):
                v.sem_inc(g_kept[s], 1)

            with dve.Fori(0, NR) as i:
                for s in range(NS):
                    dve.wait_ge(au_full[s], i + 1)
                    v.scalar_tensor_tensor(Xr[s][:], GR[:, grp(i * NS + s), 0:P], -X16 * scales[0] * start * start,
                                           bc_b(firstI), ALU.mult, ALU.add).then_inc(x_init[s], 1)
                make_v(i * NIT, NIT, LOW)
                for s in range(NS):
                    dve.wait_ge(g_full[s], i + 1)
                    v.tensor_tensor(GR[:, grp(i * NS + s), 0:P], pT[s][:], bc_b(ident), ALU.add)\
                        .then_inc(g_kept[s], 1)

            def stage_s64(s, r):
                q = r * NS + s
                for to in (Sst[s], Sr[s]):
                    for h in range(2):
                        rows = slice(HALF * h, HALF * (h + 1))
                        ins = v.tensor_copy(to[rows, :, rows], GR[0:HALF, grp(2 * q + h), 0:HALF])
                ins.then_inc(s64_staged, 1)

            for s in range(NS):
                st.done(v.memset(Sst[s][:], 0.0))
                st.done(v.memset(Sr[s][:], 0.0))
            st.wait()
            for s in range(NS):
                stage_s64(s, 0)
            for r in range(NR64):
                for s in range(NS):
                    dve.wait_ge(s64_staged, r * NS + s + 1)
                    v.scalar_tensor_tensor(Xr[s][:], Sst[s][:], -X16 * scales64[0] * start64 * start64,
                                           bc_b(firstI64), ALU.mult, ALU.add).then_inc(x_init[s], 1)
                make_v(STEPS1 + r * NIT64, NIT64, LOW64)
                if r + 1 < NR64:
                    for s in range(NS):
                        stage_s64(s, r + 1)
                for g in range(2 * r * NS, 2 * (r + 1) * NS):
                    dve.wait_ge(half_full, g + 1)
                    v.tensor_tensor(GR[HALF:P, grp(g), HALF:2 * P], GR[HALF:P, grp(g), HALF:2 * P],
                                    pV[g % 2][HALF:P, :, HALF:2 * P], ALU.subtract).then_inc(half_done, 1)

            dve.wait_ge(consts3, 1)
            for j in range(NJ):
                dve.wait_ge(blocks_gathered, j + 1)
                if j:
                    dve.wait_ge(y_full, 3 * j)
                v.tensor_copy(work[:], pWork).then_inc(blocks_copied, 1)
                dve.wait_ge(blocks_copied, j + 1)

                def beside(c):
                    m = M1 + j * MJ + c // SLOT
                    at = c % SLOT
                    experts(m, m % 2, at // 2, 2 * (at % 2), m // 2)
                    if at == 1 and m + 1 < 2 * K:
                        xm_low(m + 1, (m + 1) % 2, True)
                    if at == 3 and m + 2 < 2 * K:
                        norm_pair(m + 2, m % 2, m // 2 + 1)

                for c in range(BLK):
                    r = BLK - 1 - c
                    st.done(v.reciprocal(RD[:, c:c + 1], work[:, c, c:c + 1]))
                    if r == 0:
                        beside(c)
                        break
                    st.wait()
                    st.done(v.tensor_scalar(work[:, c, c:c + 1], work[:, c, c:c + 1], 1.0, None, ALU.add))
                    st.wait()
                    st.done(v.tensor_tensor(prod[:, 0:r], work[:, c:c + 1, :].broadcast_to([P, r, BLK]),
                                            work[:, c + 1:BLK, c:c + 1].broadcast_to([P, r, BLK]), ALU.mult))
                    beside(c)
                    st.wait()
                    st.done(v.scalar_tensor_tensor(work[:, c + 1:BLK], prod[:, 0:r], RD[:, c:c + 1],
                                                   work[:, c + 1:BLK], ALU.mult, ALU.subtract, reverse1=True))
                    st.wait()
                st.done(v.tensor_tensor(work[:], work[:], below[:], ALU.mult))
                st.wait()
                v.memset(work[:].rearrange("p a b -> p (a b)")[:, 0:BLK * BLK:BLK + 1], 1.0)\
                    .then_inc(blocks_factored, 1)
                yts = YTs4 if j == NJ - 1 else YTs
                dve.wait_ge(y_full, 3 * j + 2)
                for h in range(2):
                    rows = slice(HALF * h + BLK * j, HALF * h + BLK * (j + 1))
                    ins = v.tensor_copy(yts[rows, :, BLK // 2:BLK].rearrange("c p i -> c i p"),
                                        pYa[0:BLK, :, h * HALF:(h + 1) * HALF])
                ins.then_inc(y_rd_kept, 1)
                dve.wait_ge(y_full, 3 * j + 3)
                for h in range(2):
                    rows = slice(HALF * h + BLK * j, HALF * h + BLK * (j + 1))
                    ins = v.tensor_copy(RDall[rows], pYb[0:BLK, 0, h * HALF:(h + 1) * HALF])
                ins.then_inc(y_rd_kept, 1)
                if j < NJ - 1:
                    with dve.Fori(0, K) as g:
                        dve.wait_ge(update_full, g + (j * K + 1))
                        v.tensor_tensor(GR[:, grp(g), BLK:2 * P], GR[:, grp(g), BLK:2 * P],
                                        pU[:, :, BLK:2 * P], ALU.subtract).then_inc(update_done, 1)

            dve.wait_ge(y_kept, NJ)
            dve.wait_ge(y_rd_kept, 2 * NJ)
            for par in range(2):
                dve.wait_ge(part_stored[par], 16 * K)
            v.memset(pM[:], 0.0).then_inc(m_zeroed, 1)
            v.memset(MT[:], 0.0).then_inc(m_zeroed, 1)
            st.done(v.tensor_tensor(SD[:], sdot[:], RDall[:], ALU.mult))
            st.wait()
            upperb = upper[:].unsqueeze(1).broadcast_to([P, B, P])

            def split_gates():
                st.done(v.tensor_copy(g_hi[:], gates[:]))
                st.wait()
                v.tensor_tensor(g_parts[:, :, 1], gates[:], g_hi[:], ALU.subtract)
                v.tensor_copy(g_parts[:, :, 0], g_hi[:]).then_inc(gates_split, 1)
                v.tensor_copy(g_parts[:, :, 2], g_hi[:]).then_inc(gates_split, 1)

            def split_be():
                dve.wait_ge(consts_ready, CONSTS)
                dve.wait_ge(out_weights_loaded, 16 * (3 * B + 1))
                st.done(v.tensor_copy(be_hi[:], be_land[:]))
                st.wait()
                st.done(v.tensor_tensor(be_lo[:], be_land[:], be_hi[:], ALU.subtract))
                st.wait()
                for b in range(B):
                    st.done(v.tensor_scalar(be_land[:], be_lo[:], mask_lo[0:GROWS, b:b + 1], None, ALU.mult))
                    st.wait()
                    v.scalar_tensor_tensor(bebo4[:, b], be_hi[:], mask_hi[0:GROWS, b:b + 1], be_land[:],
                                           ALU.mult, ALU.add).then_inc(be_ready, 1)
                    dve.wait_ge(be_ready, b + 1)

            def scale_v(k, par, i, done):
                dve.wait_ge(v_loaded[par], i * 16 + 16)
                if done is not None:
                    dve.wait_ge(m_full, done)
                v.tensor_tensor(Vs[:], vin[par][:], SD[:, grp(k)].unsqueeze(2).broadcast_to([P, B, H]),
                                ALU.mult).then_inc(vs_ready, 1)

            def mask_pt(k):
                dve.wait_ge(pt_full, k + 1)
                v.tensor_tensor(PTm[:], pPT[:], upperb, ALU.mult).then_inc(pt_masked, 1)

            def finish(k, par, i):
                dve.wait_ge(out_full, k + 1)
                dve.wait_ge(in_summed, k + 1)
                if i is not None:
                    dve.wait_ge(out_stored[par], i * 16)
                v.tensor_tensor(obuf[par][:], pOut[:], pin[par][:], ALU.add).then_inc(out_ready, 1)

            scale_v(0, 0, 0, None)
            split_gates()
            split_be()
            mask_pt(0)
            for k in (0, 1):
                scale_v(k + 1, 1 - k, k, k + 1)
                mask_pt(k + 1)
                finish(k, k, None)
            with dve.Fori(1, K // 2 - 1) as i:
                for par in range(2):
                    k = i * 2 + par
                    scale_v(k + 1, 1 - par, i + par, k + 1)
                    mask_pt(k + 1)
                    finish(k, par, i)
            scale_v(K - 1, 1, K // 2 - 1, K - 1)
            mask_pt(K - 1)
            finish(K - 2, 0, K // 2 - 1)
            finish(K - 1, 1, K // 2 - 1)

        @block.tensor
        def _(pe):
            mm = nc.tensor.matmul
            tr = nc.tensor.transpose

            def three(o, hi_t, lo_t, w_hi, w_lo):
                for c in range(DC):
                    mm(o, hi_t(c), w_hi(c), start=(c == 0), stop=False)
                    mm(o, hi_t(c), w_lo(c), start=False, stop=False)
                for c in range(DC):
                    ins = mm(o, lo_t(c), w_hi(c), start=False, stop=(c == DC - 1))
                return ins

            def pair_transpose(m, par):
                pe.wait_ge(xm_ready, m + 1)
                for t in range(2):
                    for c in range(DC):
                        ins = tr(tb[:, 2 * t + c], xm[par][:, t, c * P:(c + 1) * P], ident[:])
                ins.then_inc(xmT_full, 1)

            def experts(m, par, t, q):
                if t == 0 and q == 0:
                    pe.wait_ge(xm_lo, m + 1)
                if t or not (isinstance(m, int) and m == 0):
                    pe.wait_ge(mb_used[q], m * 2 + t)
                three(mb[q][:].rearrange("p h n -> p (h n)"),
                      lambda c: xh[par][:, c, t], lambda c: xl[par][:, c, t],
                      lambda c: we_hi[:, c, q * 512:(q + 1) * 512],
                      lambda c: we_lo[:, c, q * 512:(q + 1) * 512]).then_inc(mb_full[q], 1)

            def x_transpose(g, par, h):
                if h == 0:
                    pe.wait_ge(xn_ready, g + 1)
                for t in range(2):
                    for c in range(DC):
                        ins = tr(tb[:, 2 * t + c], xbuf[par][:, 2 * h + t, c * P:(c + 1) * P], ident[:])
                ins.then_inc(xT_full, 1)

            def project_qkv(g):
                pe.wait_ge(xT_lo, g * 2 + 2)
                for t in range(B):
                    if t >= 2 or not (isinstance(g, int) and g == 0):
                        pe.wait_ge(qkv_ready, g * B + (t - 1))
                    three(qb[t % 2][:, 0:NQ], lambda c: qh[:, c, t], lambda c: ql[:, c, t],
                          lambda c: wq_hi[:, c], lambda c: wq_lo[:, c]).then_inc(qb_full[t % 2], 1)

            def uq_transpose(g, h):
                if h == 0:
                    pe.wait_ge(u_ready, g + 1)
                else:
                    pe.wait_ge(uq_kept, g * 2 + 1)
                for t in range(2):
                    tr(tb[:, 2 * t], qkv[:, 2 * h + t, H:2 * H], ident[:])
                    ins = tr(tb[:, 2 * t + 1], qkv[:, 2 * h + t, 0:H], ident[:])
                ins.then_inc(uq_full, 1)

            def gram(g):
                pe.wait_ge(prefix_kept, g + 1)
                for b in range(B):
                    u = qkv[:, b, H:2 * H]
                    ins = mm(psS[:, b], u, u, start=False, stop=True, skip_group_check=True)
                ins.then_inc(gram_done, 1)

            pe.wait_ge(consts_ready, 2)
            x_transpose(0, 0, 0)
            pe.wait_ge(xT_lo, 1)
            x_transpose(0, 0, 1)
            pe.wait_ge(xT_lo, 2)
            pair_transpose(0, 0)
            pe.wait_ge(wq_split, 1)
            project_qkv(0)
            pe.wait_ge(xm_lo, 1)
            x_transpose(1, 1, 0)
            pe.wait_ge(xT_lo, 3)
            x_transpose(1, 1, 1)
            pe.wait_ge(xT_lo, 4)
            uq_transpose(0, 0)
            gram(0)
            uq_transpose(0, 1)
            pe.wait_ge(we_split, 1)

            def step(k, par, i):
                g = k + 1
                more = within(g, K)
                if more:
                    project_qkv(g)
                if within(k + 2, K):
                    pe.wait_ge(uq_kept, k * 2 + 2)
                    x_transpose(k + 2, par, 0)
                experts(k, par, 0, 0)
                experts(k, par, 0, 1)
                if within(k + 2, K):
                    pe.wait_ge(xT_lo, k * 2 + 5)
                    x_transpose(k + 2, par, 1)
                experts(k, par, 0, 2)
                experts(k, par, 0, 3)
                if within(k + 2, K):
                    pe.wait_ge(xT_lo, k * 2 + 6)
                elif not more:
                    pe.wait_ge(uq_kept, 2 * K)
                else:
                    pe.wait_ge(uq_kept, k * 2 + 2)
                pair_transpose(k + 1, 1 - par)
                experts(k, par, 1, 0)
                if more:
                    pe.wait_ge(xm_lo, k + 2)
                    uq_transpose(g, 0)
                experts(k, par, 1, 1)
                if within(g, K - 1):
                    gram(g)
                experts(k, par, 1, 2)
                if more:
                    uq_transpose(g, 1)
                experts(k, par, 1, 3)

            steps_beside_stage1(pe, step)
            pe.wait_ge(mb_full[NB - 1], 2 * K)
            nc.tensor.sem_inc(stage1_over, 1)
            pe.wait_ge(stage1_over, 3)
            pe.wait_ge(xm_lo, K + 1)
            for q in range(NB):
                pe.wait_ge(mb_used[q], 2 * K)

            def au(s, k, lhs):
                for b in range(B):
                    ins = mm(pT[s][:, b], lhs(b), GR[:, bass.ds(k * B + b, 1), P:2 * P].squeeze(1), start=True, stop=True)
                ins.then_inc(au_full[s], 1)

            def gmat(s, k, done):
                pe.wait_ge(au_ready[s], done)
                for b in range(B):
                    tr(pX[s][:, b], Vn[s][:, b], ident[:])
                for b in range(B):
                    ins = mm(pT[s][:, b], Vn[s][:, b], GR[:, bass.ds(k * B + b, 1), P:2 * P].squeeze(1), start=True, stop=True)
                ins.then_inc(g_full[s], 1)

            def newton(before, nit, low, ready_to_start, ready_for_float32):
                for it in range(nit):
                    for s in range(NS):
                        if it == 0:
                            ready_to_start(s)
                        if it == low:
                            ready_for_float32(s)
                        if it > 0:
                            pe.wait_ge(x_ready[s], before + it)
                        lhs, x = (Sr[s], Xr[s]) if it < low else (Sst[s], X[s])
                        for b in range(B):
                            ins = mm(pT[s][:, b], lhs[:, b], x[:, b], start=True, stop=True)
                        ins.then_inc(t_full[s], 1)
                    for s in range(NS):
                        pe.wait_ge(v_ready[s], before + (it + 1))
                        x, vn = (Xr[s], Vr[s]) if it < low else (X[s], Vn[s])
                        both = it == low - 1
                        for b in range(B):
                            ins = mm(pX[s][:, b], x[:, b], vn[:, b], start=True, stop=not both)
                            if both:
                                ins = mm(pX[s][:, b], vn[:, b], x[:, b], start=False, stop=True)
                        ins.then_inc(x_full[s], 1)

            for s in range(NS):
                nc.tensor.sem_inc(t_full[s], 1)
                nc.tensor.sem_inc(au_full[s], 1)
            with pe.Fori(0, NR) as i:
                def ready_to_start(s):
                    pe.wait_ge(s16_staged[s], i + 1)
                    pe.wait_ge(x_init[s], i + 1)
                    pe.wait_ge(g_kept[s], i + 1)
                    pe.wait_ge(ua_kept[s], i + 1)

                newton(i * NIT, NIT, LOW, ready_to_start, lambda s: pe.wait_ge(s_staged[s], i + 1))
                for s in range(NS):
                    pe.wait_ge(x_ready[s], i * NIT + NIT)
                    au(s, i * NS + s, lambda b, s=s: X[s][:, b])
                for s in range(NS):
                    gmat(s, i * NS + s, i + 1)

            def prob(g, b, rows, cols):
                return GR[rows, bass.ds(g * B + b, 1), cols].squeeze(1)

            top = slice(0, HALF)
            for s in range(NS):
                pe.wait_ge(g_kept[s], NR + 1)
                pe.wait_ge(ua_kept[s], NR + 1)
            for r in range(NR64):
                def ready_to_start(s):
                    pe.wait_ge(s64_staged, r * NS + s + 1)
                    pe.wait_ge(x_init[s], NR + r + 1)
                    if r and s == 0:
                        pe.wait_ge(half_done, 2 * NS * r)

                newton(STEPS1 + r * NIT64, NIT64, LOW64, ready_to_start, lambda s: None)
                for s in range(NS):
                    pe.wait_ge(xodd_ready, r * NS + s + 1)
                    for h in range(2):
                        for b in range(B):
                            inv = Xodd[s][:, b] if h else X[s][0:HALF, b, 0:HALF]
                            ins = mm(pF[s][0:HALF, h, b], inv, prob(2 * (r * NS + s) + h, b, top, slice(HALF, P)),
                                     start=True, stop=True)
                    ins.then_inc(f_full, 1)
                for g in range(2 * r * NS, 2 * (r + 1) * NS):
                    s, h = g // 2 % NS, g % 2
                    pe.wait_ge(f_ready, g // 2 + 1)
                    if g >= 2:
                        pe.wait_ge(half_done, g - 1)
                    for b in range(B):
                        ins = mm(pV[g % 2][HALF:P, b, HALF:2 * P], Fst[s][:, h, b],
                                 prob(g, b, top, slice(HALF, 2 * P)), start=True, stop=True)
                    ins.then_inc(half_full, 1)

            pe.wait_ge(half_done, K)
            for j in range(NJ):
                if j:
                    pe.wait_ge(update_done, j * K)
                    pe.wait_ge(panel_kept, j * K)
                for c in range(BLK):
                    for h in range(2):
                        at = HALF * h + BLK * j
                        ins = mm(pWork[HALF * h:HALF * (h + 1), c], GR[:, :, at + c], ident[:, at:at + BLK],
                                 start=True, stop=True)
                ins.then_inc(blocks_gathered, 1)
                pe.wait_ge(blocks_copied, j + 1)
                if j:
                    pe.wait_ge(y_rd_kept, 2 * j)
                for m in range(M1 + j * MJ, M1 + j * MJ + MJ):
                    if m + 1 < 2 * K:
                        pair_transpose(m + 1, (m + 1) % 2)
                    for t in range(2):
                        for q in range(NB):
                            experts(m, m % 2, t, q)
                pe.wait_ge(blocks_factored, j + 1)
                for q in range(NB):
                    pe.wait_ge(mb_used[q], 2 * (m + 1))
                for i in range(BLK // 2):
                    ins = tr(pYb[0:BLK, i], work[:, i], ident[:])
                ins.then_inc(y_full, 1)
                if m + 1 < 2 * K:
                    pe.wait_ge(xm_lo, m + 2)
                for i in range(BLK // 2):
                    ins = tr(pYa[0:BLK, i], work[:, BLK // 2 + i], ident[:])
                ins.then_inc(y_full, 1)
                pe.wait_ge(y_kept, j + 1)
                tr(pYb[0:BLK, 0], RD[:], ident[:]).then_inc(y_full, 1)

                if j == NJ - 1:
                    break
                c0 = BLK * (j + 1)

                def panel(g, par, seen):
                    pe.wait_ge(yt_ready, g * 2 + (2 * j * K + 2))
                    if seen:
                        pe.wait_ge(panel_kept, g + j * K)
                    for b in range(B):
                        ins = mm(pP[:, b, c0:2 * P], YT[par][:, b], prob(g, b, slice(0, P), slice(c0, 2 * P)),
                                 start=True, stop=True)
                    ins.then_inc(panel_full, 1)

                def trail(g, par, seen):
                    pe.wait_ge(lt_ready, g * 2 + (2 * j * K + 2))
                    if seen:
                        pe.wait_ge(update_done, g + j * K)
                    for b in range(B):
                        ins = mm(pU[:, b, c0:2 * P], LT[par][:, b], prob(g, b, slice(0, P), slice(c0, 2 * P)),
                                 start=True, stop=True)
                    ins.then_inc(update_full, 1)

                panel(0, 0, False)
                panel(1, 1, True)
                trail(0, 0, False)
                panel(2, 0, True)
                trail(1, 1, True)
                with pe.Fori(1, K // 2 - 1) as i:
                    for par in range(2):
                        g = i * 2 + par
                        panel(g + 1, 1 - par, True)
                        trail(g, par, True)
                panel(K - 1, 1, True)
                trail(K - 2, 0, True)
                trail(K - 1, 1, True)

            def q_of(k, b):
                return QT[:, bass.ds(k * B + b, 1), :].squeeze(1)

            def w_transpose(k, par):
                pe.wait_ge(w_staged, k + 1)
                for b in range(B):
                    ins = tr(pWT[:, b], Wst[par][:, b], ident[:])
                ins.then_inc(wt_full, 1)

            def pt(k):
                pe.wait_ge(wt_ready, k + 1)
                for b in range(B):
                    ins = mm(pPT[:, b], WT[:, b], q_of(k, b), start=True, stop=True)
                ins.then_inc(pt_full, 1)

            def ot(k, seen):
                pe.wait_ge(vs_ready, k + 1)
                pe.wait_ge(pt_masked, k + 1)
                if seen:
                    pe.wait_ge(m_kept, k)
                    pe.wait_ge(ot_ready, k)
                for b in range(B):
                    mm(pOT[:, b], MT[:, b], q_of(k, b), start=True, stop=False)
                    ins = mm(pOT[:, b], Vs[:, b], PTm[:, b], start=False, stop=True)
                ins.then_inc(ot_full, 1)

            def m_update(k, par):
                for b in range(B):
                    ins = mm(pM[:, b], Wst[par][:, b], Vs[:, b], start=False, stop=True, skip_group_check=True)
                ins.then_inc(m_full, 1)

            def gates_transpose(k):
                pe.wait_ge(gates_staged, k + 1)
                if not (isinstance(k, int) and k == 0):
                    pe.wait_ge(gt_ready, k)
                tr(pG[:, 0:P], gst[:], ident[:]).then_inc(gt_full, 1)

            def project(k, seen):
                pe.wait_ge(gt_ready, k + 1)
                pe.wait_ge(ot_ready, k + 1)
                if seen:
                    pe.wait_ge(out_ready, k)
                else:
                    pe.wait_ge(be_ready, B)
                for b in range(B):
                    mm(pOut[:, b], OT[:, b], wo_sb[:], start=True, stop=False)
                    ins = mm(pOut[:, b], gT[0:GROWS], bebo4[:, b], start=False, stop=True)
                ins.then_inc(out_full, 1)

            pe.wait_ge(y_kept, NJ)
            pe.wait_ge(y_rd_kept, 2 * NJ)

            def last_panel(k, par, seen):
                pe.wait_ge(yt_ready, k * 2 + (2 * (NJ - 1) * K + 2))
                if seen:
                    pe.wait_ge(w_staged, k)
                for b in range(B):
                    ins = mm(pW[:, b], YT4[par][:, b], prob(k, b, slice(0, P), slice(P, 2 * P)), start=True, stop=True)
                ins.then_inc(w_full, 1)

            last_panel(0, 0, False)
            last_panel(1, 1, True)
            w_transpose(0, 0)
            gates_transpose(0)
            pt(0)
            pe.wait_ge(m_zeroed, 2)
            pe.wait_ge(out_weights_loaded, 16 * (3 * B + 1))

            def step(k, par, seen):
                w_transpose(k + 1, 1 - par)
                ot(k, seen)
                m_update(k, par)
                if within(k + 2, K):
                    last_panel(k + 2, par, True)
                pt(k + 1)
                project(k, seen)
                gates_transpose(k + 1)

            step(0, 0, False)
            step(1, 1, True)
            with pe.Fori(1, K // 2 - 1) as i:
                for par in range(2):
                    step(i * 2 + par, par, True)
            step(K - 2, 0, True)
            ot(K - 1, True)
            project(K - 1, True)


_OUT = ((4, 2048, 256), "float32")


def kernel(**inputs):
    import numpy as np
    import concourse.bacc as bacc
    from concourse.bass_utils import run_bass_kernel_spmd

    a = {name: np.asarray(value) for name, value in inputs.items()}
    E, O, D = a["L0_ffn_We"].shape
    arrays = {
        "x": a["L0_attn_x"],
        "wqkvg": np.concatenate([a["L0_attn_Wq"].T, a["L0_attn_Wk"].T, a["L0_attn_Wv"].T, a["L0_ffn_Wg"]], axis=1),
        "bias_row": np.concatenate([a["L0_attn_bq"], a["L0_attn_bk"], a["L0_attn_bv"], a["L0_ffn_bg"]]),
        "we": a["L0_ffn_We"].transpose(2, 0, 1).reshape(D, E * O),
        "be_bo": np.concatenate([a["L0_ffn_be"], a["L0_attn_bo"][None]], axis=0),
        "wo": a["L0_attn_Wo"].T,
    }
    nc = bacc.Bacc("TRN2", target_bir_lowering=False, num_devices=1)
    ins, args = {}, []
    for name, value in arrays.items():
        value = np.ascontiguousarray(value)
        ins[f"in_{name}"] = value
        args.append(nc.dram_tensor(f"in_{name}", value.shape, mybir.dt.from_np(value.dtype), kind="ExternalInput").ap())
    shape, dtype = _OUT
    args.append(nc.dram_tensor("out_0", shape, mybir.dt.from_np(np.dtype(dtype)), kind="ExternalOutput").ap())
    build(nc, *args)
    r = run_bass_kernel_spmd(nc, [ins], core_ids=[0])
    return r.results[0]["out_0"]
```

```python
from contextlib import ExitStack

import concourse.bass as bass
from concourse import mybir

F32 = mybir.dt.float32
F32R = mybir.dt.float32r
BF16 = mybir.dt.bfloat16
F16 = mybir.dt.float16
ALU = mybir.AluOpType
ACT = mybir.ActivationFunctionType
AX = mybir.AxisListType.X

P = 128
LN_EPS = 1e-5
NORM_EPS = 1e-6
BLK = 32


def newton_scales(largest):
    r = (largest - 1.0) / (largest + 1.0)
    start = 2.0 / (1.0 + largest)
    scales = []
    while r * r > 1e-7:
        scales.append(2.0 / (2.0 - r * r))
        r = r * r / (2.0 - r * r)
    return start, scales + [1.0]


class Steps:

    def __init__(self, eng, sem):
        self.eng, self.sem, self.base, self.n = eng, sem, 0, 0

    def done(self, ins):
        ins.then_inc(self.sem, 1)
        self.n += 1

    def wait(self, but=0):
        self.eng.wait_ge(self.sem, self.base + (self.n - but))

    def loop(self, i, per):
        self.start = self.base + self.n
        self.base, self.n = self.start + i * per, 0

    def end(self, rounds, per):
        assert self.n == per, (self.n, per)
        self.base, self.n = self.start + rounds * per, 0


def build(nc, x, wqkvg, bias_row, we, be_bo, wo, out):
    B, T, D = x.shape
    H = wo.shape[0]
    E = be_bo.shape[0] - 1
    DC = D // P
    K = T // P
    NP = B * K
    NQ = 3 * H + E
    NB = E * D // 512
    HALF = P // 2
    NJ = HALF // BLK

    x_v = x.rearrange("b (k p) d -> k p b d", p=P)
    out_v = out.rearrange("b (k p) d -> k p b d", p=P)
    part_dram = nc.dram_tensor("part_dram", [K, P, B, D], F32, kind="Internal").ap()
    v_dram = nc.dram_tensor("v_dram", [K, P, B, H], F32, kind="Internal").ap()
    M1 = K
    MJ = (2 * K - M1) // NJ
    SLOT = BLK // MJ
    assert (2 * K - M1) % NJ == 0 and M1 % 2 == 0 and MJ % 2 == 0 and SLOT == 4

    start, scales = newton_scales(1.0 + P * (K - 1))
    NIT = len(scales) - 1
    start64, scales64 = newton_scales(1.0 + HALF)
    NIT64 = len(scales64) - 1
    LOW, LOW64 = NIT - 2, NIT64 - 1
    GROWS = B * 3 * (E + 1)
    X16 = 64.0
    NS = 4
    NR, NR64 = K // NS, K // NS // 2
    STEPS1 = NR * NIT

    assert B == 4 and D == 2 * H and H == P and NB == 4 and K % (2 * NS) == 0 and LOW > 0 and LOW64 > 0

    with ExitStack() as ctx:
        def sem(name):
            return ctx.enter_context(nc.semaphore(name))

        def sb_in(stack):
            return lambda name, shape, dt=F32: stack.enter_context(nc.sbuf_tensor(name, shape, dt))

        def ps_in(stack):
            return lambda name, shape: stack.enter_context(nc.psum_tensor(name, shape, F32))

        sb = sb_in(ctx)
        GR = sb("GR", [P, NP, 2 * P])
        QT = sb("QT", [P, NP, P])
        sdot = sb("sdot", [P, NP])
        RDall = sb("RDall", [P, NP])
        ident = sb("ident", [P, P])
        mean = sb("mean", [P, NP])
        rstd = sb("rstd", [P, NP])
        gates = sb("gates", [P, NP, E + 1])

        with ExitStack() as sm:
            sb = sb_in(sm)
            we_hi = sb("we_hi", [P, DC, E * D], F32R)
            we_lo = sb("we_lo", [P, DC, E * D], F32R)
            xm = [sb(f"xm{i}", [P, 2, D]) for i in range(2)]
            xh = [sb(f"xh{i}", [P, DC, 2, P], F32R) for i in range(2)]
            xl = [sb(f"xl{i}", [P, DC, 2, P], F32R) for i in range(2)]
            acc = [sb(f"acc{i}", [P, 2, D]) for i in range(2)]
            tmp = [sb(f"tmp{i}", [P, 2, 2, D]) for i in range(2)]

            twoI = sb("twoI", [P, P])
            firstI = sb("firstI", [P, P])
            firstI64 = sb("firstI64", [P, P])
            deltaI = sb("deltaI", [P, P])

            with ExitStack() as s1:
                sb = sb_in(s1)
                ps = ps_in(s1)
                wq_hi = sb("wq_hi", [P, DC, NQ], F32R)
                wq_lo = sb("wq_lo", [P, DC, NQ], F32R)
                bias_bc = sb("bias_bc", [P, NQ])
                rev = sb("rev", [P, E])
                xbuf = [sb(f"xbuf{i}", [P, B, D]) for i in range(2)]
                qh = sb("qh", [P, DC, B, P], F32R)
                ql = sb("ql", [P, DC, B, P], F32R)
                qkv = sb("qkv", [P, B, NQ])
                bnst = sb("bnst", [P, B, 6])
                mdiff = sb("mdiff", [P, B])
                msum = sb("msum", [P, B, 2])
                veps = sb("veps", [P, B])
                std = sb("std", [P, B])
                ksq = sb("ksq", [P, B, H], BF16)
                kq = sb("kq", [P, B, H], BF16)
                ss = sb("ss", [P, B])
                nrm = sb("nrm", [P, B])
                nrme = sb("nrme", [P, B])
                rn = sb("rn", [P, B])
                gsum = sb("gsum", [P, B])
                gd = sb("gd", [P, B, E])
                gex = sb("gex", [P, B, E])
                gm = sb("gm", [P, B])
                g1 = sb("g1", [P, B, E])
                g2 = sb("g2", [P, B, E])
                g3 = sb("g3", [P, B, E])

                tb = ps("tb", [P, 4, P])
                qb = [ps(f"qb{i}", [P, 512]) for i in range(2)]
                psS = ps("psS", [P, B, P])
                mb = [ps(f"mb{i}", [P, 2, D]) for i in range(NB)]
                early_banks = [t[:].rearrange("p e n -> p (e n)").rearrange("p (a n) -> p a n", n=P) for t in mb]

            early = {(0, 0): tb, (0, 1): early_banks[0], (1, 0): early_banks[1], (1, 1): early_banks[2]}

            we_land = GR[:, NP - 16:NP, :].rearrange("p a n -> p (a n)").rearrange("p (c n) -> p c n", c=DC)
            wq_land = GR[:, NP - 20:NP - 16, :].rearrange("p a n -> p (a n)")[:, 0:DC * NQ]\
                .rearrange("p (c n) -> p c n", c=DC)

            with ExitStack() as s2f:
                sb = sb_in(s2f)
                X = [sb(f"X{i}", [P, B, P]) for i in range(NS)]
                Vn = [sb(f"Vn{i}", [P, B, P]) for i in range(NS)]
            with ExitStack() as s2:
                sb = sb_in(s2)
                ps = ps_in(s2)
                Xr = [sb(f"Xr{i}", [P, 2, B, P], F16)[:, 0] for i in range(NS)]
                Vr = [sb(f"Vr{i}", [P, 2, B, P], F16)[:, 0] for i in range(NS)]
                Sst = [sb(f"Sst{i}", [P, B, P]) for i in range(NS)]
                Sr = [sb(f"Sr{i}", [P, B, P], F16) for i in range(NS)]
                Sl = [sb(f"Sl{i}", [P, B, P], F16) for i in range(NS)]
                Xodd = [sb(f"Xodd{i}", [HALF, B, HALF]) for i in range(NS)]
                Fst = [t[0:HALF].rearrange("r b (h c) -> r (b h) c", h=2).rearrange("r (h b) c -> r h b c", h=2)
                       for t in Vn]
                pT = [ps(f"pT{i}", [P, B, P]) for i in range(NS)]
                pX = [ps(f"pX{i}", [P, B, P]) for i in range(NS)]
            with ExitStack() as s2b:
                ps = ps_in(s2b)
                pF = [ps(f"pF{i}", [P, 2, B, HALF]) for i in range(NS)]
                pV = [ps(f"pV{i}", [P, B, 2 * P]) for i in range(2)]

            with ExitStack() as s3b:
                sb = sb_in(s3b)
                work = sb("work", [P, BLK, BLK])
                prod = sb("prod", [P, BLK, BLK])
                below = sb("below", [P, BLK, BLK])
                RD = sb("RD", [P, BLK])
                YTs = sb("YTs", [P, NP, BLK])
                YT = [sb(f"YT{i}", [P, B, P]) for i in range(2)]
                LT = [sb(f"LT{i}", [P, B, P]) for i in range(2)]
            with ExitStack() as s3:
                ps = ps_in(s3)
                pP = ps("pP", [P, B, 2 * P])
                pU = ps("pU", [P, B, 2 * P])
                pYb = ps("pYb", [P, BLK // 2, P])
                pWork = pP[:].rearrange("p b n -> p (b n)").rearrange("p (c r) -> p c r", c=BLK)

            with ExitStack() as s3c:
                pYa = ps_in(s3c)("pYa", [P, BLK // 2, P])

        with ExitStack() as s4:
            sb = sb_in(s4)
            ps = ps_in(s4)
            YTs4 = sb("YTs4", [P, NP, BLK])
            YT4 = [sb(f"YTl{i}", [P, B, P]) for i in range(2)]
            Wst = [sb(f"Wst{i}", [P, B, P]) for i in range(2)]
            WT = sb("WT", [P, B, P])
            wo_sb = sb("wo_sb", [P, D])
            wo_hi = sb("wo_hi", [P, D], F32R)
            wo_lo = sb("wo_lo", [P, D], F32R)
            g_hi = sb("g_hi", [P, NP, E + 1], F32R)
            g_parts = sb("g_parts", [P, NP, 3, E + 1])
            be_land = sb("be_land", [GROWS, D])
            be_hi = sb("be_hi", [GROWS, D], F32R)
            be_lo = sb("be_lo", [GROWS, D])
            mask_hi = sb("mask_hi", [P, B])
            mask_lo = sb("mask_lo", [P, B])
            bebo4 = sb("bebo4", [GROWS, B, D], F32R)
            gst = sb("gst", [P, P])
            gT = sb("gT", [P, P], F32R)
            Vs = sb("Vs", [P, B, H])
            SD = sb("SD", [P, NP])
            upper = sb("upper", [P, P])
            PTm = sb("PTm", [P, B, P])
            MT = sb("MT", [P, B, H])
            O_hi = sb("O_hi", [P, B, P], F32R)
            O_lo = sb("O_lo", [P, B, P], F32R)
            xin = [sb(f"xin{i}", [P, B, D]) for i in range(2)]
            pin = [sb(f"pin{i}", [P, B, D]) for i in range(2)]
            vin = [sb(f"vin{i}", [P, B, H]) for i in range(2)]
            obuf = [sb(f"obuf{i}", [P, B, D]) for i in range(2)]
            pWT = ps("pWT", [P, B, P])
            pPT = ps("pPT", [P, B, P])
            pOT = ps("pOT", [P, B, P])
            pM = ps("pM", [P, B, H])
            pOut = ps("pOut", [P, B, D])
            pG = ps("pG", [P, 512])
            pW = ps("pW", [P, B, P])

        wq_loaded = sem("wq_loaded")
        we_loaded = sem("we_loaded")
        wq_split = sem("wq_split")
        we_hi_ready = sem("we_hi_ready")
        we_split = sem("we_split")
        consts_ready = sem("consts_ready")
        pool_step = sem("pool_step")
        dve_step = sem("dve_step")
        x_loaded = [sem(f"x_loaded{i}") for i in range(2)]
        var_ready = sem("var_ready")
        std_ready = sem("std_ready")
        rstd_ready = sem("rstd_ready")
        xn_ready = sem("xn_ready")
        xT_full = sem("xT_full")
        xT_hi = sem("xT_hi")
        xT_lo = sem("xT_lo")
        uq_full = sem("uq_full")
        uq_kept = sem("uq_kept")
        qb_full = [sem(f"qb_full{i}") for i in range(2)]
        qkv_ready = sem("qkv_ready")
        squares_done = sem("squares_done")
        norm_ready = sem("norm_ready")
        logits_shifted = sem("logits_shifted")
        exp_ready = sem("exp_ready")
        gates_ready = sem("gates_ready")
        u_ready = sem("u_ready")
        v_stored = sem("v_stored")
        gram_done = sem("gram_done")
        prefix_kept = sem("prefix_kept")
        stage1_over = sem("stage1_over")

        xm_loaded = [sem(f"xm_loaded{i}") for i in range(2)]
        xm_ready = sem("xm_ready")
        xmT_full = sem("xmT_full")
        xm_hi = sem("xm_hi")
        xm_lo = sem("xm_lo")
        mb_full = [sem(f"mb_full{i}") for i in range(NB)]
        mb_used = [sem(f"mb_used{i}") for i in range(NB)]
        tile_summed = sem("tile_summed")
        part_stored = [sem(f"part_stored{i}") for i in range(2)]

        s_staged = [sem(f"s_staged{i}") for i in range(NS)]
        x_init = [sem(f"x_init{i}") for i in range(NS)]
        t_full = [sem(f"t_full{i}") for i in range(NS)]
        v_ready = [sem(f"v_ready{i}") for i in range(NS)]
        x_full = [sem(f"x_full{i}") for i in range(NS)]
        x_ready = [sem(f"x_ready{i}") for i in range(NS)]
        x_half_ready = sem("x_half_ready")
        x_done = sem("x_done")
        au_full = [sem(f"au_full{i}") for i in range(NS)]
        au_ready = [sem(f"au_ready{i}") for i in range(NS)]
        g_full = [sem(f"g_full{i}") for i in range(NS)]
        g_kept = [sem(f"g_kept{i}") for i in range(NS)]
        ua_kept = [sem(f"ua_kept{i}") for i in range(NS)]

        s16_staged = [sem(f"s16_staged{i}") for i in range(NS)]
        xodd_ready = sem("xodd_ready")
        f_full = sem("f_full")
        f_ready = sem("f_ready")
        half_full = sem("half_full")
        half_done = sem("half_done")
        half_done_odd = sem("half_done_odd")
        consts3 = sem("consts3")
        blocks_gathered = sem("blocks_gathered")
        blocks_copied = sem("blocks_copied")
        blocks_factored = sem("blocks_factored")
        y_full = sem("y_full")
        y_kept = sem("y_kept")
        y_rd_kept = sem("y_rd_kept")
        yt_ready = sem("yt_ready")
        panel_full = sem("panel_full")
        panel_kept = sem("panel_kept")
        lt_ready = sem("lt_ready")
        update_full = sem("update_full")
        update_done = sem("update_done")

        yt4_set = sem("yt4_set")
        w_full = sem("w_full")
        w_staged = sem("w_staged")
        gates_split = sem("gates_split")
        be_ready = sem("be_ready")
        out_weights_loaded = sem("out_weights_loaded")
        gates_staged = sem("gates_staged")
        gt_full = sem("gt_full")
        gt_ready = sem("gt_ready")
        wt_full = sem("wt_full")
        wt_ready = sem("wt_ready")
        vs_ready = sem("vs_ready")
        pt_full = sem("pt_full")
        pt_masked = sem("pt_masked")
        ot_full = sem("ot_full")
        ot_high = sem("ot_high")
        ot_ready = sem("ot_ready")
        m_full = sem("m_full")
        m_zeroed = sem("m_zeroed")
        m_kept = sem("m_kept")
        out_full = sem("out_full")
        in_loaded = [sem(f"in_loaded{i}") for i in range(2)]
        in_summed = sem("in_summed")
        v_loaded = [sem(f"v_loaded{i}") for i in range(2)]
        out_ready = sem("out_ready")
        out_stored = [sem(f"out_stored{i}") for i in range(2)]

        block = ctx.enter_context(nc.Block())

        def within(g, n):
            return not isinstance(g, int) or g < n

        def steps_beside_stage1(eng, step, loop=lambda i: None, end=lambda: None):
            step(0, 0, 0)
            step(1, 1, 0)
            with eng.Fori(1, M1 // 2 - 2) as i:
                loop(i - 1)
                for par in range(2):
                    step(i * 2 + par, par, i)
                end()
            for k in range(M1 - 4, M1):
                step(k, k % 2, k // 2)

        def grp(k):
            return bass.ds(k * B, B)

        CONSTS = 10

        @block.sync
        def _(sp):
            def load_x(k, par):
                sp.dma_start(xbuf[par][:], x_v[k]).then_inc(x_loaded[par], 16)

            def load_xm(k, par):
                sp.dma_start(xm[par][:], x_v[k][:, 2 * par:2 * par + 2]).then_inc(xm_loaded[par], 16)

            def store_part(m, k, par):
                sp.wait_ge(tile_summed, m * 2 + 2)
                sp.dma_start(part_dram[k][:, 2 * par:2 * par + 2], acc[par][:]).then_inc(part_stored[par], 16)

            def store_v(g):
                sp.wait_ge(qkv_ready, g * B + B)
                sp.dma_start(v_dram[g], qkv[:, :, 2 * H:3 * H]).then_inc(v_stored, 16)

            load_x(0, 0)
            sp.dma_start(wq_land, wqkvg.rearrange("(c p) n -> p c n", p=P)).then_inc(wq_loaded, 16)
            sp.dma_start(bias_bc[:], bias_row.partition_broadcast(P)).then_inc(wq_loaded, 16)
            load_x(1, 1)
            load_xm(0, 0)
            load_xm(0, 1)
            sp.dma_start(we_land, we.rearrange("(c p) n -> p c n", p=P)).then_inc(we_loaded, 16)
            store_v(0)
            for g in range(2):
                sp.wait_ge(xT_full, 2 * g + 2)
                load_x(g + 2, g)
            sp.wait_ge(xmT_full, 1)
            load_xm(1, 0)

            def step(k, par, i):
                if within(k + 1, K):
                    store_v(k + 1)
                if within(k + 4, K):
                    sp.wait_ge(xT_full, k * 2 + 6)
                    load_x(k + 4, par)
                if within(k + 3, 2 * K):
                    sp.wait_ge(xmT_full, k + 2)
                    load_xm(i + 1 + par, 1 - par)
                store_part(k, i, par)

            steps_beside_stage1(sp, step)
            for m in range(M1, 2 * K):
                step(m, m % 2, m // 2)

            for par in range(2):
                sp.wait_ge(part_stored[par], 16 * K)
            sp.wait_ge(v_stored, 16 * K)
            sp.wait_ge(y_full, 3 * NJ)

            def load_v(k, par):
                sp.dma_start(vin[par][:], v_dram[k]).then_inc(v_loaded[par], 16)

            def load_in(k, par):
                sp.dma_start(xin[par][:], x_v[k]).then_inc(in_loaded[par], 16)
                sp.dma_start(pin[par][:], part_dram[k]).then_inc(in_loaded[par], 16)

            def store_out(k, par):
                sp.wait_ge(out_ready, k + 1)
                sp.dma_start(out_v[k], obuf[par][:]).then_inc(out_stored[par], 16)

            load_v(0, 0)
            load_v(1, 1)
            sp.dma_start(wo_sb[:], wo).then_inc(out_weights_loaded, 16)
            for n in range(B * 3):
                sp.dma_start(be_land[(E + 1) * n:(E + 1) * (n + 1), :], be_bo).then_inc(out_weights_loaded, 16)
            load_in(0, 0)
            load_in(1, 1)
            with sp.Fori(0, K // 2 - 1) as i:
                for par in range(2):
                    k = i * 2 + par
                    sp.wait_ge(vs_ready, k + 1)
                    load_v(k + 2, par)
                    store_out(k, par)
                    load_in(k + 2, par)
            for k in range(K - 2, K):
                store_out(k, k % 2)
            for par in range(2):
                sp.wait_ge(out_stored[par], 16 * (K // 2))

        @block.gpsimd
        def _(pool):
            st = Steps(pool, pool_step)
            st.done(nc.gpsimd.memset(ident[:], 0.0))
            st.wait()
            nc.gpsimd.affine_select(out=ident[:], in_=ident[:], compare_op=ALU.not_equal, fill=1.0, base=0,
                                    pattern=[[-1, P]], channel_multiplier=1).then_inc(consts_ready, 1)
            for e in range(E):
                nc.gpsimd.memset(rev[:, e:e + 1], float(E - e))
            nc.gpsimd.memset(gates[:], 1.0).then_inc(consts_ready, 1)
            pool.wait_ge(consts_ready, 2)
            nc.gpsimd.tensor_copy(GR[:, 0:B, 0:P], ident[:].unsqueeze(1).broadcast_to([P, B, P]))\
                .then_inc(consts_ready, 1)

            def normalise(xt, stats, tiles):
                st.done(nc.gpsimd.tensor_tensor(xt, xt, mean[:, stats].unsqueeze(2).broadcast_to([P, tiles, D]),
                                                ALU.subtract))
                st.wait()
                return nc.gpsimd.tensor_tensor(xt, xt, rstd[:, stats].unsqueeze(2).broadcast_to([P, tiles, D]),
                                               ALU.mult)

            def norm_group(g, par):
                pool.wait_ge(rstd_ready, g + 1)
                normalise(xbuf[par][:], grp(g), B).then_inc(xn_ready, 1)

            def norm_pair(m, par, i, chunk):
                pool.wait_ge(xm_loaded[par], i * 16 + 16)
                if chunk is not None:
                    pool.wait_ge(rstd_ready, chunk + 1)
                normalise(xm[par][:], bass.ds(m * 2, 2), 2).then_inc(xm_ready, 1)

            def sum_tile(m, par, t):
                n = m * 2 + t
                four = tmp[t]
                pool.wait_ge(mb_used[3], n + 1)
                st.done(nc.gpsimd.tensor_tensor(four[:, 0], four[:, 0], four[:, 1], ALU.add))
                st.wait()
                st.done(nc.gpsimd.tensor_tensor(four[:, 0, 0], four[:, 0, 0], four[:, 0, 1], ALU.add))
                st.wait()
                pool.wait_ge(mb_used[2], n + 1)
                nc.gpsimd.tensor_tensor(acc[par][:, t], four[:, 0, 0], acc[par][:, t], ALU.add)\
                    .then_inc(tile_summed, 1)

            norm_pair(0, 0, 0, 0)
            norm_pair(1, 1, 0, None)
            pool.wait_ge(we_hi_ready, 1)
            nc.gpsimd.tensor_tensor(we_lo[:], we_land, we_hi[:].bitcast(F32), ALU.subtract).then_inc(we_split, 1)
            nc.gpsimd.tensor_scalar(twoI[:], ident[:], 2.0, None, ALU.mult).then_inc(consts_ready, 1)
            nc.gpsimd.tensor_scalar(firstI[:], ident[:], X16 * 2.0 * start * scales[0], None, ALU.mult).then_inc(consts_ready, 1)
            nc.gpsimd.tensor_scalar(deltaI[:], ident[:], X16, None, ALU.mult).then_inc(consts_ready, 1)
            nc.gpsimd.tensor_scalar(firstI64[:], ident[:], X16 * 2.0 * start64 * scales64[0], None, ALU.mult)\
                .then_inc(consts_ready, 1)


            def step(m, par, i):
                norm_pair(m + 2, par, i + 1, i + 1 if par == 0 else None)
                sum_tile(m, par, 0)
                if within(m + 3, K):
                    norm_group(m + 3, 1 - par)
                sum_tile(m, par, 1)

            PER = 2 * (4 + 1 + 1)
            steps_beside_stage1(pool, step, lambda i: st.loop(i, PER), lambda: st.end(M1 // 2 - 3, PER))

            pool.wait_ge(stage1_over, 3)
            pool.wait_ge(v_stored, 16 * K)
            def stage_high(k, s):
                nc.gpsimd.tensor_copy(Sr[s][:], GR[:, grp(k), 0:P]).then_inc(s16_staged[s], 1)

            def stage_low(s, high):
                pool.wait_ge(s16_staged[s], high)
                st.wait()
                nc.gpsimd.tensor_tensor(Sl[s][:], Sst[s][:], Sr[s][:], ALU.subtract).then_inc(s_staged[s], 1)

            def stage_s(k, s, high):
                st.done(nc.gpsimd.tensor_copy(Sst[s][:], GR[:, grp(k), 0:P]))
                pool.wait_ge(au_full[s], high)
                stage_low(s, high)

            with pool.Fori(0, NR - 1) as i:
                st.loop(i, NS)
                for s in range(NS):
                    pool.wait_ge(t_full[s], i * NIT + 1)
                    stage_s(i * NS + s, s, i + 1)
                st.end(NR - 1, NS)
                for s in range(NS):
                    pool.wait_ge(t_full[s], i * NIT + (LOW + 1))
                    stage_high(i * NS + (NS + s), s)
            for s in range(NS):
                pool.wait_ge(t_full[s], (NR - 1) * NIT + 1)
                stage_s((NR - 1) * NS + s, s, NR)

            def stage_s64(s, r, to):
                for h in range(2):
                    st.wait()
                    rows = slice(HALF * h, HALF * (h + 1))
                    st.done(nc.gpsimd.tensor_copy(to[s][rows, :, rows],
                                                  GR[0:HALF, grp(2 * (r * NS + s) + h), 0:HALF]))
                st.wait()

            for s in range(NS):
                pool.wait_ge(g_kept[s], NR64 + 1)
            for s in range(NS):
                pool.wait_ge(t_full[s], (NR - 1) * NIT + (LOW + 1))
                st.done(nc.gpsimd.memset(Sr[s][:], 0.0))
                stage_s64(s, 0, Sr)
                nc.gpsimd.sem_inc(s16_staged[s], 1)
            for s in range(NS):
                pool.wait_ge(t_full[s], STEPS1 + 1)
                st.done(nc.gpsimd.memset(Sst[s][:], 0.0))
            for r in range(NR64):
                for s in range(NS):
                    pool.wait_ge(t_full[s], STEPS1 + r * NIT64 + 1)
                    pool.wait_ge(g_kept[s], NR + 1)
                    stage_s64(s, r, Sst)
                    pool.wait_ge(x_full[s], STEPS1 + r * NIT64)
                    stage_low(s, NR + r + 1)
                if r + 1 < NR64:
                    for s in range(NS):
                        pool.wait_ge(t_full[s], STEPS1 + r * NIT64 + LOW64 + 1)
                        stage_s64(s, r + 1, Sr)
                        nc.gpsimd.sem_inc(s16_staged[s], 1)

            pool.wait_ge(half_done, K // 2)
            pool.wait_ge(half_done_odd, K // 2)

            st.done(nc.gpsimd.memset(below[:], 1.0))
            st.wait()
            nc.gpsimd.affine_select(out=below[:], in_=below[:], compare_op=ALU.is_gt, fill=0.0, base=0,
                                    pattern=[[1, BLK], [-1, BLK]], channel_multiplier=0).then_inc(consts3, 1)
            def block_rows(j, h):
                return slice(HALF * h + BLK * j, HALF * h + BLK * (j + 1))

            for j in range(NJ):
                if j:
                    pool.wait_ge(panel_full, j * K)
                    pool.wait_ge(update_full, j * K)
                last = j == NJ - 1
                for par in range(0 if last else 2):
                    st.done(nc.gpsimd.tensor_copy(YT[par][:], ident[:].unsqueeze(1).broadcast_to([P, B, P])))
                    st.done(nc.gpsimd.memset(LT[par][:], 0.0))
                for m in range(M1 + j * MJ, M1 + j * MJ + MJ):
                    if m + 2 < 2 * K:
                        norm_pair(m + 2, m % 2, m // 2 + 1, None)
                    sum_tile(m, m % 2, 0)
                    sum_tile(m, m % 2, 1)
                pool.wait_ge(tile_summed, 2 * (m + 1))
                if last:
                    break
                pool.wait_ge(y_kept, j + 1)
                pool.wait_ge(y_rd_kept, 2 * (j + 1))

                def stage_yt(g, par):
                    for h in range(2):
                        rows = block_rows(j, h)
                        nc.gpsimd.tensor_copy(YT[par][rows, :, rows], YTs[rows, grp(g), :]).then_inc(yt_ready, 1)
                        pool.wait_ge(yt_ready, g * 2 + (2 * j * K + h + 1))

                def make_lt(g, par):
                    pool.wait_ge(panel_kept, g + (j * K + 1))
                    for h in range(2):
                        rows = block_rows(j, h)
                        cols = block_rows(j + 1, h)
                        nc.gpsimd.tensor_tensor(LT[par][rows, :, cols], GR[rows, grp(g), cols],
                                                RDall[rows, grp(g)].unsqueeze(2).broadcast_to([BLK, B, BLK]),
                                                ALU.mult).then_inc(lt_ready, 1)
                        pool.wait_ge(lt_ready, g * 2 + (2 * j * K + h + 1))

                def step(g, par):
                    pool.wait_ge(panel_full, g + (j * K + 1))
                    stage_yt(g + 2, par)
                    if not (isinstance(g, int) and g < 2):
                        pool.wait_ge(update_full, g + (j * K - 1))
                    make_lt(g, par)

                stage_yt(0, 0)
                stage_yt(1, 1)
                step(0, 0)
                step(1, 1)
                with pool.Fori(1, K // 2 - 1) as i:
                    for par in range(2):
                        step(i * 2 + par, par)
                for g in (K - 2, K - 1):
                    pool.wait_ge(update_full, g + j * K - 1)
                    make_lt(g, g % 2)

            pool.wait_ge(y_full, 3 * NJ)
            pool.wait_ge(y_kept, NJ)
            pool.wait_ge(y_rd_kept, 2 * NJ)
            pool.wait_ge(yt4_set, 2)

            def stage_yt4(g, par, done):
                if done is not None:
                    pool.wait_ge(w_full, done)
                for h in range(2):
                    rows = block_rows(NJ - 1, h)
                    nc.gpsimd.tensor_copy(YT4[par][rows, :, rows], YTs4[rows, grp(g), :]).then_inc(yt_ready, 1)
                    pool.wait_ge(yt_ready, g * 2 + (2 * (NJ - 1) * K + h + 1))

            stage_yt4(0, 0, None)
            stage_yt4(1, 1, None)
            for par in range(2):
                pool.wait_ge(part_stored[par], 16 * K)
            st.done(nc.gpsimd.memset(upper[:], 1.0))
            st.done(nc.gpsimd.memset(mask_hi[:], 1.0))
            st.done(nc.gpsimd.memset(mask_lo[:], 1.0))
            st.done(nc.gpsimd.memset(gst[:], 0.0))
            st.wait()
            nc.gpsimd.affine_select(out=upper[:], in_=upper[:], compare_op=ALU.is_ge, fill=0.0, base=0,
                                    pattern=[[1, P]], channel_multiplier=-1).then_inc(consts_ready, 1)
            for mask, lo, hi in ((mask_hi, 0, 2), (mask_lo, 2, 3)):
                step = 3 * (E + 1)
                st.done(nc.gpsimd.affine_select(out=mask[:], in_=mask[:], compare_op=ALU.is_ge, fill=0.0,
                                                base=-lo * (E + 1), pattern=[[-step, B]], channel_multiplier=1))
                st.wait()
                nc.gpsimd.affine_select(out=mask[:], in_=mask[:], compare_op=ALU.is_ge, fill=0.0,
                                        base=hi * (E + 1) - 1, pattern=[[step, B]], channel_multiplier=-1)\
                    .then_inc(consts_ready, 1)

            def stage_gates(k):
                if not (isinstance(k, int) and k == 0):
                    pool.wait_ge(gt_full, k)
                nc.gpsimd.tensor_copy(gst[:, 0:GROWS].rearrange("p (b f) -> p b f", b=B),
                                      g_parts[:, grp(k)].rearrange("p b a e -> p b (a e)")).then_inc(gates_staged, 1)

            def add_in(k, par, i):
                pool.wait_ge(in_loaded[par], i * 32 + 32)
                nc.gpsimd.tensor_tensor(pin[par][:], pin[par][:], xin[par][:], ALU.add).then_inc(in_summed, 1)

            pool.wait_ge(gates_split, 2)
            stage_gates(0)
            pool.wait_ge(gates_staged, 1)
            with pool.Fori(0, K // 2 - 1) as i:
                for par in range(2):
                    k = i * 2 + par
                    stage_yt4(k + 2, par, k + 1)
                    stage_gates(k + 1)
                    add_in(k, par, i)
                    pool.wait_ge(gates_staged, k + 2)
                    pool.wait_ge(in_summed, k + 1)
            stage_gates(K - 1)
            for k in (K - 2, K - 1):
                add_in(k, k % 2, K // 2 - 1)

        @block.scalar
        def _(act):
            def copy(o, i, scale=1.0):
                return nc.scalar.activation(o, i, ACT.Copy, scale=scale)

            def sqrt_var(g):
                act.wait_ge(var_ready, g + 1)
                nc.scalar.activation(std[:], veps[:], ACT.Sqrt).then_inc(std_ready, 1)

            def xm_high(m, par, used):
                act.wait_ge(xmT_full, m + 1)
                if used:
                    act.wait_ge(mb_full[NB - 1], m * 2 - 2)
                bank = early_banks[3] if isinstance(m, int) and m == 0 else tb[:]
                copy(xh[par][:], bank.rearrange("p (t c) m -> p c t m", c=DC)).then_inc(xm_hi, 1)

            def x_high(g, h):
                act.wait_ge(xT_full, g * 2 + (h + 1))
                if not (isinstance(g, int) and g == 0):
                    act.wait_ge(qb_full[1], g * 2)
                bank = early.get((g, h), tb) if isinstance(g, int) else tb
                copy(qh[:, :, 2 * h:2 * h + 2, :],
                     bank[:, 0:4].rearrange("p (t c) m -> p c t m", c=DC)).then_inc(xT_hi, 1)

            def norms(g):
                for t in range(B):
                    act.wait_ge(qkv_ready, g * B + (t + 1))
                    nc.scalar.activation(ksq[:, t], qkv[:, t, H:2 * H], ACT.Square,
                                         accum_out=ss[:, t:t + 1]).then_inc(squares_done, 1)
                act.wait_ge(squares_done, g * B + B)
                nc.scalar.activation(nrm[:], ss[:], ACT.Sqrt).then_inc(norm_ready, 1)

            def exps(g):
                act.wait_ge(logits_shifted, g + 1)
                nc.scalar.activation(gex[:], gd[:], ACT.Exp).then_inc(exp_ready, 1)

            def experts(m, t, b):
                n = m * 2 + t
                q = 2 * b + 1
                if b == 0 and not (isinstance(m, int) and m == 0):
                    act.wait_ge(tile_summed, n - 1)
                act.wait_ge(mb_full[q], n + 1)
                for h in range(2):
                    e = 2 * q + h
                    ins = copy(tmp[t][:, b, h], mb[q][:, h], gates[:, bass.ds(n, 1), e:e + 1].squeeze(1))
                ins.then_inc(mb_used[q], 1)

            def keep_uq(g, h):
                act.wait_ge(uq_full, g * 2 + (h + 1))
                uq = tb[:].rearrange("p (t a) m -> p a t m", a=2)
                tiles = bass.ds(g * B + 2 * h, 2)
                copy(GR[:, tiles, P:2 * P], uq[:, 0])
                copy(QT[:, tiles, :], uq[:, 1]).then_inc(uq_kept, 1)

            sqrt_var(0)
            x_high(0, 0)
            x_high(0, 1)
            xm_high(0, 0, False)
            sqrt_var(1)
            act.wait_ge(we_loaded, 16)
            copy(we_hi[:], we_land).then_inc(we_hi_ready, 1)
            norms(0)
            x_high(1, 0)
            x_high(1, 1)
            exps(0)
            keep_uq(0, 0)
            keep_uq(0, 1)
            sqrt_var(2)

            def step(k, par, i):
                g = k + 1
                if within(g, K):
                    if within(k + 2, K):
                        x_high(k + 2, 0)
                    norms(g)
                    exps(g)
                    if within(k + 2, K):
                        x_high(k + 2, 1)
                act.wait_ge(gates_ready, k + 1)
                experts(k, 0, 0)
                xm_high(k + 1, 1 - par, not (isinstance(k, int) and k == 0))
                experts(k, 0, 1)
                if within(k + 3, K):
                    sqrt_var(k + 3)
                if within(g, K):
                    keep_uq(g, 0)
                experts(k, 1, 0)
                if within(g, K):
                    keep_uq(g, 1)
                experts(k, 1, 1)

            steps_beside_stage1(act, step)
            act.wait_ge(uq_kept, 2 * K)
            nc.scalar.sem_inc(stage1_over, 1)
            act.wait_ge(stage1_over, 3)
            act.wait_ge(v_stored, 16 * K)

            def newton(before, nit, low, scales):
                for it in range(nit - 1):
                    x = Xr if it < low - 1 else X
                    scale = scales[it + 1] * (0.5 / X16 if it == low - 1 else 1.0)
                    for s in range(NS):
                        act.wait_ge(x_full[s], before + (it + 1))
                        copy(x[s][:], pX[s][:], scale).then_inc(x_ready[s], 1)
                        if it == nit - 2:
                            copy(Sl[s][:], pX[s][:], scale * X16).then_inc(x_half_ready, 1)

            for s in range(NS):
                nc.scalar.sem_inc(ua_kept[s], 1)
            with act.Fori(0, NR) as i:
                newton(i * NIT, NIT, LOW, scales)
                for s in range(NS):
                    act.wait_ge(au_full[s], i + 2)
                    copy(Vn[s][:], pT[s][:]).then_inc(au_ready[s], 1)
                for s in range(NS):
                    act.wait_ge(g_full[s], i + 1)
                    copy(GR[:, grp(i * NS + s), P:2 * P], pX[s][:]).then_inc(ua_kept[s], 1)

            for r in range(NR64):
                newton(STEPS1 + r * NIT64, NIT64, LOW64, scales64)
                for s in range(NS):
                    act.wait_ge(x_done, (NR + r) * NS + s + 1)
                    copy(Xodd[s][:], X[s][HALF:P, :, HALF:P]).then_inc(xodd_ready, 1)
                for s in range(NS):
                    act.wait_ge(f_full, r * NS + s + 1)
                    copy(Fst[s][:, 0], pF[s][0:HALF, 0])
                    copy(Fst[s][:, 1], pF[s][0:HALF, 1], -1.0).then_inc(f_ready, 1)
                for g in range(2 * r * NS + 1, 2 * (r + 1) * NS, 2):
                    act.wait_ge(half_full, g + 1)
                    copy(GR[HALF:P, grp(g), HALF:2 * P], pV[1][HALF:P, :, HALF:2 * P]).then_inc(half_done_odd, 1)

            for j in range(NJ):
                for m in range(M1 + j * MJ, M1 + j * MJ + MJ):
                    if m + 1 < 2 * K:
                        xm_high(m + 1, (m + 1) % 2, True)
                    experts(m, 0, 0)
                    experts(m, 0, 1)
                    experts(m, 1, 0)
                    experts(m, 1, 1)
                last = j == NJ - 1
                if last:
                    act.wait_ge(mb_full[NB - 1], 4 * K)
                    for par in range(2):
                        copy(YT4[par][:], ident[:].unsqueeze(1).broadcast_to([P, B, P])).then_inc(yt4_set, 1)
                yts = YTs4 if last else YTs
                act.wait_ge(y_full, 3 * j + 2)
                for h in range(2):
                    rows = slice(HALF * h + BLK * j, HALF * h + BLK * (j + 1))
                    ins = copy(yts[rows, :, 0:BLK // 2].rearrange("c p i -> c i p"),
                               pYb[0:BLK, :, h * HALF:(h + 1) * HALF])
                ins.then_inc(y_kept, 1)

                if last:
                    break

                def keep_panel(g):
                    act.wait_ge(panel_full, g + (j * K + 1))
                    copy(GR[:, grp(g), BLK * (j + 1):2 * P], pP[:, :, BLK * (j + 1):2 * P]).then_inc(panel_kept, 1)

                with act.Fori(0, K) as g:
                    keep_panel(g)

            act.wait_ge(y_full, 3 * NJ)
            act.wait_ge(y_rd_kept, 2 * NJ)
            for par in range(2):
                act.wait_ge(part_stored[par], 16 * K)

            def keep_w(k, par, done):
                act.wait_ge(w_full, k + 1)
                if done is not None:
                    act.wait_ge(m_full, done)
                copy(Wst[par][:], pW[:]).then_inc(w_staged, 1)

            def keep_wt(k):
                act.wait_ge(wt_full, k + 1)
                copy(WT[:], pWT[:]).then_inc(wt_ready, 1)

            def keep_ot(k):
                act.wait_ge(ot_full, k + 1)
                if not (isinstance(k, int) and k == 0):
                    act.wait_ge(out_full, k)
                copy(O_hi[:], pOT[:]).then_inc(ot_high, 1)

            def keep_m(k):
                act.wait_ge(m_full, k + 1)
                copy(MT[:], pM[:]).then_inc(m_kept, 1)

            def keep_gt(k):
                act.wait_ge(gt_full, k + 1)
                if not (isinstance(k, int) and k == 0):
                    act.wait_ge(out_full, k)
                copy(gT[:], pG[:, 0:P]).then_inc(gt_ready, 1)

            keep_w(0, 0, None)
            keep_w(1, 1, None)
            keep_wt(0)
            keep_gt(0)

            def step(k, par):
                keep_wt(k + 1)
                keep_ot(k)
                keep_m(k)
                if within(k + 2, K):
                    keep_w(k + 2, par, k + 1)
                keep_gt(k + 1)

            step(0, 0)
            step(1, 1)
            with act.Fori(1, K // 2 - 1) as i:
                for par in range(2):
                    step(i * 2 + par, par)
            step(K - 2, 0)
            keep_ot(K - 1)

        @block.vector
        def _(dve):
            st = Steps(dve, dve_step)
            v = nc.vector
            v.memset(psS[:], 0.0).then_inc(prefix_kept, 1)

            def split_low(lo, whole, hi):
                return v.tensor_tensor(lo, whole, hi.bitcast(F32), ALU.subtract)

            def stats_a(g, par, i):
                dve.wait_ge(x_loaded[par], i * 16 + 16)
                for t in range(B):
                    ins = v.bn_stats(bnst[:, t], xbuf[par][:, t])
                st.done(ins)

            def join_stats(g):
                st.wait()
                v.tensor_tensor(mdiff[:], bnst[:, :, 1], bnst[:, :, 4], ALU.subtract)
                st.done(v.tensor_tensor(msum[:], bnst[:, :, 1:3], bnst[:, :, 4:6], ALU.add))
                st.wait()
                v.tensor_scalar(mean[:, grp(g)], msum[:, :, 0], 0.5, None, ALU.mult)
                st.done(v.scalar_tensor_tensor(mdiff[:], mdiff[:], 0.25, mdiff[:], ALU.mult, ALU.mult))
                st.wait()
                st.done(v.scalar_tensor_tensor(veps[:], msum[:, :, 1], 1.0 / D, mdiff[:], ALU.mult, ALU.add))
                st.wait()
                v.tensor_scalar(veps[:], veps[:], LN_EPS, None, ALU.add).then_inc(var_ready, 1)

            def stats_b(g):
                dve.wait_ge(std_ready, g + 1)
                v.reciprocal(rstd[:, grp(g)], std[:]).then_inc(rstd_ready, 1)

            def norm_group(g, par):
                dve.wait_ge(rstd_ready, g + 1)
                for t in range(B):
                    one = slice(g * B + t, g * B + t + 1)
                    ins = v.tensor_scalar(xbuf[par][:, t], xbuf[par][:, t], mean[:, one], rstd[:, one],
                                          ALU.subtract, ALU.mult)
                ins.then_inc(xn_ready, 1)

            def xm_low(m, par, used):
                dve.wait_ge(xm_hi, m + 1)
                if used:
                    dve.wait_ge(mb_full[NB - 1], m * 2 - 2)
                bank = early_banks[3] if isinstance(m, int) and m == 0 else tb[:]
                split_low(xl[par][:], bank.rearrange("p (t c) m -> p c t m", c=DC), xh[par][:]).then_inc(xm_lo, 1)

            def expert(m, par, t, q, h, i=None, but=0):
                n, e = m * 2 + t, 2 * q + h
                gate = gates[:, bass.ds(n, 1), e:e + 1].squeeze(1)
                if h == 0:
                    dve.wait_ge(mb_full[q], n + 1)
                    if q == 2:
                        dve.wait_ge(mb_used[0], n + 1)
                    elif t == 0 and i is not None:
                        dve.wait_ge(part_stored[par], i * 16)
                else:
                    st.wait(but)
                if e == 0:
                    ins = v.tensor_scalar(acc[par][:, t], mb[q][:, h], gate, None, ALU.mult)
                else:
                    ins = v.scalar_tensor_tensor(acc[par][:, t], mb[q][:, h], gate, acc[par][:, t],
                                                 ALU.mult, ALU.add)
                if h == 0:
                    st.done(ins)
                else:
                    ins.then_inc(mb_used[q], 1)

            def experts(m, par, t, q):
                for h in range(2):
                    expert(m, par, t, q, h)

            def bc(a):
                return a.unsqueeze(2).broadcast_to([P, B, E])

            def x_low(g, h):
                dve.wait_ge(xT_hi, g * 2 + (h + 1))
                bank = early.get((g, h), tb) if isinstance(g, int) else tb
                split_low(ql[:, :, 2 * h:2 * h + 2, :], bank[:, 0:4].rearrange("p (t c) m -> p c t m", c=DC),
                          qh[:, :, 2 * h:2 * h + 2, :]).then_inc(xT_lo, 1)

            def keep_qkv(g, t):
                if t == 0 and not (isinstance(g, int) and g == 0):
                    dve.wait_ge(uq_full, g * 2)
                    dve.wait_ge(gram_done, g)
                    dve.wait_ge(v_stored, g * 16)
                dve.wait_ge(qb_full[t % 2], g * 2 + (t // 2 + 1))
                v.tensor_tensor(qkv[:, t], qb[t % 2][:, 0:NQ], bias_bc[:], ALU.add).then_inc(qkv_ready, 1)

            def shift_logits(g):
                dve.wait_ge(qkv_ready, g * B + B)
                lg = qkv[:, :, 3 * H:NQ]
                st.done(v.tensor_reduce(gm[:], lg, AX, ALU.max))
                st.wait()
                v.tensor_tensor(gd[:], lg, bc(gm[:]), ALU.subtract).then_inc(logits_shifted, 1)

            def dots(g):
                for t in range(B):
                    v.scalar_tensor_tensor(kq[:, t], qkv[:, t, 0:H], 1.0, qkv[:, t, H:2 * H], ALU.mult,
                                           ALU.mult, accum_out=sdot[:, bass.ds(g * B + t, 1)])

            def pad_norms(g):
                dve.wait_ge(norm_ready, g + 1)
                st.done(v.tensor_scalar(nrme[:], nrm[:], NORM_EPS, None, ALU.add))

            def make_u(g):
                st.wait()
                st.done(v.reciprocal(rn[:], nrme[:]))
                st.wait()
                v.tensor_tensor(qkv[:, :, H:2 * H], qkv[:, :, H:2 * H],
                                rn[:].unsqueeze(2).broadcast_to([P, B, H]), ALU.mult).then_inc(u_ready, 1)

            def choose(g):
                revb = rev[:].unsqueeze(1).broadcast_to([P, B, E])
                dve.wait_ge(logits_shifted, g + 1)
                st.done(v.scalar_tensor_tensor(g1[:], gd[:], 0.0, revb, ALU.is_equal, ALU.mult))
                st.wait()
                st.done(v.tensor_reduce(gm[:], g1[:], AX, ALU.max))
                st.wait()
                st.done(v.tensor_tensor(g1[:], g1[:], bc(gm[:]), ALU.is_equal))
                st.wait()
                st.done(v.scalar_tensor_tensor(g2[:], g1[:], -3.0e38, gd[:], ALU.mult, ALU.add))
                st.wait()
                st.done(v.tensor_reduce(gm[:], g2[:], AX, ALU.max))
                st.wait()
                st.done(v.tensor_tensor(g3[:], g2[:], bc(gm[:]), ALU.is_equal))
                st.wait()
                st.done(v.tensor_tensor(g3[:], g3[:], revb, ALU.mult))
                st.wait()
                st.done(v.tensor_reduce(gm[:], g3[:], AX, ALU.max))
                st.wait()
                st.done(v.tensor_tensor(g3[:], g3[:], bc(gm[:]), ALU.is_equal))
                st.wait()
                st.done(v.tensor_tensor(g1[:], g1[:], g3[:], ALU.add))
                st.wait()
                dve.wait_ge(exp_ready, g + 1)
                st.done(v.tensor_tensor(g1[:], g1[:], gex[:], ALU.mult))
                st.wait()
                st.done(v.tensor_reduce(gsum[:], g1[:], AX, ALU.add))
                st.wait()
                st.done(v.reciprocal(gm[:], gsum[:]))
                st.wait()
                v.tensor_tensor(gates[:, grp(g), 0:E], g1[:], bc(gm[:]), ALU.mult).then_inc(gates_ready, 1)

            def keep_prefix(g):
                dve.wait_ge(gram_done, g + 1)
                v.tensor_tensor(GR[:, grp(g + 1), 0:P], psS[:],
                                ident[:].unsqueeze(1).broadcast_to([P, B, P]), ALU.add).then_inc(prefix_kept, 1)

            dve.wait_ge(consts_ready, 2)
            stats_a(0, 0, 0)
            join_stats(0)
            dve.wait_ge(wq_loaded, 32)
            st.done(v.tensor_copy(wq_hi[:], wq_land))
            st.wait()
            split_low(wq_lo[:], wq_land, wq_hi[:]).then_inc(wq_split, 1)
            stats_b(0)
            norm_group(0, 0)
            stats_a(1, 1, 0)
            join_stats(1)
            x_low(0, 0)
            x_low(0, 1)
            xm_low(0, 0, False)
            stats_b(1)
            norm_group(1, 1)
            for t in range(B):
                keep_qkv(0, t)
            shift_logits(0)
            dots(0)
            pad_norms(0)
            make_u(0)
            x_low(1, 0)
            x_low(1, 1)
            choose(0)
            stats_a(2, 0, 1)
            join_stats(2)
            stats_b(2)
            norm_group(2, 0)

            def step(k, par, i):
                g = k + 1
                more = within(g, K)
                if more:
                    keep_qkv(g, 0)
                    keep_qkv(g, 1)
                if not (isinstance(k, int) and k == 0):
                    experts(k - 1, 1 - par, 1, 2)
                if more:
                    keep_prefix(k)
                    keep_qkv(g, 2)
                    keep_qkv(g, 3)
                    shift_logits(g)
                    if within(k + 2, K):
                        x_low(k + 2, 0)
                    dots(g)
                expert(k, par, 0, 0, 0, None if isinstance(k, int) and k < 2 else i)
                if more:
                    pad_norms(g)
                expert(k, par, 0, 0, 1, but=int(more))
                if more:
                    make_u(g)
                if within(k + 2, K):
                    x_low(k + 2, 1)
                if within(k + 3, K):
                    stats_a(k + 3, 1 - par, i + 1 + par)
                xm_low(k + 1, 1 - par, not (isinstance(k, int) and k == 0))
                expert(k, par, 0, 2, 0)
                expert(k, par, 1, 0, 0)
                expert(k, par, 0, 2, 1, but=1)
                expert(k, par, 1, 0, 1)
                if within(k + 3, K):
                    join_stats(k + 3)
                if within(k + 3, K):
                    stats_b(k + 3)
                if more:
                    choose(g)

            PER = 2 * (2 + 5 + 13 + 4)
            steps_beside_stage1(dve, step, lambda i: st.loop(i, PER), lambda: st.end(M1 // 2 - 3, PER))
            experts(M1 - 1, (M1 - 1) % 2, 1, 2)
            dve.wait_ge(u_ready, K)
            v.sem_inc(stage1_over, 1)
            dve.wait_ge(stage1_over, 3)
            dve.wait_ge(v_stored, 16 * K)
            dve.wait_ge(consts_ready, CONSTS - 3)

            def bc_b(a):
                return a[:].unsqueeze(1).broadcast_to([P, B, P])

            def make_v(before, nit, low):
                for it in range(nit):
                    for s in range(NS):
                        dve.wait_ge(t_full[s], before + (it + 2))
                        if it < nit - 1:
                            o = (Vr if it < low else Vn)[s][:]
                            ins = v.scalar_tensor_tensor(o, pT[s][:], -1.0 / X16 if it < low else -1.0, bc_b(twoI),
                                                         ALU.mult, ALU.add)
                        else:
                            ins = v.scalar_tensor_tensor(Vr[s][:], pT[s][:], -X16, bc_b(deltaI), ALU.mult, ALU.add)
                        ins.then_inc(v_ready[s], 1)
                for s in range(NS):
                    dve.wait_ge(x_full[s], before + nit)
                    v.scalar_tensor_tensor(X[s][:], pX[s][:], 1.0 / (X16 * X16), X[s][:], ALU.mult, ALU.add)\
                        .then_inc(x_done, 1)

            for s in range(NS):
                v.sem_inc(g_kept[s], 1)

            for s in range(NS):
                v.tensor_copy(Sr[s][:], GR[:, grp(s), 0:P]).then_inc(s16_staged[s], 1)

            def first_x(k, s, done):
                dve.wait_ge(au_full[s], done)
                v.scalar_tensor_tensor(Xr[s][:], GR[:, grp(k), 0:P], -X16 * scales[0] * start * start,
                                       bc_b(firstI), ALU.mult, ALU.add).then_inc(x_init[s], 1)

            def keep_g(k, s, done):
                dve.wait_ge(g_full[s], done)
                v.tensor_tensor(GR[:, grp(k), 0:P], pT[s][:], bc_b(ident), ALU.add).then_inc(g_kept[s], 1)

            for s in range(NS):
                first_x(s, s, 1)
            with dve.Fori(0, NR - 1) as i:
                make_v(i * NIT, NIT, LOW)
                for s in range(NS):
                    first_x(i * NS + (NS + s), s, i + 2)
                for s in range(NS):
                    keep_g(i * NS + s, s, i + 1)
            make_v((NR - 1) * NIT, NIT, LOW)

            def first_x64(s, r):
                dve.wait_ge(s16_staged[s], NR + r + 1)
                v.scalar_tensor_tensor(Xr[s][:], Sr[s][:], -X16 * scales64[0] * start64 * start64,
                                       bc_b(firstI64), ALU.mult, ALU.add).then_inc(x_init[s], 1)

            for s in range(NS):
                dve.wait_ge(au_full[s], NR + 1)
                first_x64(s, 0)
            for s in range(NS):
                keep_g((NR - 1) * NS + s, s, NR)

            for r in range(NR64):
                make_v(STEPS1 + r * NIT64, NIT64, LOW64)
                if r + 1 < NR64:
                    for s in range(NS):
                        dve.wait_ge(f_full, r * NS + s + 1)
                        first_x64(s, r + 1)
                for g in range(2 * r * NS, 2 * (r + 1) * NS, 2):
                    dve.wait_ge(half_full, g + 1)
                    v.tensor_tensor(GR[HALF:P, grp(g), HALF:2 * P], GR[HALF:P, grp(g), HALF:2 * P],
                                    pV[0][HALF:P, :, HALF:2 * P], ALU.subtract).then_inc(half_done, 1)

            dve.wait_ge(consts3, 1)
            for j in range(NJ):
                dve.wait_ge(blocks_gathered, 2 * j + 1)
                if j:
                    dve.wait_ge(y_full, 3 * j)
                v.tensor_copy(work[:, 0:BLK // 2], pWork[:, 0:BLK // 2])
                dve.wait_ge(blocks_gathered, 2 * j + 2)
                v.tensor_copy(work[:, BLK // 2:BLK], pWork[:, BLK // 2:BLK]).then_inc(blocks_copied, 1)
                dve.wait_ge(blocks_copied, j + 1)

                def beside(c, h, but):
                    m = M1 + j * MJ + c // SLOT
                    at = c % SLOT
                    expert(m, m % 2, at // 2, 2 * (at % 2), h, m // 2, but)
                    if h == 1 and at == 1 and m + 1 < 2 * K:
                        xm_low(m + 1, (m + 1) % 2, True)

                for c in range(BLK):
                    r = BLK - 1 - c
                    st.done(v.reciprocal(RD[:, c:c + 1], work[:, c, c:c + 1]))
                    if r == 0:
                        beside(c, 0, 0)
                        beside(c, 1, 0)
                        break
                    st.done(v.tensor_scalar(work[:, c, c:c + 1], work[:, c, c:c + 1], 1.0, None, ALU.add))
                    beside(c, 0, 0)
                    st.wait(but=1)
                    st.done(v.tensor_tensor(prod[:, 0:r], work[:, c:c + 1, :].broadcast_to([P, r, BLK]),
                                            work[:, c + 1:BLK, c:c + 1].broadcast_to([P, r, BLK]), ALU.mult))
                    beside(c, 1, 1)
                    st.wait()
                    st.done(v.scalar_tensor_tensor(work[:, c + 1:BLK], prod[:, 0:r], RD[:, c:c + 1],
                                                   work[:, c + 1:BLK], ALU.mult, ALU.subtract, reverse1=True))
                    st.wait()
                st.done(v.tensor_tensor(work[:], work[:], below[:], ALU.mult))
                st.wait()
                v.memset(work[:].rearrange("p a b -> p (a b)")[:, 0:BLK * BLK:BLK + 1], 1.0)\
                    .then_inc(blocks_factored, 1)
                yts = YTs4 if j == NJ - 1 else YTs
                dve.wait_ge(y_full, 3 * j + 1)
                for h in range(2):
                    rows = slice(HALF * h + BLK * j, HALF * h + BLK * (j + 1))
                    ins = v.tensor_copy(RDall[rows], pYa[0:BLK, 0, h * HALF:(h + 1) * HALF])
                ins.then_inc(y_rd_kept, 1)
                dve.wait_ge(y_full, 3 * j + 3)
                for h in range(2):
                    rows = slice(HALF * h + BLK * j, HALF * h + BLK * (j + 1))
                    ins = v.tensor_copy(yts[rows, :, BLK // 2:BLK].rearrange("c p i -> c i p"),
                                        pYa[0:BLK, :, h * HALF:(h + 1) * HALF])
                ins.then_inc(y_rd_kept, 1)
                if j < NJ - 1:
                    with dve.Fori(0, K) as g:
                        dve.wait_ge(update_full, g + (j * K + 1))
                        v.tensor_tensor(GR[:, grp(g), BLK:2 * P], GR[:, grp(g), BLK:2 * P],
                                        pU[:, :, BLK:2 * P], ALU.subtract).then_inc(update_done, 1)

            dve.wait_ge(y_kept, NJ)
            dve.wait_ge(y_rd_kept, 2 * NJ)
            for par in range(2):
                dve.wait_ge(part_stored[par], 16 * K)
            v.memset(pM[:], 0.0).then_inc(m_zeroed, 1)
            v.memset(MT[:], 0.0).then_inc(m_zeroed, 1)
            st.done(v.tensor_tensor(SD[:], sdot[:], RDall[:], ALU.mult))
            st.wait()
            upperb = upper[:].unsqueeze(1).broadcast_to([P, B, P])

            def split_gates():
                st.done(v.tensor_copy(g_hi[:], gates[:]))
                st.wait()
                v.tensor_tensor(g_parts[:, :, 1], gates[:], g_hi[:], ALU.subtract)
                v.tensor_copy(g_parts[:, :, 0], g_hi[:]).then_inc(gates_split, 1)
                v.tensor_copy(g_parts[:, :, 2], g_hi[:]).then_inc(gates_split, 1)

            def split_be():
                dve.wait_ge(consts_ready, CONSTS)
                dve.wait_ge(out_weights_loaded, 16 * (3 * B + 1))
                st.done(v.tensor_copy(wo_hi[:], wo_sb[:]))
                st.wait()
                st.done(split_low(wo_lo[:], wo_sb[:], wo_hi[:]))
                st.done(v.tensor_copy(be_hi[:], be_land[:]))
                st.wait()
                st.done(v.tensor_tensor(be_lo[:], be_land[:], be_hi[:], ALU.subtract))
                st.wait()
                for b in range(B):
                    st.done(v.tensor_scalar(be_land[:], be_lo[:], mask_lo[0:GROWS, b:b + 1], None, ALU.mult))
                    st.wait()
                    v.scalar_tensor_tensor(bebo4[:, b], be_hi[:], mask_hi[0:GROWS, b:b + 1], be_land[:],
                                           ALU.mult, ALU.add).then_inc(be_ready, 1)
                    dve.wait_ge(be_ready, b + 1)

            def scale_v(k, par, i, done):
                dve.wait_ge(v_loaded[par], i * 16 + 16)
                if done is not None:
                    dve.wait_ge(m_full, done)
                v.tensor_tensor(Vs[:], vin[par][:], SD[:, grp(k)].unsqueeze(2).broadcast_to([P, B, H]),
                                ALU.mult).then_inc(vs_ready, 1)

            def mask_pt(k):
                dve.wait_ge(pt_full, k + 1)
                v.tensor_tensor(PTm[:], pPT[:], upperb, ALU.mult).then_inc(pt_masked, 1)

            def low_ot(k):
                dve.wait_ge(ot_high, k + 1)
                split_low(O_lo[:], pOT[:], O_hi[:]).then_inc(ot_ready, 1)

            def finish(k, par, i):
                dve.wait_ge(out_full, k + 1)
                dve.wait_ge(in_summed, k + 1)
                if i is not None:
                    dve.wait_ge(out_stored[par], i * 16)
                v.tensor_tensor(obuf[par][:], pOut[:], pin[par][:], ALU.add).then_inc(out_ready, 1)

            scale_v(0, 0, 0, None)
            split_gates()
            mask_pt(0)
            split_be()
            for k in (0, 1):
                low_ot(k)
                scale_v(k + 1, 1 - k, k, k + 1)
                mask_pt(k + 1)
                finish(k, k, None)
            with dve.Fori(1, K // 2 - 1) as i:
                for par in range(2):
                    k = i * 2 + par
                    low_ot(k)
                    scale_v(k + 1, 1 - par, i + par, k + 1)
                    mask_pt(k + 1)
                    finish(k, par, i)
            low_ot(K - 2)
            scale_v(K - 1, 1, K // 2 - 1, K - 1)
            mask_pt(K - 1)
            finish(K - 2, 0, K // 2 - 1)
            low_ot(K - 1)
            finish(K - 1, 1, K // 2 - 1)

        @block.tensor
        def _(pe):
            mm = nc.tensor.matmul
            tr = nc.tensor.transpose

            def three(o, hi_t, lo_t, w_hi, w_lo):
                for c in range(DC):
                    mm(o, hi_t(c), w_hi(c), start=(c == 0), stop=False)
                    mm(o, hi_t(c), w_lo(c), start=False, stop=False)
                for c in range(DC):
                    ins = mm(o, lo_t(c), w_hi(c), start=False, stop=(c == DC - 1))
                return ins

            def pair_transpose(m, par):
                pe.wait_ge(xm_ready, m + 1)
                if not (isinstance(m, int) and m == 0):
                    pe.wait_ge(xm_lo, m)
                bank = early_banks[3] if isinstance(m, int) and m == 0 else tb
                for t in range(2):
                    for c in range(DC):
                        ins = tr(bank[:, 2 * t + c], xm[par][:, t, c * P:(c + 1) * P], ident[:])
                ins.then_inc(xmT_full, 1)

            def experts(m, par, t, q):
                if t == 0 and q == 0:
                    pe.wait_ge(xm_lo, m + 1)
                if t or not (isinstance(m, int) and m == 0):
                    pe.wait_ge(mb_used[q], m * 2 + t)
                three(mb[q][:].rearrange("p h n -> p (h n)"),
                      lambda c: xh[par][:, c, t], lambda c: xl[par][:, c, t],
                      lambda c: we_hi[:, c, q * 512:(q + 1) * 512],
                      lambda c: we_lo[:, c, q * 512:(q + 1) * 512]).then_inc(mb_full[q], 1)

            def x_transpose(g, par, h):
                if h == 0:
                    pe.wait_ge(xn_ready, g + 1)
                bank = early.get((g, h), tb) if isinstance(g, int) else tb
                for t in range(2):
                    for c in range(DC):
                        ins = tr(bank[:, 2 * t + c], xbuf[par][:, 2 * h + t, c * P:(c + 1) * P], ident[:])
                ins.then_inc(xT_full, 1)

            def project_qkv(g):
                pe.wait_ge(xT_lo, g * 2 + 2)
                for t in range(B):
                    if t >= 2 or not (isinstance(g, int) and g == 0):
                        pe.wait_ge(qkv_ready, g * B + (t - 1))
                    three(qb[t % 2][:, 0:NQ], lambda c: qh[:, c, t], lambda c: ql[:, c, t],
                          lambda c: wq_hi[:, c], lambda c: wq_lo[:, c]).then_inc(qb_full[t % 2], 1)

            def uq_transpose(g, h):
                if h == 0:
                    pe.wait_ge(u_ready, g + 1)
                else:
                    pe.wait_ge(uq_kept, g * 2 + 1)
                for t in range(2):
                    tr(tb[:, 2 * t], qkv[:, 2 * h + t, H:2 * H], ident[:])
                    ins = tr(tb[:, 2 * t + 1], qkv[:, 2 * h + t, 0:H], ident[:])
                ins.then_inc(uq_full, 1)

            def gram(g):
                pe.wait_ge(prefix_kept, g + 1)
                for b in range(B):
                    u = qkv[:, b, H:2 * H]
                    ins = mm(psS[:, b], u, u, start=False, stop=True, skip_group_check=True)
                ins.then_inc(gram_done, 1)

            pe.wait_ge(consts_ready, 2)
            x_transpose(0, 0, 0)
            x_transpose(0, 0, 1)
            pair_transpose(0, 0)
            pe.wait_ge(wq_split, 1)
            project_qkv(0)
            x_transpose(1, 1, 0)
            x_transpose(1, 1, 1)
            pe.wait_ge(xT_lo, 4)
            uq_transpose(0, 0)
            gram(0)
            uq_transpose(0, 1)
            pe.wait_ge(we_split, 1)

            def step(k, par, i):
                g = k + 1
                more = within(g, K)
                if more:
                    project_qkv(g)
                if within(k + 2, K):
                    pe.wait_ge(uq_kept, k * 2 + 2)
                    x_transpose(k + 2, par, 0)
                experts(k, par, 0, 0)
                experts(k, par, 0, 1)
                if within(k + 2, K):
                    pe.wait_ge(xT_lo, k * 2 + 5)
                    x_transpose(k + 2, par, 1)
                experts(k, par, 0, 2)
                experts(k, par, 0, 3)
                if within(k + 2, K):
                    pe.wait_ge(xT_lo, k * 2 + 6)
                elif not more:
                    pe.wait_ge(uq_kept, 2 * K)
                else:
                    pe.wait_ge(uq_kept, k * 2 + 2)
                pair_transpose(k + 1, 1 - par)
                experts(k, par, 1, 0)
                experts(k, par, 1, 1)
                if more:
                    pe.wait_ge(xm_lo, k + 2)
                    uq_transpose(g, 0)
                experts(k, par, 1, 2)
                if within(g, K - 1):
                    gram(g)
                if more:
                    uq_transpose(g, 1)
                experts(k, par, 1, 3)

            steps_beside_stage1(pe, step)
            pe.wait_ge(mb_full[NB - 1], 2 * K)
            nc.tensor.sem_inc(stage1_over, 1)
            pe.wait_ge(stage1_over, 3)
            pe.wait_ge(xm_lo, K + 1)
            for q in range(NB):
                pe.wait_ge(mb_used[q], 2 * K)

            def au(s, k, lhs):
                for b in range(B):
                    ins = mm(pT[s][:, b], lhs(b), GR[:, bass.ds(k * B + b, 1), P:2 * P].squeeze(1), start=True, stop=True)
                ins.then_inc(au_full[s], 1)

            def gmat(s, k, done):
                pe.wait_ge(au_ready[s], done)
                for b in range(B):
                    tr(pX[s][:, b], Vn[s][:, b], ident[:])
                for b in range(B):
                    ins = mm(pT[s][:, b], Vn[s][:, b], GR[:, bass.ds(k * B + b, 1), P:2 * P].squeeze(1), start=True, stop=True)
                ins.then_inc(g_full[s], 1)

            def newton(before, before_x, half, nit, low, ready_to_start, whole_ready):
                def s_times_x(it, s):
                    if it == 0:
                        ready_to_start(s)
                    if it == low - 1:
                        whole_ready(s)
                    if it > 0:
                        pe.wait_ge(x_ready[s], before_x + it)
                    lhs, x = (Sr[s], Xr[s]) if it < low else (Sst[s], X[s])
                    both = it == low - 1
                    for b in range(B):
                        ins = mm(pT[s][:, b], lhs[:, b], x[:, b], start=True, stop=not both)
                        if both:
                            ins = mm(pT[s][:, b], Sl[s][:, b], x[:, b], start=False, stop=True)
                    ins.then_inc(t_full[s], 1)

                def x_times_v(it, s):
                    pe.wait_ge(v_ready[s], before + (it + 1))
                    x, vn = (Xr[s], Vr[s]) if it < low else (X[s], Vn[s])
                    if it == nit - 1:
                        pe.wait_ge(x_half_ready, half + (s + 1))
                        x, vn = Sl[s], Vr[s]
                    both = it == low - 1
                    for b in range(B):
                        ins = mm(pX[s][:, b], x[:, b], vn[:, b], start=True, stop=not both)
                        if both:
                            ins = mm(pX[s][:, b], vn[:, b], x[:, b], start=False, stop=True)
                    ins.then_inc(x_full[s], 1)

                for s in range(NS - 1):
                    s_times_x(0, s)
                for it in range(nit):
                    for s in range(NS):
                        x_times_v(it, s)
                        if s == 0:
                            s_times_x(it, NS - 1)
                        elif it + 1 < nit:
                            s_times_x(it + 1, s - 1)

            for s in range(NS):
                nc.tensor.sem_inc(t_full[s], 1)
                nc.tensor.sem_inc(au_full[s], 1)
            with pe.Fori(0, NR) as i:
                def ready_to_start(s):
                    pe.wait_ge(s16_staged[s], i + 1)
                    pe.wait_ge(x_init[s], i + 1)
                    pe.wait_ge(g_kept[s], i + 1)
                    pe.wait_ge(ua_kept[s], i + 1)

                newton(i * NIT, i * (NIT - 1), i * NS, NIT, LOW, ready_to_start, lambda s: pe.wait_ge(s_staged[s], i + 1))
                for s in range(NS):
                    pe.wait_ge(x_done, i * NS + (s + 1))
                    au(s, i * NS + s, lambda b, s=s: X[s][:, b])
                for s in range(NS):
                    gmat(s, i * NS + s, i + 1)

            def prob(g, b, rows, cols):
                return GR[rows, bass.ds(g * B + b, 1), cols].squeeze(1)

            top = slice(0, HALF)
            for r in range(NR64):
                def ready_to_start(s):
                    pe.wait_ge(s16_staged[s], NR + r + 1)
                    pe.wait_ge(x_init[s], NR + r + 1)
                    if r == 0:
                        pe.wait_ge(g_kept[s], NR + 1)
                        pe.wait_ge(ua_kept[s], NR + 1)
                    elif s == 0:
                        pe.wait_ge(half_done, NS * r)
                        pe.wait_ge(half_done_odd, NS * r)

                newton(STEPS1 + r * NIT64, NR * (NIT - 1) + r * (NIT64 - 1), (NR + r) * NS, NIT64, LOW64, ready_to_start,
                       lambda s: pe.wait_ge(s_staged[s], NR + r + 1))
                for s in range(NS):
                    pe.wait_ge(xodd_ready, r * NS + s + 1)
                    for h in range(2):
                        for b in range(B):
                            inv = Xodd[s][:, b] if h else X[s][0:HALF, b, 0:HALF]
                            ins = mm(pF[s][0:HALF, h, b], inv, prob(2 * (r * NS + s) + h, b, top, slice(HALF, P)),
                                     start=True, stop=True)
                    ins.then_inc(f_full, 1)
                for g in range(2 * r * NS, 2 * (r + 1) * NS):
                    s, h = g // 2 % NS, g % 2
                    pe.wait_ge(f_ready, g // 2 + 1)
                    if g >= 2:
                        pe.wait_ge(half_done_odd if h else half_done, g // 2)
                    for b in range(B):
                        o = pV[h][HALF:P, b, HALF:2 * P]
                        ins = mm(o, Fst[s][:, h, b], prob(g, b, top, slice(HALF, 2 * P)), start=True, stop=not h)
                        if h:
                            ins = mm(o, ident[:, HALF:P], prob(g, b, slice(0, P), slice(HALF, 2 * P)),
                                     start=False, stop=True)
                    ins.then_inc(half_full, 1)

            pe.wait_ge(half_done, K // 2)
            pe.wait_ge(half_done_odd, K // 2)
            for j in range(NJ):
                if j:
                    pe.wait_ge(update_done, j * K)
                    pe.wait_ge(panel_kept, j * K)
                for c in range(BLK):
                    for h in range(2):
                        at = HALF * h + BLK * j
                        ins = mm(pWork[HALF * h:HALF * (h + 1), c], GR[:, :, at + c], ident[:, at:at + BLK],
                                 start=True, stop=True)
                    if c % (BLK // 2) == BLK // 2 - 1:
                        ins.then_inc(blocks_gathered, 1)
                pe.wait_ge(blocks_copied, j + 1)
                if j:
                    pe.wait_ge(y_rd_kept, 2 * j)
                for m in range(M1 + j * MJ, M1 + j * MJ + MJ):
                    if m + 1 < 2 * K:
                        pair_transpose(m + 1, (m + 1) % 2)
                    for t in range(2):
                        for q in range(NB):
                            experts(m, m % 2, t, q)
                pe.wait_ge(blocks_factored, j + 1)
                for q in range(NB):
                    pe.wait_ge(mb_used[q], 2 * (m + 1))
                if m + 1 < 2 * K:
                    pe.wait_ge(xm_lo, m + 2)
                tr(pYa[0:BLK, 0], RD[:], ident[:]).then_inc(y_full, 1)
                for i in range(BLK // 2):
                    ins = tr(pYb[0:BLK, i], work[:, i], ident[:])
                ins.then_inc(y_full, 1)
                pe.wait_ge(y_rd_kept, 2 * j + 1)
                for i in range(BLK // 2):
                    ins = tr(pYa[0:BLK, i], work[:, BLK // 2 + i], ident[:])
                ins.then_inc(y_full, 1)

                if j == NJ - 1:
                    break
                c0 = BLK * (j + 1)

                def panel(g, par, seen):
                    pe.wait_ge(yt_ready, g * 2 + (2 * j * K + 2))
                    if seen:
                        pe.wait_ge(panel_kept, g + j * K)
                    for b in range(B):
                        ins = mm(pP[:, b, c0:2 * P], YT[par][:, b], prob(g, b, slice(0, P), slice(c0, 2 * P)),
                                 start=True, stop=True)
                    ins.then_inc(panel_full, 1)

                def trail(g, par, seen):
                    pe.wait_ge(lt_ready, g * 2 + (2 * j * K + 2))
                    if seen:
                        pe.wait_ge(update_done, g + j * K)
                    for b in range(B):
                        ins = mm(pU[:, b, c0:2 * P], LT[par][:, b], prob(g, b, slice(0, P), slice(c0, 2 * P)),
                                 start=True, stop=True)
                    ins.then_inc(update_full, 1)

                panel(0, 0, False)
                panel(1, 1, True)
                trail(0, 0, False)
                panel(2, 0, True)
                trail(1, 1, True)
                with pe.Fori(1, K // 2 - 1) as i:
                    for par in range(2):
                        g = i * 2 + par
                        panel(g + 1, 1 - par, True)
                        trail(g, par, True)
                panel(K - 1, 1, True)
                trail(K - 2, 0, True)
                trail(K - 1, 1, True)

            def q_of(k, b):
                return QT[:, bass.ds(k * B + b, 1), :].squeeze(1)

            def w_transpose(k, par):
                pe.wait_ge(w_staged, k + 1)
                for b in range(B):
                    ins = tr(pWT[:, b], Wst[par][:, b], ident[:])
                ins.then_inc(wt_full, 1)

            def pt(k):
                pe.wait_ge(wt_ready, k + 1)
                for b in range(B):
                    ins = mm(pPT[:, b], WT[:, b], q_of(k, b), start=True, stop=True)
                ins.then_inc(pt_full, 1)

            def ot(k, seen):
                pe.wait_ge(vs_ready, k + 1)
                pe.wait_ge(pt_masked, k + 1)
                if seen:
                    pe.wait_ge(m_kept, k)
                    pe.wait_ge(ot_ready, k)
                for b in range(B):
                    mm(pOT[:, b], MT[:, b], q_of(k, b), start=True, stop=False)
                    ins = mm(pOT[:, b], Vs[:, b], PTm[:, b], start=False, stop=True)
                ins.then_inc(ot_full, 1)

            def m_update(k, par):
                for b in range(B):
                    ins = mm(pM[:, b], Wst[par][:, b], Vs[:, b], start=False, stop=True, skip_group_check=True)
                ins.then_inc(m_full, 1)

            def gates_transpose(k):
                pe.wait_ge(gates_staged, k + 1)
                if not (isinstance(k, int) and k == 0):
                    pe.wait_ge(gt_ready, k)
                tr(pG[:, 0:P], gst[:], ident[:]).then_inc(gt_full, 1)

            def project(k, seen):
                pe.wait_ge(gt_ready, k + 1)
                pe.wait_ge(ot_ready, k + 1)
                if seen:
                    pe.wait_ge(out_ready, k)
                else:
                    pe.wait_ge(be_ready, B)
                for b in range(B):
                    mm(pOut[:, b], O_hi[:, b], wo_hi[:], start=True, stop=False)
                    mm(pOut[:, b], O_hi[:, b], wo_lo[:], start=False, stop=False)
                    mm(pOut[:, b], O_lo[:, b], wo_hi[:], start=False, stop=False)
                    ins = mm(pOut[:, b], gT[0:GROWS], bebo4[:, b], start=False, stop=True)
                ins.then_inc(out_full, 1)

            pe.wait_ge(y_kept, NJ)
            pe.wait_ge(y_rd_kept, 2 * NJ)

            def last_panel(k, par, seen):
                pe.wait_ge(yt_ready, k * 2 + (2 * (NJ - 1) * K + 2))
                if seen:
                    pe.wait_ge(w_staged, k)
                for b in range(B):
                    ins = mm(pW[:, b], YT4[par][:, b], prob(k, b, slice(0, P), slice(P, 2 * P)), start=True, stop=True)
                ins.then_inc(w_full, 1)

            last_panel(0, 0, False)
            last_panel(1, 1, True)
            w_transpose(0, 0)
            gates_transpose(0)
            pt(0)
            pe.wait_ge(m_zeroed, 2)
            pe.wait_ge(out_weights_loaded, 16 * (3 * B + 1))

            def step(k, par, seen):
                w_transpose(k + 1, 1 - par)
                ot(k, seen)
                m_update(k, par)
                if within(k + 2, K):
                    last_panel(k + 2, par, True)
                pt(k + 1)
                project(k, seen)
                gates_transpose(k + 1)

            step(0, 0, False)
            step(1, 1, True)
            with pe.Fori(1, K // 2 - 1) as i:
                for par in range(2):
                    step(i * 2 + par, par, True)
            step(K - 2, 0, True)
            ot(K - 1, True)
            project(K - 1, True)


_OUT = ((4, 2048, 256), "float32")


def kernel(**inputs):
    import numpy as np
    import concourse.bacc as bacc
    from concourse.bass_utils import run_bass_kernel_spmd

    a = {name: np.asarray(value) for name, value in inputs.items()}
    E, O, D = a["L0_ffn_We"].shape
    arrays = {
        "x": a["L0_attn_x"],
        "wqkvg": np.concatenate([a["L0_attn_Wq"].T, a["L0_attn_Wk"].T, a["L0_attn_Wv"].T, a["L0_ffn_Wg"]], axis=1),
        "bias_row": np.concatenate([a["L0_attn_bq"], a["L0_attn_bk"], a["L0_attn_bv"], a["L0_ffn_bg"]]),
        "we": a["L0_ffn_We"].transpose(2, 0, 1).reshape(D, E * O),
        "be_bo": np.concatenate([a["L0_ffn_be"], a["L0_attn_bo"][None]], axis=0),
        "wo": a["L0_attn_Wo"].T,
    }
    nc = bacc.Bacc("TRN2", target_bir_lowering=False, num_devices=1)
    ins, args = {}, []
    for name, value in arrays.items():
        value = np.ascontiguousarray(value)
        ins[f"in_{name}"] = value
        args.append(nc.dram_tensor(f"in_{name}", value.shape, mybir.dt.from_np(value.dtype), kind="ExternalInput").ap())
    shape, dtype = _OUT
    args.append(nc.dram_tensor("out_0", shape, mybir.dt.from_np(np.dtype(dtype)), kind="ExternalOutput").ap())
    build(nc, *args)
    r = run_bass_kernel_spmd(nc, [ins], core_ids=[0])
    return r.results[0]["out_0"]
```
